# Optimizing a Trainium2 kernel written in Bass

```python
import numpy as np
import jax
import jax.numpy as jnp

def _softmax(x, axis=-1):
    return jax.nn.softmax(x, axis=axis)

def _gelu(x):
    return jax.nn.gelu(x, approximate=True)

def _silu(x):
    return jax.nn.silu(x)

def _sigmoid(x):
    return jax.nn.sigmoid(x)

def _layernorm(x, axis=-1, eps=1e-05):
    m = jnp.mean(x, axis=axis, keepdims=True)
    v = jnp.var(x, axis=axis, keepdims=True)
    return (x - m) / jnp.sqrt(v + eps)

def _scatter_add(tgt, idx, src, axis=0):
    return tgt.at[idx].add(src)

def _segment_sum(src, seg, n):
    return jax.ops.segment_sum(src, seg, n)
kernel_name = 'mk_gps_d1_gnn_r8_f4f71c'

def setup_inputs(seed: int=0):
    np.random.seed(seed)
    _w = jnp.asarray

    def _rec_inputs():
        import jax
        import jax.numpy as jnp
        _gk = jax.random.key(seed)
        x = -0.0003713 + 1 * jax.random.normal(jax.random.fold_in(_gk, 1), (6250, 256), jnp.float32)
        src = jax.random.randint(jax.random.fold_in(_gk, 2), (200000,), 0, 6250, jnp.int32)
        dst = jnp.minimum((6250 * jax.random.uniform(jax.random.fold_in(_gk, 3), (200000,)) ** 2.0).astype(jnp.int32), 49999)
        _o = jnp.argsort(dst, stable=True)
        src = src[_o]
        dst = dst[_o]
        return (x, src, dst)
    x, src, dst = _rec_inputs()

    def _L0_gnn_setup():
        import jax, jax.numpy as jnp
        import numpy as np
        N_NODES = 6250
        N_EDGES = 100000
        IN_FEATS = 256
        N_HIDDEN = 256

        def _degree_norms(src, dst, n_nodes):
            ones = jnp.ones(src.shape, jnp.float32)
            out_deg = jax.ops.segment_sum(ones, src, num_segments=n_nodes)
            in_deg = jax.ops.segment_sum(ones, dst, num_segments=n_nodes)
            norm_src = jax.lax.rsqrt(jnp.maximum(out_deg, 1.0))
            norm_dst = jax.lax.rsqrt(jnp.maximum(in_deg, 1.0))
            return (norm_src, norm_dst)

        def _graph_conv(h, W, b, src, dst, norm_src, norm_dst, activation):
            h = h * norm_src[:, None] @ W
            msg = h[src]
            agg = jax.ops.segment_sum(msg, dst, num_segments=h.shape[0])
            out = agg * norm_dst[:, None] + b
            if activation:
                out = jax.nn.relu(out)
            return out
        key = jax.random.key(seed)
        ks = jax.random.split(key, 8)
        scale_in = 1.0 / np.sqrt(IN_FEATS)
        scale_h = 1.0 / np.sqrt(N_HIDDEN)
        return {'features': jax.random.normal(ks[0], (N_NODES, IN_FEATS), jnp.float32), 'W0': jax.random.normal(ks[1], (IN_FEATS, N_HIDDEN), jnp.float32) * scale_in, 'b0': jnp.zeros((N_HIDDEN,), jnp.float32), 'W1': jax.random.normal(ks[2], (N_HIDDEN, N_HIDDEN), jnp.float32) * scale_h, 'b1': jnp.zeros((N_HIDDEN,), jnp.float32), 'W2': jax.random.normal(ks[3], (N_HIDDEN, N_HIDDEN), jnp.float32) * scale_h, 'b2': jnp.zeros((N_HIDDEN,), jnp.float32), 'src': jax.random.randint(ks[4], (N_EDGES,), 0, N_NODES, jnp.int32), 'dst': jax.random.randint(ks[5], (N_EDGES,), 0, N_NODES, jnp.int32)}
    _L0_gnn_all = _L0_gnn_setup()
    _L0_gnn_in = {k: v for k, v in _L0_gnn_all.items() if k in ('W0', 'b0', 'W1', 'b1', 'W2', 'b2')}
    del _L0_gnn_all

    def _L0_mix_setup():
        import jax, jax.numpy as jnp
        import numpy as np
        N, F, C, H = (32, 512, 256, 8)
        D = C // H
        EPS_ATTN = 1e-06
        EPS_LN = 1e-05

        def layer_norm(x, g, b):
            mu = jnp.mean(x, axis=-1, keepdims=True)
            var = jnp.var(x, axis=-1, keepdims=True)
            return (x - mu) * jax.lax.rsqrt(var + EPS_LN) * g + b
        key = jax.random.key(seed)
        ks = jax.random.split(key, 8)
        s = 1.0 / np.sqrt(C)
        return {'x': jax.random.normal(ks[0], (N, F, C), jnp.float32), 'Wqkv': jax.random.uniform(ks[1], (3 * C, C), jnp.float32, -s, s), 'ln1_g': jnp.ones((C,), jnp.float32), 'ln1_b': jnp.zeros((C,), jnp.float32), 'W1': jax.random.uniform(ks[2], (C, C), jnp.float32, -s, s), 'b1': jax.random.uniform(ks[3], (C,), jnp.float32, -s, s), 'W2': jax.random.uniform(ks[4], (C, C), jnp.float32, -s, s), 'b2': jax.random.uniform(ks[5], (C,), jnp.float32, -s, s), 'ln2_g': jnp.ones((C,), jnp.float32), 'ln2_b': jnp.zeros((C,), jnp.float32)}
    _L0_mix_all = _L0_mix_setup()
    _L0_mix_in = {k: v for k, v in _L0_mix_all.items() if k in ('Wqkv', 'ln1_g', 'ln1_b', 'W1', 'b1', 'W2', 'b2', 'ln2_g', 'ln2_b')}
    del _L0_mix_all

    def _L0_ffn_setup():
        import jax, jax.numpy as jnp
        import numpy as np
        TOP_K = 2
        LN_EPS = 1e-05
        key = jax.random.key(seed)
        ks = jax.random.split(key, 8)
        B, S, D, E, H = (16, 1024, 256, 8, 1024)
        x = jax.random.normal(ks[0], (B, S, D), dtype=jnp.float32)
        Wr = jax.random.normal(ks[1], (D, E), dtype=jnp.float32) * 0.1
        br = jnp.zeros((E,), dtype=jnp.float32)
        ln_g = jnp.ones((E, D), dtype=jnp.float32)
        ln_b = jnp.zeros((E, D), dtype=jnp.float32)
        W1 = jax.random.normal(ks[2], (E, D, H), dtype=jnp.float32) * (1.0 / np.sqrt(D))
        b1 = jnp.zeros((E, H), dtype=jnp.float32)
        W2 = jax.random.normal(ks[3], (E, H, D), dtype=jnp.float32) * (1.0 / np.sqrt(H))
        b2 = jnp.zeros((E, D), dtype=jnp.float32)
        return {'x': x, 'Wr': Wr, 'br': br, 'ln_g': ln_g, 'ln_b': ln_b, 'W1': W1, 'b1': b1, 'W2': W2, 'b2': b2}
    _L0_ffn_all = _L0_ffn_setup()
    _L0_ffn_in = {k: v for k, v in _L0_ffn_all.items() if k in ('Wr', 'br', 'ln_g', 'ln_b', 'W1', 'b1', 'W2', 'b2')}
    del _L0_ffn_all
    return {'x': x, 'src': src, 'dst': dst, 'L0_gnn_W0': _L0_gnn_in['W0'], 'L0_gnn_b0': _L0_gnn_in['b0'], 'L0_gnn_W1': _L0_gnn_in['W1'], 'L0_gnn_b1': _L0_gnn_in['b1'], 'L0_gnn_W2': _L0_gnn_in['W2'], 'L0_gnn_b2': _L0_gnn_in['b2'], 'L0_mix_Wqkv': _L0_mix_in['Wqkv'], 'L0_mix_ln1_g': _L0_mix_in['ln1_g'], 'L0_mix_ln1_b': _L0_mix_in['ln1_b'], 'L0_mix_W1': _L0_mix_in['W1'], 'L0_mix_b1': _L0_mix_in['b1'], 'L0_mix_W2': _L0_mix_in['W2'], 'L0_mix_b2': _L0_mix_in['b2'], 'L0_mix_ln2_g': _L0_mix_in['ln2_g'], 'L0_mix_ln2_b': _L0_mix_in['ln2_b'], 'L0_ffn_Wr': _L0_ffn_in['Wr'], 'L0_ffn_br': _L0_ffn_in['br'], 'L0_ffn_ln_g': _L0_ffn_in['ln_g'], 'L0_ffn_ln_b': _L0_ffn_in['ln_b'], 'L0_ffn_W1': _L0_ffn_in['W1'], 'L0_ffn_b1': _L0_ffn_in['b1'], 'L0_ffn_W2': _L0_ffn_in['W2'], 'L0_ffn_b2': _L0_ffn_in['b2']}

def reference(x, src, dst, L0_gnn_W0, L0_gnn_b0, L0_gnn_W1, L0_gnn_b1, L0_gnn_W2, L0_gnn_b2, L0_mix_Wqkv, L0_mix_ln1_g, L0_mix_ln1_b, L0_mix_W1, L0_mix_b1, L0_mix_W2, L0_mix_b2, L0_mix_ln2_g, L0_mix_ln2_b, L0_ffn_Wr, L0_ffn_br, L0_ffn_ln_g, L0_ffn_ln_b, L0_ffn_W1, L0_ffn_b1, L0_ffn_W2, L0_ffn_b2):
    import jax
    import jax.numpy as jnp

    def _L0_gnn_ref(features, W0, b0, W1, b1, W2, b2, src, dst):
        import jax, jax.numpy as jnp
        import numpy as np
        N_NODES = 6250
        N_EDGES = 100000
        IN_FEATS = 256
        N_HIDDEN = 256

        def _degree_norms(src, dst, n_nodes):
            ones = jnp.ones(src.shape, jnp.float32)
            out_deg = jax.ops.segment_sum(ones, src, num_segments=n_nodes)
            in_deg = jax.ops.segment_sum(ones, dst, num_segments=n_nodes)
            norm_src = jax.lax.rsqrt(jnp.maximum(out_deg, 1.0))
            norm_dst = jax.lax.rsqrt(jnp.maximum(in_deg, 1.0))
            return (norm_src, norm_dst)

        def _graph_conv(h, W, b, src, dst, norm_src, norm_dst, activation):
            h = h * norm_src[:, None] @ W
            msg = h[src]
            agg = jax.ops.segment_sum(msg, dst, num_segments=h.shape[0])
            out = agg * norm_dst[:, None] + b
            if activation:
                out = jax.nn.relu(out)
            return out
        n = features.shape[0]
        norm_src, norm_dst = _degree_norms(src, dst, n)
        h = _graph_conv(features, W0, b0, src, dst, norm_src, norm_dst, True)
        h = _graph_conv(h, W1, b1, src, dst, norm_src, norm_dst, True)
        h = _graph_conv(h, W2, b2, src, dst, norm_src, norm_dst, False)
        return h

    def _L0_mix_ref(x, Wqkv, ln1_g, ln1_b, W1, b1, W2, b2, ln2_g, ln2_b):
        import jax, jax.numpy as jnp
        import numpy as np
        N, F, C, H = (32, 512, 256, 8)
        D = C // H
        EPS_ATTN = 1e-06
        EPS_LN = 1e-05

        def layer_norm(x, g, b):
            mu = jnp.mean(x, axis=-1, keepdims=True)
            var = jnp.var(x, axis=-1, keepdims=True)
            return (x - mu) * jax.lax.rsqrt(var + EPS_LN) * g + b
        n, f, c = x.shape
        qkv = jnp.einsum('nfc,oc->nfo', x, Wqkv)
        q, k, v = jnp.split(qkv, 3, axis=-1)
        q = q.reshape(n, f, H, D)
        k = k.reshape(n, f, H, D)
        v = v.reshape(n, f, H, D)
        q = jax.nn.elu(q) + 1.0
        k = jax.nn.elu(k) + 1.0
        kv = jnp.einsum('nshd,nshm->nhmd', k, v)
        ksum = jnp.sum(k, axis=1)
        z = 1.0 / (jnp.einsum('nlhd,nhd->nlh', q, ksum) + EPS_ATTN)
        t = jnp.einsum('nlhd,nhmd,nlh->nlhm', q, kv, z)
        t = t.reshape(n, f, c)
        x1 = layer_norm(t + x, ln1_g, ln1_b)
        h = jax.nn.gelu(jnp.einsum('nfc,oc->nfo', x1, W1) + b1, approximate=False)
        y = jnp.einsum('nfc,oc->nfo', h, W2) + b2
        return layer_norm(y + x1, ln2_g, ln2_b)

    def _L0_ffn_ref(x, Wr, br, ln_g, ln_b, W1, b1, W2, b2):
        import jax, jax.numpy as jnp
        import numpy as np
        TOP_K = 2
        LN_EPS = 1e-05
        B, S, D = x.shape
        N = B * S
        xt = x.reshape(N, D)
        logits = xt @ Wr + br
        probs = jax.nn.softmax(logits, axis=-1)
        top_p, top_idx = jax.lax.top_k(probs, TOP_K)
        weights = top_p / top_p.sum(axis=-1, keepdims=True)
        mu = xt.mean(axis=-1, keepdims=True)
        var = ((xt - mu) ** 2).mean(axis=-1, keepdims=True)
        xn = (xt - mu) * jax.lax.rsqrt(var + LN_EPS)
        xe = xn[None, :, :] * ln_g[:, None, :] + ln_b[:, None, :]
        h = jax.nn.gelu(jnp.einsum('end,edh->enh', xe, W1) + b1[:, None, :], approximate=False)
        y = jnp.einsum('enh,ehd->end', h, W2) + b2[:, None, :]
        y_tok = jnp.transpose(y, (1, 0, 2))
        sel = jnp.take_along_axis(y_tok, top_idx[:, :, None], axis=1)
        out = (weights[:, :, None] * sel).sum(axis=1)
        return out.reshape(B, S, D)
    xn = _layernorm(x, axis=-1)
    x = x + _L0_gnn_ref(xn, L0_gnn_W0, L0_gnn_b0, L0_gnn_W1, L0_gnn_b1, L0_gnn_W2, L0_gnn_b2, src, dst) + _L0_mix_ref(xn[None], L0_mix_Wqkv, L0_mix_ln1_g, L0_mix_ln1_b, L0_mix_W1, L0_mix_b1, L0_mix_W2, L0_mix_b2, L0_mix_ln2_g, L0_mix_ln2_b)[0]
    x = x + _L0_ffn_ref(_layernorm(x, axis=-1)[None], L0_ffn_Wr, L0_ffn_br, L0_ffn_ln_g, L0_ffn_ln_b, L0_ffn_W1, L0_ffn_b1, L0_ffn_W2, L0_ffn_b2)[0]
    return x

_drawn_inputs = setup_inputs


def setup_inputs(seed=0):
    import zlib

    import numpy as np

    out = dict(_drawn_inputs(seed))
    spreads = {'L0_gnn_b0': (0.0, 0.301),
     'L0_gnn_b1': (0.0, 0.1),
     'L0_gnn_b2': (0.0, 0.1),
     'L0_mix_ln1_g': (1.0, 0.2),
     'L0_mix_ln1_b': (0.0, 0.1),
     'L0_mix_ln2_g': (1.0, 0.2),
     'L0_mix_ln2_b': (0.0, 0.1),
     'L0_ffn_br': (0.0, 0.1),
     'L0_ffn_ln_g': (1.0, 0.2),
     'L0_ffn_ln_b': (0.0, 0.311),
     'L0_ffn_b1': (0.0, 0.308),
     'L0_ffn_b2': (0.0, 0.1)}
    factors = {'L0_gnn_W0': 8.0, 'L0_mix_Wqkv': 4.385, 'L0_mix_b1': 4.621}
    for name, (base, spread) in spreads.items():
        noise = np.random.default_rng([zlib.crc32(name.encode()), seed]).standard_normal(out[name].shape)
        drawn = base * np.exp(spread * noise) if base else spread * noise
        out[name] = jnp.asarray(drawn.astype(out[name].dtype))
    for name, factor in factors.items():
        out[name] = (out[name] * factor).astype(out[name].dtype)
    return out
```

```python
from contextlib import ExitStack

import numpy as np

import concourse.bass as bass
from concourse import mybir

ALU = mybir.AluOpType
ACT = mybir.ActivationFunctionType
AX_X = mybir.AxisListType.X
F32 = mybir.dt.float32
BF16 = mybir.dt.bfloat16
I32 = mybir.dt.int32
I16 = mybir.dt.int16
U32 = mybir.dt.uint32

P = 128
LN_EPS = 1e-5
ATTN_EPS = 1e-6
RING = 2


class Chain:

    def __init__(self, eng, sem, start=0):
        self.eng, self.sem, self.start, self.n = eng, sem, start, 0

    def link(self, ins, alone=None):
        self.n += 1
        ins.then_inc(self.sem, 1)
        self.eng.wait_ge(self.sem, self.start + self.n)
        if alone is not None:
            self.eng.sem_inc(alone, 1)


def gps_layer(nc, x, src, dst, gnn_W, gnn_b, Wqkv, ln1_g, ln1_b, mix_W1, mix_b1, mix_W2, mix_b2,
              ln2_g, ln2_b, Wr, br, ffn_g, ffn_b, ffn_W1, ffn_b1, ffn_W2, ffn_b2, out):
    N, D = x.shape
    E = src.shape[0]
    HALVES = D // P
    NT = -(-N // P)
    LAST = N - (NT - 1) * P
    NX = ffn_W1.shape[0]
    HID = ffn_W1.shape[2]
    MH = HID // P
    HEADS = 8
    HD = D // HEADS
    HPB = P // HD

    GC = 8
    NCH = -(-E // P)
    NG = -(-NCH // GC)
    GPT = NG // NT
    assert NG == GPT * NT and GPT == 4 and NT % 2 == 1
    LASTCH = NCH - (NG - 1) * GC
    CB = -(-NG * GC // P)
    FULLB = E // (P * P)
    TAILCH = (E - FULLB * P * P) // P
    TAILE = E - FULLB * P * P - TAILCH * P
    GE = GC * P
    FULLG = E // GE

    BT = 256
    NBLK = (2 * N) // BT + NX
    SLOTS = NBLK * BT
    LEAST = -(-2 * N // BT)
    NE = NT * NX

    tables = [nc.dram_tensor(f"table{l}", (NT * P, D), F32, kind="Internal").ap() for l in range(3)]
    bounds_d = nc.dram_tensor("bounds", (2, 2 * P), I32, kind="Internal").ap()
    routed_in = nc.dram_tensor("routed_in", (SLOTS + 2 * P, D), F32, kind="Internal").ap()
    routed_out = nc.dram_tensor("routed_out", (SLOTS, D), F32, kind="Internal").ap()

    with ExitStack() as ctx:
        def sb(name, shape, dt=F32):
            return ctx.enter_context(nc.sbuf_tensor(name, shape, dt))

        def sem(name):
            return ctx.enter_context(nc.semaphore(name))

        nodes = sb("nodes", [P, NT, D])
        agg = sb("agg", [P, NT, D + 1])
        wide = sb("wide", [P, 3584])
        node_no = wide[:, :].bitcast(I16)[:, 0:NT * P]
        dst_c = sb("dst_c", [P, CB * P], I16)
        src_c = sb("src_c", [P, CB * P], I16)
        msgs = sb("msgs", [P, GPT * GC, D + 1])
        flat = msgs[:, :, :].rearrange("p a b -> p (a b)")
        onehot = sb("onehot", [P, 2, GC // 2, P])
        onehot_lo = onehot[:, :, :, :].rearrange("p a b c -> p (a b c)").bitcast(BF16).rearrange(
            "p (s c n) -> p s c n", s=RING, c=GC)
        wqkvT = sb("wqkvT", [P, HALVES, 3 * D])
        w1T = sb("w1T", [P, HALVES, D])
        w2T = sb("w2T", [P, HALVES, D])
        wg = sb("wg", [P, 3, HALVES, D])
        wr = sb("wr", [P, HALVES, NX])
        rows = sb("rows", [P, 8, D])
        gb0, gb1, gb2, r1g, r1b, r2g, r2b, rb2 = (rows[:, i, :] for i in range(8))
        br_row = sb("br_row", [P, NX])
        b1col = sb("b1col", [P, HALVES])
        fgcol = sb("fgcol", [P, NX, HALVES])
        fbcol = sb("fbcol", [P, NX, HALVES])
        fb1col = sb("fb1col", [P, NX, MH])
        desc8 = sb("desc8", [P, NX])
        fb2row = sb("fb2row", [1, RING, D])
        ident = sb("ident", [P, P])
        before = sb("before", [P, P])
        ones = sb("ones", [P, P])
        zeros = sb("zeros", [P, D + 8])
        iota_b = sb("iota_b", [P, P], BF16)
        eps_ln = sb("eps_ln", [P, 1])
        idx = sb("idx", [P, GPT, GC], I32)
        cum = sb("cum", [1, 256], I32)
        shift = sb("shift", [1, 256], I32)
        mm = sb("mm", [P, 2, 2], I32)
        norm_src = sb("norm_src", [P, NT])
        norm_dst = sb("norm_dst", [P, NT])
        deg = sb("deg", [P, NT])
        mv = sb("mv", [P, NT, 2])
        st6 = sb("st6", [P, 6])
        rstd = sb("rstd", [P, NT])
        hs = sb("hs", [P, RING, D])
        onehot_hi = hs[:, :, :].rearrange("p s d -> p (s d)").bitcast(BF16).rearrange("p (s c n) -> p s c n", s=RING, c=GC)
        hT = sb("hT", [P, RING, D])
        st = sb("st", [P, RING, D])
        tmp = sb("tmp", [P, D])
        mix4 = sb("mix4", [P, 4, D])
        mrow, mT, melu, mexp = (mix4[:, i, :] for i in range(4))
        cnt_f = mix4[0:1, :, :]
        mfeat = sb("mfeat", [P, D])
        vaug = sb("vaug", [P, HALVES, P + 1])
        kvblk = sb("kvblk", [P, HALVES, P + HPB])
        x1 = sb("x1", [P, D])
        xo = sb("xo", [P, D])
        z = sb("z", [P, HALVES, HPB])
        mv1 = sb("mv1", [P, 2])
        sd1 = sb("sd1", [P, 1])

        W_ = CB * P
        dst_i = flat[:, 0:W_].bitcast(I32)
        src_i = flat[:, W_:2 * W_].bitcast(I32)
        dst_f = flat[:, 2 * W_:3 * W_]
        src_f = flat[:, 3 * W_:4 * W_]
        src_t, hi_i, lo_f, hi_f = dst_i, src_i, dst_f, src_f
        group_rows = agg[:, :, :].rearrange("p a b -> p (a b)")[:, 0:2 * GE].bitcast(I32).rearrange(
            "p (j e) -> p j e", j=2)

        agg_flat = agg[:, :, :].rearrange("p a b -> p (a b)")
        raw_qkv = agg_flat[:, 2 * GE:2 * GE + 6 * D].rearrange("p (o c) -> p o c", o=6)
        raw_w1 = agg_flat[:, 2 * GE + 6 * D:2 * GE + 8 * D].rearrange("p (o c) -> p o c", o=2)
        raw_w2 = agg_flat[:, 2 * GE + 8 * D:2 * GE + 10 * D].rearrange("p (o c) -> p o c", o=2)
        turned = [(raw_qkv, wqkvT, c, o, n) for c in range(HALVES) for o, n in ((0, 4), (4, 2))]
        turned += [(raw, to, c, 0, 2) for raw, to in ((raw_w1, w1T), (raw_w2, w2T)) for c in range(HALVES)]

        def cut(i):
            return flat[:, i * 400:i * 400 + NE]
        logits, s_a, s_b, oh1, oh2, pick, incl, tot, start_r, ex = (cut(i) for i in range(10))
        small = flat[:, 4000:4000 + 20 * NT].rearrange("p (a b) -> p a b", b=NT)
        w_up = [flat[:, s * 4096:s * 4096 + HALVES * HID].rearrange("p (c n) -> p c n", c=HALVES) for s in range(2)]
        w_dn = [flat[:, s * 4096 + HALVES * HID:(s + 1) * 4096].rearrange("p (m n) -> p m n", m=MH) for s in range(2)]
        gate1 = sb("gate1", [P, NT])
        gate2 = sb("gate2", [P, NT])
        slot1 = sb("slot1", [P, NT], I32)
        slot2 = sb("slot2", [P, NT], I32)
        take1 = sb("take1", [P, NT], I32)
        take2 = sb("take2", [P, NT], I32)
        valid = sb("valid", [P, NT])
        dump = sb("dump", [P, NT])
        sidx = sb("sidx", [P, RING, 2], I32)
        blk_no = sb("blk_no", [P, 16], I32)
        cnt8 = sb("cnt8", [P, 4, 16])
        cnt8i = sb("cnt8i", [P, 16], I32)
        xs = wide[:, 0:2 * D].rearrange("p (a n) -> p a n", a=2)
        xeT = wide[:, 2 * D:4 * D].rearrange("p (a n) -> p a n", a=2)
        ys = wide[:, 4 * D:6 * D].rearrange("p (a n) -> p a n", a=2)
        hidT = wide[:, 6 * D:6 * D + MH * BT].rearrange("p (m n) -> p m n", m=MH)

        bank = [ctx.enter_context(nc.psum_tensor(f"bank{i}", [P, 512], F32)) for i in range(8)]
        acc = bank[0][:, 0:D + 1]
        psT = [bank[1], bank[4]]
        psO = [bank[2], bank[5]]
        psKV = bank[3][:, 0:HALVES * (P + 1)]
        psA = bank[4]
        psB = bank[5]
        psC = bank[6]
        psH = bank[7]

        c_iota = sem("c_iota"); c_mat = sem("c_mat"); c_vec = sem("c_vec"); c_agg = sem("c_agg")
        vo = sem("vo"); po = sem("po")
        dve_past = sem("dve_past"); pe_past = sem("pe_past"); pool_past = sem("pool_past")
        raw_clear = sem("raw_clear"); dst_in = sem("dst_in"); src_in = sem("src_in")
        gr_clear = sem("gr_clear"); gr_in = sem("gr_in"); mm_ready = sem("mm_ready")
        bounds_out = sem("bounds_out"); bounds_in = sem("bounds_in"); cum_ready = sem("cum_ready")
        edges_f = sem("edges_f"); edgesT = sem("edgesT"); edges_c = sem("edges_c")
        lohi = sem("lohi"); hist_oh = sem("hist_oh"); src_ready = sem("src_ready"); agg_clear = sem("agg_clear"); hist_used = sem("hist_used"); hist_done = sem("hist_done")
        w_in = sem("w_in"); wraw_in = sem("wraw_in"); wT = sem("wT"); wT_out = sem("wT_out")
        x_in = sem("x_in"); mv_ready = sem("mv_ready"); sd_ready = sem("sd_ready")
        xn_ready = sem("xn_ready")
        hs_ready = sem("hs_ready"); hsT_ready = sem("hsT_ready"); ht_ready = sem("ht_ready")
        row_ready = sem("row_ready"); st_ready = sem("st_ready")
        st_out = [sem(f"st_out{s}") for s in range(RING)]
        ones_col = sem("ones_col")
        idx_ready = [sem(f"idx_ready{g}") for g in range(GPT)]
        gathered = [sem(f"gathered{g}") for g in range(GPT)]
        oh_ready = [[sem(f"oh_ready{l}{h}") for h in range(2)] for l in range(3)]
        pair_mm = [[sem(f"pair_mm{l}{h}") for h in range(2)] for l in range(3)]
        drained = [sem(f"drained{l}") for l in range(3)]
        m_row = sem("m_row"); m_T = sem("m_T"); m_xT = sem("m_xT"); m_P = sem("m_P"); m_min = sem("m_min")
        m_exp = sem("m_exp"); m_v = sem("m_v"); m_f = sem("m_f"); m_KV = sem("m_KV"); kv_ready = sem("kv_ready")
        n_t = sem("n_t"); n_mv = sem("n_mv"); n_sd = sem("n_sd"); n_x1 = sem("n_x1"); n_T = sem("n_T")
        n_x1T = sem("n_x1T"); n_h = sem("n_h"); n_g = sem("n_g"); n_y = sem("n_y")
        n_out = sem("n_out"); xo_in = sem("xo_in"); n_vo = sem("n_vo")
        deg_ready = sem("deg_ready"); deg_sd = sem("deg_sd"); nd_ready = sem("nd_ready")
        zero_out = sem("zero_out")
        r_u = sem("r_u"); u_kept = sem("u_kept"); r_vo = sem("r_vo"); r_T = sem("r_T"); r_uT = sem("r_uT"); r_l = sem("r_l"); r_lc = sem("r_lc")
        r_xs = sem("r_xs"); scat = [sem(f"scat{s}") for s in range(RING)]
        fm = sem("fm"); fe = sem("fe"); rank_mm = sem("rank_mm"); mask_ready = sem("mask_ready")
        slots_ready = sem("slots_ready"); pool_c = sem("pool_c")
        wx_in = [sem(f"wx_in{s}") for s in range(RING)]
        xs_in = sem("xs_in"); b_T = sem("b_T"); b_xT = sem("b_xT"); b_up = sem("b_up"); b_h = sem("b_h")
        b_y = sem("b_y"); b_yc = sem("b_yc"); b_out = sem("b_out")
        f_idx = sem("f_idx"); f_got = [sem(f"f_got{s}") for s in range(RING)]; f_vo = sem("f_vo")
        f_ready = sem("f_ready"); f_out = [sem(f"f_out{s}") for s in range(RING)]

        block = ctx.enter_context(nc.Block())

        def by_two(eng, body):
            with eng.Fori(0, NT // 2) as i:
                body(2 * i, 0, i)
                body(2 * i + 1, 1, i)
            body(NT - 1, 0, NT // 2)

        USES = [NT // 2 + 1, NT // 2]
        GATHERED = [P * NT] * (GPT - 1) + [P * (NT - 1) + 16 * LASTCH]

        @block.sync
        def _(sp):
            sp.wait_ge(raw_clear, 2)
            for e_dram, e_sb, s in ((dst, dst_i, dst_in), (src, src_i, src_in)):
                v = e_sb.rearrange("p (g e) -> p g e", e=P)
                full = FULLB * P * P
                sp.dma_start(v[:, 0:FULLB, :], e_dram[0:full].rearrange("(g q e) -> q g e", q=P, e=P)).then_inc(s, 16)
                sp.dma_start(v[0:TAILCH, FULLB, :],
                             e_dram[full:full + TAILCH * P].rearrange("(q e) -> q e", e=P)).then_inc(s, 16)
                sp.dma_start(v[TAILCH:TAILCH + 1, FULLB, 0:TAILE],
                             e_dram[full + TAILCH * P:E].rearrange("(q e) -> q e", q=1)).then_inc(s, 16)
            sp.wait_ge(gr_clear, 1)
            sp.dma_start(group_rows[:, 0, :], dst[0:P * GE].rearrange("(q e) -> q e", e=GE)).then_inc(gr_in, 16)
            sp.dma_start(group_rows[0:FULLG - P, 1, :],
                         dst[P * GE:FULLG * GE].rearrange("(q e) -> q e", e=GE)).then_inc(gr_in, 16)
            sp.dma_start(group_rows[FULLG - P:FULLG - P + 1, 1, :],
                         dst[E - GE:E].rearrange("(q e) -> q e", q=1)).then_inc(gr_in, 16)
            sp.wait_ge(c_vec, 1)
            sp.dma_start(nodes[:, 0:NT - 1, :], x[0:(NT - 1) * P, :].rearrange("(t p) d -> p t d", p=P)).then_inc(x_in, 16)
            sp.dma_start(nodes[0:LAST, NT - 1, :], x[(NT - 1) * P:N, :]).then_inc(x_in, 16)
            for l in range(3):
                sp.dma_start(wg[:, l, :, :], gnn_W[l].rearrange("(c p) n -> p c n", p=P)).then_inc(w_in, 16)
            sp.dma_start(wr[:, :, :], Wr.rearrange("(c p) n -> p c n", p=P)).then_inc(w_in, 16)
            for i, v in enumerate((gnn_b[0], gnn_b[1], gnn_b[2], ln1_g, ln1_b, ln2_g, ln2_b, mix_b2)):
                sp.dma_start(rows[:, i, :], v.rearrange("(a n) -> a n", a=1).broadcast_to([P, D])).then_inc(w_in, 16)
            sp.dma_start(br_row[:, :], br.rearrange("(a n) -> a n", a=1).broadcast_to([P, NX])).then_inc(w_in, 16)
            sp.dma_start(b1col[:, :], mix_b1.rearrange("(c p) -> p c", p=P), allow_slow_non_contiguous=True).then_inc(w_in, 16)
            for c_sb, c_dram in ((fgcol, ffn_g), (fbcol, ffn_b), (fb1col, ffn_b1)):
                v = c_dram.rearrange("e (c p) -> p e c", p=P)
                for e in range(NX):
                    sp.dma_start(c_sb[:, e, :], v[:, e, :], allow_slow_non_contiguous=True).then_inc(w_in, 16)
            sp.wait_ge(mm_ready, 1)
            for m in range(2):
                for j in range(2):
                    sp.dma_start(bounds_d[m:m + 1, j * P:(j + 1) * P].rearrange("m p -> p m"), mm[:, m, j:j + 1], allow_slow_non_contiguous=True).then_inc(bounds_out, 16)
            sp.wait_ge(bounds_out, 64)
            sp.dma_start(shift[0:1, :], bounds_d[0:1, :]).then_inc(bounds_in, 16)
            sp.dma_start(cum[0:1, :], bounds_d[1:2, :]).then_inc(bounds_in, 16)
            zr = zeros[:, 0:D].unsqueeze(1).broadcast_to([P, NBLK * BT // P, D])
            sp.dma_start(routed_in[0:SLOTS, :].rearrange("(a p) d -> p a d", p=P), zr).then_inc(zero_out, 16)
            zr = zeros[:, 0:D].unsqueeze(1).broadcast_to([P, (NBLK - LEAST) * BT // P, D])
            sp.dma_start(routed_out[LEAST * BT:SLOTS, :].rearrange("(a p) d -> p a d", p=P), zr).then_inc(zero_out, 16)

            def store_table(l):
                def tile(t, s, before_):
                    sp.wait_ge(st_ready, l * NT + t + 1 + RING)
                    sp.dma_start(tables[l][bass.ds(t * P, P), :], st[:, s, :]).then_inc(st_out[s], 16)
                by_two(sp, tile)

            store_table(0)
            store_table(1)
            def again(t, rows_):
                sp.wait_ge(n_out, t)
                sp.dma_start(xo[0:rows_, :], x[bass.ds(t * P, rows_), :]).then_inc(xo_in, 16)
            with sp.Fori(0, NT - 1) as t:
                again(t, P)
            again(NT - 1, LAST)
            store_table(2)

            sp.wait_ge(slots_ready, 1)
            sp.wait_ge(zero_out, 32)
            for s in range(RING):
                sp.wait_ge(scat[s], 32 * USES[s])
            last = sp.value_load(blk_no[0:1, NX:NX + 1], min_val=NX, max_val=NBLK)
            with sp.Fori(0, last) as b:
                sp.wait_ge(b_T, b)
                sp.dma_start(xs, routed_in[bass.ds(b * BT, BT), :].rearrange("(a p) d -> p a d", p=P)).then_inc(xs_in, 16)

            def store(t, s, rows_=P):
                sp.wait_ge(f_ready, t + 1)
                sp.dma_start(out[bass.ds(t * P, rows_), :], st[0:rows_, s, :]).then_inc(f_out[s], 16)
            with sp.Fori(0, NT // 2) as i:
                store(2 * i, 0)
                store(2 * i + 1, 1)
            store(NT - 1, 0, LAST)
            for s in range(RING):
                sp.wait_ge(f_out[s], 16 * USES[s])

        @block.gpsimd
        def _(pool):
            c = Chain(pool, po)
            pool.iota(node_no, [[1, NT * P]], base=0, channel_multiplier=0, allow_small_or_imprecise_dtypes=True).then_inc(c_iota, 1)
            pool.iota(iota_b[:, :], [[1, P]], base=0, channel_multiplier=0, allow_small_or_imprecise_dtypes=True).then_inc(c_iota, 1)
            pool.memset(ident[:, :], 0.0)
            pool.memset(before[:, :], 1.0)
            pool.memset(ones[:, :], 1.0)
            pool.memset(valid[:, :], 1.0)
            c.link(pool.iota(dump[:, :], [[0, NT]], base=SLOTS, channel_multiplier=1, allow_small_or_imprecise_dtypes=True))
            pool.affine_select(out=ident[:, :], in_=ident[:, :], compare_op=ALU.not_equal, fill=1.0, base=0,
                               pattern=[[-1, P]], channel_multiplier=1)
            pool.affine_select(out=before[:, :], in_=before[:, :], compare_op=ALU.is_gt, fill=0.0, base=0,
                               pattern=[[1, P]], channel_multiplier=-1)
            pool.affine_select(out=valid[:, :], in_=valid[:, :], compare_op=ALU.is_ge, fill=0.0, base=N - 1,
                               pattern=[[-P, NT]], channel_multiplier=-1)
            pool.affine_select(out=dump[:, :], in_=dump[:, :], compare_op=ALU.is_ge, fill=0.0, base=-N,
                               pattern=[[P, NT]], channel_multiplier=1)
            pool.iota(desc8[:, :], [[-1, NX]], base=NX, channel_multiplier=0, allow_small_or_imprecise_dtypes=True)
            pool.memset(vaug[:, :, P:P + 1], 1.0).then_inc(c_mat, 1)

            for l in range(3):
                for s in range(RING):
                    pool.wait_ge(st_out[s], 16 * USES[s] * (l + 1))
                if l == 0:
                    pool.wait_ge(ones_col, 1)
                    pool.wait_ge(cum_ready, 1)

                def gather(t, g, chunks):
                    k = t * GPT + g
                    free = pool.value_load(cum[0:1, bass.ds(k, 1)], min_val=0, max_val=NG * NT)
                    pool.wait_ge(pair_mm[l][1], free)
                    pool.wait_ge(idx_ready[g], l * NT + t + 1)
                    pool.sem_inc(pool_past, 1)
                    for j in range(chunks):
                        pool.indirect_dma_start(
                            out=msgs[:, g * GC + j, 0:D], out_offset=None, in_=tables[l],
                            in_offset=bass.IndirectOffsetOnAxis(ap=idx[:, g, j:j + 1].bitcast(U32), axis=0)
                        ).then_inc(gathered[g], 16)
                with pool.Fori(0, NT - 1) as t:
                    for g in range(GPT):
                        gather(t, g, GC)
                for g in range(GPT):
                    gather(NT - 1, g, GC if g < GPT - 1 else LASTCH)

            pool.wait_ge(slots_ready, 1)
            pool.wait_ge(zero_out, 32)

            def scatter(t, s, before_):
                pool.wait_ge(r_xs, t + 1)
                pool.sem_inc(pool_past, 1)
                for k in range(2):
                    pool.indirect_dma_start(
                        out=routed_in, out_offset=bass.IndirectOffsetOnAxis(ap=sidx[:, s, k:k + 1].bitcast(U32), axis=0),
                        in_=st[:, s, :], in_offset=None).then_inc(scat[s], 16)
            by_two(pool, scatter)

            def weights(e, s):
                if not (isinstance(e, int) and e < RING):
                    pool.wait_ge(b_y, pool.value_load(blk_no[0:1, bass.ds(e - 1, 1)], min_val=0, max_val=NBLK))
                pool.dma_start(w_up[s], ffn_W1[bass.ds(e, 1), :, :].rearrange("e (c p) n -> p (e c) n", p=P)).then_inc(wx_in[s], 16)
                pool.dma_start(w_dn[s], ffn_W2[bass.ds(e, 1), :, :].rearrange("e (m p) n -> p (e m) n", p=P)).then_inc(wx_in[s], 16)
                pool.dma_start(fb2row[0:1, s, :], ffn_b2[bass.ds(e, 1), :]).then_inc(wx_in[s], 16)

            def stores(e):
                lo = pool.value_load(blk_no[0:1, bass.ds(e, 1)], min_val=0, max_val=NBLK)
                hi = pool.value_load(blk_no[0:1, bass.ds(e + 1, 1)], min_val=0, max_val=NBLK)
                with pool.Fori(lo, hi) as b:
                    pool.wait_ge(b_yc, b + 1)
                    pool.dma_start(routed_out[bass.ds(b * BT, BT), :].rearrange("(a p) d -> p a d", p=P), ys).then_inc(b_out, 16)
            weights(0, 0)
            weights(1, 1)
            with pool.Fori(0, NX // 2 - 1) as i:
                stores(2 * i)
                weights(2 * i + 2, 0)
                stores(2 * i + 1)
                weights(2 * i + 3, 1)
            stores(NX - 2)
            stores(NX - 1)

            total = pool.value_load(blk_no[0:1, NX:NX + 1], min_val=NX, max_val=NBLK)
            pool.wait_ge(b_out, total * 16)
            pool.sem_inc(pool_past, 1)

            def fetch(t, s, before_):
                pool.wait_ge(f_idx, t + 1)
                pool.sem_inc(pool_past, 1)
                for k, to in ((0, hs), (1, hT)):
                    pool.indirect_dma_start(
                        out=to[:, s, :], out_offset=None, in_=routed_out,
                        in_offset=bass.IndirectOffsetOnAxis(ap=sidx[:, s, k:k + 1].bitcast(U32), axis=0)
                    ).then_inc(f_got[s], 16)
            by_two(pool, fetch)

        @block.tensor
        def _(pe):
            pe.wait_ge(c_mat, 1)
            pe.wait_ge(c_vec, 1)
            pe.sem_inc(hist_used, RING)
            pe.sem_inc(hsT_ready, RING)
            pe.sem_inc(row_ready, RING)
            pe.wait_ge(edges_f, 2)
            n = 0
            for v in (dst_f, src_f):
                for b0 in range(0, CB, 4):
                    if n >= 2:
                        pe.wait_ge(edges_c, n - 1)
                    ps = (psA, psB)[n % 2]
                    for b in range(b0, min(b0 + 4, CB)):
                        mm_ = pe.transpose(ps[:, (b - b0) * P:(b - b0 + 1) * P], v[:, b * P:(b + 1) * P], ident[:, :])
                    mm_.then_inc(edgesT, 1)
                    n += 1
            pe.wait_ge(wraw_in, 16 * 3)
            for i, (raw, _, c_, o0, nb) in enumerate(turned):
                pe.wait_ge((edges_c if i < 2 else wT_out), (n - 1 + i if i < 2 else i - 1))
                for o in range(nb):
                    mm_ = pe.transpose((psA, psB)[i % 2][:, o * P:(o + 1) * P], raw[:, o0 + o, c_ * P:(c_ + 1) * P], ident[:, :])
                mm_.then_inc(wT, 1)
            zb = zeros[:, :].bitcast(BF16)
            pe.matmul(psH[:, 0:NT], zb[:, 0:P], zb[:, 0:NT], start=True, stop=False)
            with pe.Fori(0, NG // 2) as i:
                for s in range(RING):
                    pe.wait_ge(hist_oh, 2 * i + s + 1)
                    for j in range(GC):
                        mm_ = pe.matmul(psH[:, 0:NT], onehot_lo[:, s, j, :], onehot_hi[:, s, j, 0:NT], start=False, stop=False)
                    mm_.then_inc(hist_used, 1)
            pe.matmul(psH[:, 0:NT], zb[:, 0:P], zb[:, 0:NT], start=False, stop=True).then_inc(hist_done, 1)

            def turn(l, t, s):
                pe.wait_ge(hs_ready, l * NT + t + 1)
                pe.wait_ge(ht_ready, l * NT + t + 1)
                for c_ in range(HALVES):
                    mm_ = pe.transpose(psT[s][:, c_ * P:(c_ + 1) * P], hs[:, s, c_ * P:(c_ + 1) * P], ident[:, :])
                mm_.then_inc(hsT_ready, 1)

            def project(l, t, s):
                pe.wait_ge(ht_ready, l * NT + t + 1 + RING)
                if l < 3:
                    pe.wait_ge(st_ready, l * NT + t + 1)
                for c_ in range(HALVES):
                    lhs = hT[:, s, c_ * P:(c_ + 1) * P]
                    if l < 3:
                        mm_ = pe.matmul(psO[s][:, 0:D], lhs, wg[:, l, c_, :], start=(c_ == 0), stop=(c_ == HALVES - 1))
                    else:
                        mm_ = pe.matmul(psH[:, bass.ds(t * NX, NX)], lhs, wr[:, c_, :], start=(c_ == 0), stop=(c_ == HALVES - 1))
                mm_.then_inc(row_ready, 1)

            def table(l):
                turn(l, 0, 0)
                with pe.Fori(0, NT // 2) as i:
                    turn(l, 2 * i + 1, 1)
                    project(l, 2 * i, 0)
                    turn(l, 2 * i + 2, 0)
                    project(l, 2 * i + 1, 1)
                project(l, NT - 1, 0)

            def pairs(l, t, g, full=True):
                k = t * GPT + g
                lo = pe.value_load(cum[0:1, bass.ds(k + 3, 1)], min_val=0, max_val=NG * NT)
                hi = pe.value_load(cum[0:1, bass.ds(k + 4, 1)], min_val=0, max_val=NG * NT)
                pe.wait_ge(gathered[g], l * GATHERED[g] + (P * (t + 1) if full else GATHERED[g]))
                pe.sem_inc(pe_past, 1)
                with pe.Fori(lo, hi) as p:
                    pe.wait_ge(drained[l], p)
                    for h in range(2):
                        pe.wait_ge(oh_ready[l][h], p + 1)
                        for j in range(GC // 2):
                            jj = h * GC // 2 + j
                            mm_ = pe.matmul(acc, onehot[:, h, j, :], msgs[:, g * GC + jj, :], start=(jj == 0), stop=(jj == GC - 1))
                        mm_.then_inc(pair_mm[l][h], 1)

            def kv_step(t, g, rows_=P):
                if g == 0:
                    pe.wait_ge(m_row, t + 1)
                    pe.wait_ge(m_xT, t)
                    for c_ in range(HALVES):
                        mm_ = pe.transpose(psA[:, c_ * P:(c_ + 1) * P], mrow[:, c_ * P:(c_ + 1) * P], ident[:, :])
                    mm_.then_inc(m_T, 1)
                if g == 1:
                    pe.wait_ge(m_xT, t + 1)
                    pe.wait_ge(m_f, t)
                    pe.wait_ge(m_v, t)
                    for ps, o in ((psB, D), (psC, 2 * D)):
                        for c_ in range(HALVES):
                            mm_ = pe.matmul(ps[:, 0:D], mT[:, c_ * P:(c_ + 1) * P], wqkvT[:, c_, o:o + D], start=(c_ == 0), stop=(c_ == HALVES - 1))
                    mm_.then_inc(m_P, 1)
                if g == 3:
                    pe.wait_ge(m_f, t + 1)
                    pe.wait_ge(m_v, t + 1)
                    for c_ in range(HALVES):
                        mm_ = pe.matmul(psKV[:, c_ * (P + 1):(c_ + 1) * (P + 1)], mfeat[0:rows_, c_ * P:(c_ + 1) * P],
                                        vaug[0:rows_, c_, :], start=False, stop=False)
                    mm_.then_inc(m_KV, 1)

            def mix_step(t, g):
                if g == 0:
                    pe.wait_ge(m_row, NT + t + 1)
                    pe.wait_ge(n_x1T, t)
                    for c_ in range(HALVES):
                        mm_ = pe.transpose(psA[:, c_ * P:(c_ + 1) * P], mrow[:, c_ * P:(c_ + 1) * P], ident[:, :])
                    mm_.then_inc(m_T, 1)
                    pe.wait_ge(m_xT, NT + t + 1)
                    pe.wait_ge(n_g, 2 * t)
                    for o in range(HALVES):
                        for c_ in range(HALVES):
                            mm_ = pe.matmul(psB[:, o * P:(o + 1) * P], wqkvT[:, c_, o * P:(o + 1) * P],
                                            mT[:, c_ * P:(c_ + 1) * P], start=(c_ == 0), stop=(c_ == HALVES - 1))
                    mm_.then_inc(m_P, 1)
                if g == 1:
                    pe.wait_ge(m_f, NT + t + 1)
                    pe.wait_ge(n_out, t)
                    for o in range(HALVES):
                        mm_ = pe.matmul(psC[:, o * (P + HPB):(o + 1) * (P + HPB)], mfeat[:, o * P:(o + 1) * P], kvblk[:, o, :], start=True, stop=True)
                    mm_.then_inc(n_t, 1)
                if g == 2:
                    pe.wait_ge(n_x1, t + 1)
                    for c_ in range(HALVES):
                        mm_ = pe.transpose(psA[:, c_ * P:(c_ + 1) * P], x1[:, c_ * P:(c_ + 1) * P], ident[:, :])
                    mm_.then_inc(n_T, 1)
                    pe.wait_ge(n_x1T, t + 1)
                    for o in range(HALVES):
                        for c_ in range(HALVES):
                            mm_ = pe.matmul(psB[:, o * P:(o + 1) * P], w1T[:, c_, o * P:(o + 1) * P],
                                            mT[:, c_ * P:(c_ + 1) * P], start=(c_ == 0), stop=(c_ == HALVES - 1))
                    mm_.then_inc(n_h, 1)
                if g == 3:
                    pe.wait_ge(n_g, 2 * t + 2)
                    for c_ in range(HALVES):
                        mm_ = pe.matmul(psC[:, 0:D], mfeat[:, c_ * P:(c_ + 1) * P], w2T[:, c_, :], start=(c_ == 0), stop=(c_ == HALVES - 1))
                    mm_.then_inc(n_y, 1)

            pe.matmul(psKV, zeros[:, 0:P], zeros[:, 0:HALVES * (P + 1)], start=True, stop=False)
            for l in range(3):
                table(l)
                if l == 0:
                    pe.wait_ge(cum_ready, 1)
                    pe.wait_ge(ones_col, 1)
                with pe.Fori(0, NT - 1) as t:
                    for g in range(GPT):
                        if l == 0:
                            kv_step(t, g)
                        if l == 1:
                            mix_step(t, g)
                        pairs(l, t, g)
                for g in range(GPT):
                    if l == 0:
                        kv_step(NT - 1, g, LAST)
                    if l == 1:
                        mix_step(NT - 1, g)
                    pairs(l, NT - 1, g, g < GPT - 1)
                if l == 0:
                    pe.matmul(psKV, zeros[:, 0:P], zeros[:, 0:HALVES * (P + 1)], start=False, stop=True).then_inc(m_KV, 1)

            table(3)
            pe.wait_ge(mask_ready, 1)
            pe.matmul(psA[:, 0:NE], before[:, :], pick, start=True, stop=True)
            pe.matmul(psB[:, 0:NE], ones[:, :], pick, start=True, stop=True).then_inc(rank_mm, 1)

            psX = bank[1]
            ups = [bank[4 + i] for i in range(4)]
            psY = [bank[2], bank[3]]
            pe.wait_ge(slots_ready, 1)

            def up(b, m, s):
                pe.wait_ge(b_h, b * MH + m + 1)
                for c_ in range(HALVES):
                    mm_ = pe.matmul(ups[m % 4][:, 0:BT], w_up[s][:, c_, m * P:(m + 1) * P], xeT[:, c_, :],
                                    start=(c_ == 0), stop=(c_ == HALVES - 1))
                mm_.then_inc(b_up, 1)

            def down(b, m, s):
                pe.wait_ge(b_h, b * MH + m + 1 + 4)
                for a in range(2):
                    mm_ = pe.matmul(psY[a][:, 0:D], hidT[:, m, a * P:(a + 1) * P], w_dn[s][:, m, :], start=False, stop=(m == MH - 1))
                return mm_

            def expert(e, s, i):
                lo = pe.value_load(blk_no[0:1, bass.ds(e, 1)], min_val=0, max_val=NBLK)
                hi = pe.value_load(blk_no[0:1, bass.ds(e + 1, 1)], min_val=0, max_val=NBLK)
                pe.wait_ge(wx_in[s], 48 * (i + 1))
                pe.sem_inc(pe_past, 1)
                with pe.Fori(lo, hi) as b:
                    pe.wait_ge(xs_in, 16 * (b + 1))
                    pe.wait_ge(b_xT, b)
                    for c_ in range(HALVES):
                        for a in range(2):
                            mm_ = pe.transpose(psX[:, c_ * BT + a * P:c_ * BT + (a + 1) * P], xs[:, a, c_ * P:(c_ + 1) * P], ident[:, :])
                    mm_.then_inc(b_T, 1)
                    pe.wait_ge(b_yc, b)
                    for a in range(2):
                        pe.matmul(psY[a][:, 0:D], ones[0:1, :], fb2row[0:1, s, :], start=True, stop=False)
                    pe.wait_ge(b_xT, b + 1)
                    up(b, 0, s)
                    for m in range(1, MH):
                        up(b, m, s)
                        down(b, m - 1, s)
                    down(b, MH - 1, s).then_inc(b_y, 1)
            with pe.Fori(0, NX // 2) as i:
                expert(2 * i, 0, i)
                expert(2 * i + 1, 1, i)

        @block.scalar
        def _(act):
            act.sem_inc(ht_ready, RING)
            act.sem_inc(st_ready, RING)
            act.sem_inc(b_h, 4)
            for raw, w_dram in ((raw_qkv, Wqkv), (raw_w1, mix_W1), (raw_w2, mix_W2)):
                act.dma_start(raw, w_dram.rearrange("(o p) c -> p o c", p=P)).then_inc(wraw_in, 16)
            n = 0
            for v in (dst_c[:, :], src_t):
                for b0 in range(0, CB, 4):
                    w = min(4, CB - b0) * P
                    act.wait_ge(edgesT, n + 1)
                    act.activation(v[:, b0 * P:b0 * P + w], (psA, psB)[n % 2][:, 0:w], ACT.Copy).then_inc(edges_c, 1)
                    n += 1
            for i, (_, to, c_, o0, nb) in enumerate(turned):
                act.wait_ge(wT, i + 1)
                act.activation(to[:, c_, o0 * P:(o0 + nb) * P], (psA, psB)[i % 2][:, 0:nb * P], ACT.Copy).then_inc(wT_out, 1)
            act.wait_ge(deg_ready, 1)
            act.activation(norm_src[:, :], deg[:, :], ACT.Sqrt).then_inc(deg_sd, 1)
            act.wait_ge(mv_ready, 1)
            act.activation(rstd[:, :], mv[:, :, 1], ACT.Sqrt, bias=eps_ln[:, 0:1]).then_inc(sd_ready, 1)

            def copy_turned(l, t, s):
                act.wait_ge(hsT_ready, l * NT + t + 1 + RING)
                act.wait_ge(row_ready, l * NT + t + 1)
                act.activation(hT[:, s, :], psT[s][:, 0:D], ACT.Copy).then_inc(ht_ready, 1)

            def copy_row(l, t, s, before_):
                act.wait_ge(row_ready, l * NT + t + 1 + RING)
                act.wait_ge(st_out[s], 16 * (l * USES[s] + before_))
                act.activation(st[:, s, :], psO[s][:, 0:D], ACT.Copy).then_inc(st_ready, 1)

            def copy_idx(l, t, g, k):
                act.wait_ge(gathered[g], l * GATHERED[g] + t * P)
                act.activation(idx[:, g, :], src_c[:, bass.ds(k * GC, GC)], ACT.Copy).then_inc(idx_ready[g], 1)

            def kv_step(t, g):
                if g == 0:
                    act.wait_ge(m_T, t)
                    act.activation(mrow[:, :], nodes[:, bass.ds(t, 1), :], ACT.Copy).then_inc(m_row, 1)
                    act.wait_ge(m_T, t + 1)
                    act.wait_ge(m_P, t)
                    act.activation(mT[:, :], psA[:, 0:D], ACT.Copy).then_inc(m_xT, 1)
                if g == 2:
                    act.wait_ge(m_P, t + 1)
                    act.wait_ge(m_KV, t)
                    act.activation(vaug[:, :, 0:P], psC[:, 0:D].rearrange("p (c n) -> p c n", c=HALVES), ACT.Copy).then_inc(m_v, 1)
                    act.wait_ge(m_min, t + 1)
                    act.wait_ge(m_f, t)
                    act.activation(mexp[:, :], melu[:, :], ACT.Exp).then_inc(m_exp, 1)

            def mix_step(t, g):
                if g == 0:
                    act.wait_ge(m_T, NT + t)
                    act.wait_ge(n_x1, t)
                    act.activation(mrow[:, :], nodes[:, bass.ds(t, 1), :], ACT.Copy).then_inc(m_row, 1)
                    act.wait_ge(m_T, NT + t + 1)
                    act.wait_ge(n_h, t)
                    act.activation(mT[:, :], psA[:, 0:D], ACT.Copy).then_inc(m_xT, 1)
                    act.wait_ge(m_min, NT + t + 1)
                    act.wait_ge(m_f, NT + t)
                    act.activation(mexp[:, :], melu[:, :], ACT.Exp).then_inc(m_exp, 1)
                if g == 1:
                    act.wait_ge(n_mv, 2 * t + 1)
                    act.activation(sd1[:, :], mv1[:, 1:2], ACT.Sqrt, bias=eps_ln[:, 0:1]).then_inc(n_sd, 1)
                if g == 2:
                    act.wait_ge(n_T, t + 1)
                    act.wait_ge(m_P, NT + t + 1)
                    act.activation(mT[:, :], psA[:, 0:D], ACT.Copy).then_inc(n_x1T, 1)
                    act.wait_ge(n_h, t + 1)
                    act.wait_ge(n_t, t + 1)
                    for o in range(HALVES):
                        act.activation(mfeat[:, o * P:(o + 1) * P], psB[:, o * P:(o + 1) * P], ACT.Gelu, bias=b1col[:, o:o + 1]).then_inc(n_g, 1)
                if g == 3:
                    act.wait_ge(n_mv, 2 * t + 2)
                    act.activation(sd1[:, :], mv1[:, 1:2], ACT.Sqrt, bias=eps_ln[:, 0:1]).then_inc(n_sd, 1)

            for l in range(3):
                copy_turned(l, 0, 0)
                with act.Fori(0, NT // 2) as i:
                    copy_turned(l, 2 * i + 1, 1)
                    copy_row(l, 2 * i, 0, i)
                    copy_turned(l, 2 * i + 2, 0)
                    copy_row(l, 2 * i + 1, 1, i)
                copy_row(l, NT - 1, 0, NT // 2)
                if l == 0:
                    act.wait_ge(src_ready, 1)
                with act.Fori(0, NT) as t:
                    for g in range(GPT):
                        copy_idx(l, t, g, t * GPT + g)
                        if l == 0:
                            kv_step(t, g)
                        if l == 1:
                            mix_step(t, g)
                if l == 0:
                    act.wait_ge(deg_ready, 2)
                    act.activation(norm_dst[:, :], deg[:, :], ACT.Sqrt).then_inc(deg_sd, 1)

            act.wait_ge(mv_ready, 2)
            act.activation(rstd[:, :], mv[:, :, 1], ACT.Sqrt, bias=eps_ln[:, 0:1]).then_inc(sd_ready, 1)
            by_two(act, lambda t, s, before_: copy_turned(3, t, s))
            act.wait_ge(mv_ready, 3)
            act.activation(rstd[:, :], mv[:, :, 1], ACT.Sqrt, bias=eps_ln[:, 0:1]).then_inc(sd_ready, 1)
            act.wait_ge(fm, 1)
            act.activation(gate2[:, :], gate1[:, :], ACT.Exp).then_inc(fe, 1)

            act.wait_ge(slots_ready, 1)
            with act.Fori(0, NX) as e:
                lo = act.value_load(blk_no[0:1, bass.ds(e, 1)], min_val=0, max_val=NBLK)
                hi = act.value_load(blk_no[0:1, bass.ds(e + 1, 1)], min_val=0, max_val=NBLK)
                with act.Fori(lo, hi) as b:
                    act.wait_ge(b_y, b)
                    for m in range(MH):
                        act.wait_ge(b_up, b * MH + m + 1)
                        act.activation(hidT[:, m, :], bank[4 + m % 4][:, 0:BT], ACT.Gelu,
                                       bias=fb1col[:, bass.ds(e, 1), m:m + 1]).then_inc(b_h, 1)

        @block.vector
        def _(dve):
            c = Chain(dve, vo)

            def copy(to, of):
                return dve.tensor_scalar(to, of, 1.0, None, ALU.mult)

            dve.memset(dst_i, -1).then_inc(raw_clear, 1)
            dve.memset(src_i, -1).then_inc(raw_clear, 1)
            dve.memset(group_rows, 0).then_inc(gr_clear, 1)
            dve.memset(zeros[:, :], 0.0)
            dve.memset(eps_ln[:, :], LN_EPS)
            dve.memset(cum[:, :], 0)
            dve.memset(cnt_f[:, :, :], 1.0)
            dve.memset(kvblk[:, :, :], 0.0)
            c.link(dve.memset(nodes[:, NT - 1, :], 0.0))
            dve.sem_inc(c_vec, 1)
            dve.wait_ge(dst_in, 48)
            dve.tensor_copy(dst_f, dst_i).then_inc(edges_f, 1)
            dve.wait_ge(src_in, 48)
            dve.tensor_copy(src_f, src_i).then_inc(edges_f, 1)
            dve.wait_ge(gr_in, 48)
            dve.tensor_reduce(mm[:, 0, :], group_rows, AX_X, ALU.min)
            c.link(dve.tensor_reduce(mm[:, 1, :], group_rows, AX_X, ALU.max))
            dve.tensor_scalar(mm[:, :, :], mm[:, :, :], 7, None, ALU.arith_shift_right).then_inc(mm_ready, 1)
            dve.wait_ge(edges_c, 2 * -(-CB // 4))
            dve.tensor_scalar(src_c[:, :], src_t, 0.0, None, ALU.max).then_inc(src_ready, 1)
            c.link(dve.tensor_scalar(hi_i, src_t, 7, None, ALU.arith_shift_right))
            c.link(dve.tensor_scalar(src_t, src_t, P - 1, None, ALU.bitwise_and))
            dve.tensor_copy(hi_f, hi_i)
            c.link(dve.tensor_copy(lo_f, src_t))
            dve.wait_ge(c_iota, 2)
            with dve.Fori(0, NG // 2) as i:
                for s in range(RING):
                    dve.wait_ge(hist_used, 2 * i + s + 1)
                    for j in range(GC):
                        dve.tensor_scalar(onehot_lo[:, s, j, :], iota_b[:, :],
                                                lo_f[:, bass.ds((2 * i + s) * GC + j, 1)], None, ALU.is_equal)
                    dve.tensor_tensor(onehot_hi[:, s, :, 0:NT],
                                      hi_f[:, bass.ds((2 * i + s) * GC, GC)].unsqueeze(2).broadcast_to([P, GC, NT]),
                                      iota_b[:, 0:NT].unsqueeze(1).broadcast_to([P, GC, NT]), ALU.is_equal).then_inc(hist_oh, 1)
            dve.wait_ge(bounds_in, 32)
            lo_r, hi_r = shift[0:1, 0:NG], cum[0:1, 0:NG]
            c.link(dve.tensor_tensor(cnt_f[0:1, 0, 0:NG], hi_r, lo_r, ALU.subtract))
            c.link(dve.tensor_scalar(cnt_f[0:1, 0, 0:NG], cnt_f[0:1, 0, 0:NG], 1.0, None, ALU.add))
            c.link(dve.tensor_tensor_scan(cnt_f[0:1, 1, 0:NG], cnt_f[0:1, 3, 0:NG], cnt_f[0:1, 0, 0:NG], 0.0, ALU.mult, ALU.add))
            c.link(dve.tensor_tensor(cnt_f[0:1, 2, 0:NG], cnt_f[0:1, 1, 0:NG], cnt_f[0:1, 0, 0:NG], ALU.subtract))
            c.link(dve.tensor_tensor(shift[0:1, 0:NG], lo_r, cnt_f[0:1, 2, 0:NG], ALU.subtract))
            c.link(dve.memset(cum[0:1, 0:4], 0))
            c.link(dve.tensor_copy(cum[0:1, 4:4 + NG], cnt_f[0:1, 1, 0:NG]))
            dve.sem_inc(cum_ready, 1)
            dve.wait_ge(hist_done, 1)
            dve.memset(msgs[:, :, D:D + 1], 1.0).then_inc(ones_col, 1)
            dve.tensor_scalar(deg[:, :], psH[:, 0:NT], 1.0, None, ALU.max).then_inc(deg_ready, 1)
            dve.wait_ge(wT, len(turned))
            dve.wait_ge(mm_ready, 1)
            c.link(dve.memset(agg[:, :, :], 0.0))
            dve.wait_ge(deg_sd, 1)
            c.link(dve.reciprocal(norm_src[:, :], norm_src[:, :]))

            def stats(l, src_of, order):
                with dve.Fori(0, NT) as t:
                    k = Chain(dve, order, (l * NT + t) * 3)
                    k.link(dve.bn_stats(st6[:, :], src_of(t)), dve_past)
                    k.link(dve.bn_aggr(mv1[:, :], st6[:, :]))
                    k.link(copy(mv[:, bass.ds(t, 1), :], mv1[:, :].unsqueeze(1)), dve_past)
                dve.sem_inc(mv_ready, 1)

            dve.wait_ge(x_in, 32)
            stats(0, lambda t: nodes[:, bass.ds(t, 1), :], r_vo)
            dve.wait_ge(sd_ready, 1)
            c.link(dve.reciprocal(rstd[:, :], rstd[:, :]))
            with dve.Fori(0, NT) as t:
                dve.tensor_scalar(nodes[:, bass.ds(t, 1), :], nodes[:, bass.ds(t, 1), :], mv[:, bass.ds(t, 1), 0:1],
                                  rstd[:, bass.ds(t, 1)], ALU.subtract, ALU.mult).then_inc(xn_ready, 1)
            dve.wait_ge(xn_ready, NT)

            def scaled(l):
                gb = (None, gb0, gb1)[l]
                def tile(t, s, before_):
                    dve.wait_ge(hsT_ready, l * NT + t + 1)
                    ns = norm_src[:, bass.ds(t, 1)]
                    if l == 0:
                        dve.tensor_scalar(hs[:, s, :], nodes[:, bass.ds(t, 1), :], ns, None, ALU.mult).then_inc(hs_ready, 1)
                        return
                    k = Chain(dve, f_vo, (l - 1) * NT + t)
                    dve.wait_ge(hs_ready, l * NT + t)
                    k.link(dve.scalar_tensor_tensor(out=tmp[:, :], in0=agg[:, bass.ds(t, 1), 0:D], scalar=norm_dst[:, bass.ds(t, 1)],
                                                    in1=gb, op0=ALU.mult, op1=ALU.add))
                    dve.tensor_scalar(hs[:, s, :], tmp[:, :], 0.0, ns, ALU.max, ALU.mult).then_inc(hs_ready, 1)
                    copy(agg[:, bass.ds(t, 1), :], zeros[:, 0:D + 1].unsqueeze(1)).then_inc(agg_clear, 1)
                by_two(dve, tile)
                if l:
                    dve.wait_ge(agg_clear, l * NT)

            def pairs(l, t, g):
                k = t * GPT + g
                lo = dve.value_load(cum[0:1, bass.ds(k + 3, 1)], min_val=0, max_val=NG * NT)
                hi = dve.value_load(cum[0:1, bass.ds(k + 4, 1)], min_val=0, max_val=NG * NT)
                off = dve.value_load(shift[0:1, bass.ds(k, 1)], min_val=-NG * NT, max_val=NT)
                with dve.Fori(lo, hi) as p:
                    b = nc.s_assert_within(dve.snap(p + off), 0, NT - 1,
                                           skip_runtime_bounds_check_because="pairs name tiles first to last of a group")
                    for h in range(2):
                        dve.wait_ge(pair_mm[l][h], p)
                        dve.tensor_tensor(onehot[:, h, :, :],
                                          dst_c[:, bass.ds(k * GC + h * (GC // 2), GC // 2)].unsqueeze(2).broadcast_to([P, GC // 2, P]),
                                          node_no[:, bass.ds(b * P, P)].unsqueeze(1).broadcast_to([P, GC // 2, P]),
                                          ALU.is_equal).then_inc(oh_ready[l][h], 1)
                    dve.wait_ge(pair_mm[l][1], p + 1)
                    dve.wait_ge(drained[l], p)
                    dve.tensor_tensor(agg[:, bass.ds(b, 1), :], agg[:, bass.ds(b, 1), :], acc.unsqueeze(1), ALU.add).then_inc(drained[l], 1)

            def elu_part(base, t, free, free_at):
                dve.wait_ge(m_P, base + t + 1)
                dve.wait_ge(m_exp, base + t)
                dve.tensor_scalar(melu[:, :], psB[:, 0:D], 0.0, None, ALU.min).then_inc(m_min, 1)
                dve.wait_ge(m_exp, base + t + 1)
                dve.wait_ge(free, free_at)
                dve.scalar_tensor_tensor(out=mfeat[:, :], in0=psB[:, 0:D], scalar=0.0, in1=mexp[:, :],
                                         op0=ALU.max, op1=ALU.add).then_inc(m_f, 1)

            def normalise(k, v, g_row, b_row, t, n):
                k.link(dve.bn_stats(st6[:, :], v), dve_past)
                dve.bn_aggr(mv1[:, :], st6[:, :]).then_inc(n_mv, 1)
                dve.wait_ge(n_sd, 2 * t + n)
                k.link(dve.reciprocal(sd1[:, :], sd1[:, :]))
                k.link(dve.tensor_scalar(v, v, mv1[:, 0:1], sd1[:, 0:1], ALU.subtract, ALU.mult))
                k.link(dve.tensor_tensor(v, v, g_row, ALU.mult))

            K1, K2 = 8, 7

            def mix_step(t, g):
                if g == 0:
                    elu_part(NT, t, n_y, t)
                if g == 1:
                    k = Chain(dve, n_vo, t * (K1 + K2))
                    dve.wait_ge(n_t, t + 1)
                    pv = psC[:, 0:HALVES * (P + HPB)].rearrange("p (c n) -> p c n", c=HALVES)
                    k.link(dve.tensor_scalar(z[:, :, :], pv[:, :, P:P + HPB], ATTN_EPS, None, ALU.add))
                    k.link(dve.reciprocal(z[:, :, :], z[:, :, :]))
                    dve.wait_ge(n_T, t)
                    k.link(dve.tensor_tensor(x1[:, :].rearrange("p (c h n) -> p c h n", c=HALVES, h=HPB),
                                             pv[:, :, 0:P].rearrange("p c (h n) -> p c h n", h=HPB),
                                             z[:, :, :].unsqueeze(3).broadcast_to([P, HALVES, HPB, HD]), ALU.mult))
                    k.link(dve.tensor_tensor(x1[:, :], x1[:, :], mrow[:, :], ALU.add), dve_past)
                    normalise(k, x1[:, :], r1g, r1b, t, 1)
                    assert k.n == K1
                    dve.tensor_tensor(x1[:, :], x1[:, :], r1b, ALU.add).then_inc(n_x1, 1)
                if g == 3:
                    k = Chain(dve, n_vo, t * (K1 + K2) + K1)
                    dve.wait_ge(n_y, t + 1)
                    dve.wait_ge(n_x1, t + 1)
                    k.link(dve.tensor_tensor(tmp[:, :], psC[:, 0:D], rb2, ALU.add))
                    k.link(dve.tensor_tensor(tmp[:, :], tmp[:, :], x1[:, :], ALU.add), dve_past)
                    normalise(k, tmp[:, :], r2g, r2b, t, 2)
                    k.link(dve.tensor_tensor(tmp[:, :], tmp[:, :], r2b, ALU.add))
                    assert k.n == K2
                    dve.wait_ge(xo_in, 16 * (t + 1))
                    dve.tensor_tensor(nodes[:, bass.ds(t, 1), :], tmp[:, :].unsqueeze(1), xo[:, :].unsqueeze(1), ALU.add).then_inc(n_out, 1)

            dve.wait_ge(w_in, 16 * (3 + 1 + 8 + 1 + 1 + 3 * NX))
            for l in range(3):
                scaled(l)
                with dve.Fori(0, NT) as t:
                    for g in range(GPT):
                        if l == 0 and g == 2:
                            elu_part(0, t, m_KV, t)
                        if l == 1:
                            mix_step(t, g)
                        pairs(l, t, g)
                if l == 0:
                    dve.wait_ge(deg_sd, 1)
                    total = dve.value_load(cum[0:1, NG + 3:NG + 4], min_val=0, max_val=NG * NT)
                    dve.wait_ge(drained[0], total)
                    dve.sem_inc(dve_past, 1)
                    dve.tensor_scalar(deg[:, :], agg[:, :, D], 1.0, None, ALU.max).then_inc(deg_ready, 1)
                    dve.wait_ge(m_KV, NT + 1)
                    for c_ in range(HALVES):
                        for h in range(HPB):
                            q, kv = slice(h * HD, (h + 1) * HD), c_ * (P + 1)
                            dve.tensor_copy(kvblk[q, c_, h * HD:(h + 1) * HD], psKV[q, kv + h * HD:kv + (h + 1) * HD])
                            ins = dve.tensor_copy(kvblk[q, c_, P + h:P + h + 1], psKV[q, kv + P:kv + P + 1])
                    ins.then_inc(kv_ready, 1)
                    dve.wait_ge(deg_sd, 2)
                    c.link(dve.reciprocal(norm_dst[:, :], norm_dst[:, :]))
                else:
                    total = dve.value_load(cum[0:1, NG + 3:NG + 4], min_val=0, max_val=NG * NT)
                    dve.wait_ge(drained[l], total)
                    dve.sem_inc(dve_past, 1)
                if l == 1:
                    dve.wait_ge(n_out, NT)

            with dve.Fori(0, NT) as t:
                k = Chain(dve, r_u, t * 5)
                k.link(dve.scalar_tensor_tensor(out=tmp[:, :], in0=agg[:, bass.ds(t, 1), 0:D], scalar=norm_dst[:, bass.ds(t, 1)],
                                                in1=gb2, op0=ALU.mult, op1=ALU.add))
                k.link(dve.tensor_tensor(nodes[:, bass.ds(t, 1), :], nodes[:, bass.ds(t, 1), :], tmp[:, :].unsqueeze(1), ALU.add), dve_past)
                k.link(dve.bn_stats(st6[:, :], nodes[:, bass.ds(t, 1), :]), dve_past)
                k.link(dve.bn_aggr(mv1[:, :], st6[:, :]))
                k.link(copy(mv[:, bass.ds(t, 1), :], mv1[:, :].unsqueeze(1)), dve_past)
            dve.sem_inc(mv_ready, 1)
            dve.wait_ge(sd_ready, 2)
            c.link(dve.reciprocal(rstd[:, :], rstd[:, :]))

            def u_tile(t, s, before_):
                dve.wait_ge(hsT_ready, 3 * NT + t + 1)
                k = Chain(dve, r_vo, 3 * NT + t * 3)
                dve.tensor_scalar(hs[:, s, :], nodes[:, bass.ds(t, 1), :], mv[:, bass.ds(t, 1), 0:1], rstd[:, bass.ds(t, 1)],
                                  ALU.subtract, ALU.mult).then_inc(hs_ready, 1)
                dve.wait_ge(hs_ready, 3 * NT + t + 1)
                copy(agg[:, bass.ds(t, 1), 0:D], hs[:, s, :].unsqueeze(1)).then_inc(u_kept, 1)
                k.link(dve.bn_stats(st6[:, :], hs[:, s, :]), dve_past)
                k.link(dve.bn_aggr(mv1[:, :], st6[:, :]))
                k.link(copy(mv[:, bass.ds(t, 1), :], mv1[:, :].unsqueeze(1)), dve_past)
            by_two(dve, u_tile)
            dve.wait_ge(u_kept, NT)
            dve.sem_inc(mv_ready, 1)

            def te(v):
                return v.rearrange("p (t e) -> p t e", e=NX)

            def over_e(v):
                return v.unsqueeze(2).broadcast_to([P, NT, NX])

            m1, p1, m2, p2, d12, inv, f1, f2 = (small[:, i, :] for i in range(8))
            desc = desc8[:, :].unsqueeze(1).broadcast_to([P, NT, NX])
            dve.wait_ge(row_ready, 4 * NT + RING)
            c.link(dve.tensor_tensor(te(logits), te(psH[:, 0:NE]), br_row[:, :].unsqueeze(1).broadcast_to([P, NT, NX]), ALU.add))

            def first_max(v, m, p_, oh):
                c.link(dve.tensor_reduce(m, te(v), AX_X, ALU.max))
                c.link(dve.tensor_tensor(te(s_a), te(v), over_e(m), ALU.is_equal))
                c.link(dve.tensor_tensor(te(s_a), te(s_a), desc, ALU.mult))
                c.link(dve.tensor_reduce(p_, te(s_a), AX_X, ALU.max))
                c.link(dve.tensor_tensor(te(oh), desc, over_e(p_), ALU.is_equal))

            first_max(logits, m1, p1, oh1)
            c.link(dve.scalar_tensor_tensor(out=s_b, in0=oh1, scalar=-3.0e38, in1=logits, op0=ALU.mult, op1=ALU.add))
            first_max(s_b, m2, p2, oh2)
            c.link(dve.tensor_tensor(gate1[:, :], m2, m1, ALU.subtract))
            dve.sem_inc(fm, 1)
            for oh in (oh1, oh2):
                c.link(dve.tensor_tensor(te(oh), te(oh), over_e(valid[:, :]), ALU.mult))
            c.link(dve.tensor_tensor(pick, oh1, oh2, ALU.add))
            dve.sem_inc(mask_ready, 1)
            dve.wait_ge(fe, 1)
            c.link(dve.tensor_scalar(d12, gate2[:, :], 1.0, None, ALU.add))
            c.link(dve.reciprocal(gate1[:, :], d12))
            c.link(dve.tensor_tensor(gate2[:, :], gate2[:, :], gate1[:, :], ALU.mult))
            dve.wait_ge(rank_mm, 1)
            c.link(dve.tensor_copy(tot, psB[:, 0:NE]))
            for e in range(NX):
                c.link(dve.tensor_tensor_scan(incl.rearrange("p (t e) -> p e t", e=NX)[:, e, :], ones[:, 0:NT],
                                              tot.rearrange("p (t e) -> p e t", e=NX)[:, e, :], 0.0, ALU.mult, ALU.add))
            c.link(dve.tensor_tensor(start_r, incl, tot, ALU.subtract))
            c.link(dve.tensor_tensor(start_r, start_r, psA[:, 0:NE], ALU.add))
            c.link(dve.tensor_scalar(cnt8i[:, 0:NX], te(incl)[:, NT - 1, :], float(BT - 1), None, ALU.add))
            c.link(dve.tensor_scalar(cnt8i[:, 0:NX], cnt8i[:, 0:NX], 8, None, ALU.arith_shift_right))
            c.link(dve.tensor_scalar(cnt8[:, 0, 0:NX], cnt8i[:, 0:NX], 1.0, None, ALU.max))
            c.link(dve.tensor_tensor_scan(cnt8[:, 1, 0:NX], ones[:, 0:NX], cnt8[:, 0, 0:NX], 0.0, ALU.mult, ALU.add))
            c.link(dve.tensor_tensor(cnt8[:, 2, 0:NX], cnt8[:, 1, 0:NX], cnt8[:, 0, 0:NX], ALU.subtract))
            c.link(dve.memset(blk_no[:, 0:1], 0))
            c.link(dve.tensor_copy(blk_no[:, 1:NX + 1], cnt8[:, 1, 0:NX]))
            c.link(dve.tensor_scalar(cnt8[:, 2, 0:NX], cnt8[:, 2, 0:NX], float(BT), None, ALU.mult))
            c.link(dve.tensor_tensor(te(start_r), te(start_r), cnt8[:, 2, 0:NX].unsqueeze(1).broadcast_to([P, NT, NX]), ALU.add))
            c.link(dve.tensor_scalar(inv, valid[:, :], -float(P), float(P), ALU.mult, ALU.add))
            for oh, f, slot, take in ((oh1, f1, slot1, take1), (oh2, f2, slot2, take2)):
                c.link(dve.tensor_tensor(s_a, oh, start_r, ALU.mult))
                c.link(dve.tensor_reduce(f, te(s_a), AX_X, ALU.add))
                c.link(dve.tensor_copy(take[:, :], f))
                if oh is oh2:
                    c.link(dve.tensor_tensor(f, f, inv, ALU.add))
                c.link(dve.tensor_tensor(slot[:, :], f, dump[:, :], ALU.add))
            dve.sem_inc(slots_ready, 1)

            dve.wait_ge(sd_ready, 3)
            c.link(dve.reciprocal(rstd[:, :], rstd[:, :]))

            def spread(t, s, before_):
                dve.wait_ge(scat[s], 32 * before_)
                copy(sidx[:, s, 0:1], slot1[:, bass.ds(t, 1)])
                copy(sidx[:, s, 1:2], slot2[:, bass.ds(t, 1)])
                dve.tensor_scalar(st[:, s, :], agg[:, bass.ds(t, 1), 0:D], mv[:, bass.ds(t, 1), 0:1], rstd[:, bass.ds(t, 1)],
                                  ALU.subtract, ALU.mult).then_inc(r_xs, 1)
            by_two(dve, spread)

            with dve.Fori(0, NX) as e:
                lo = dve.value_load(blk_no[0:1, bass.ds(e, 1)], min_val=0, max_val=NBLK)
                hi = dve.value_load(blk_no[0:1, bass.ds(e + 1, 1)], min_val=0, max_val=NBLK)
                with dve.Fori(lo, hi) as b:
                    dve.wait_ge(b_T, b + 1)
                    dve.wait_ge(b_y, b)
                    for c_ in range(HALVES):
                        ins = dve.tensor_scalar(xeT[:, c_, :], bank[1][:, c_ * BT:(c_ + 1) * BT], fgcol[:, bass.ds(e, 1), c_:c_ + 1],
                                                fbcol[:, bass.ds(e, 1), c_:c_ + 1], ALU.mult, ALU.add)
                    ins.then_inc(b_xT, 1)
                    dve.wait_ge(b_y, b + 1)
                    dve.wait_ge(b_out, b * 16)
                    for a in range(2):
                        ins = dve.tensor_copy(ys[:, a, :], bank[2 + a][:, 0:D])
                    ins.then_inc(b_yc, 1)

            def combine(t, s, before_):
                dve.wait_ge(f_idx, t)
                if not isinstance(before_, int) or before_:
                    pass
                dve.wait_ge(f_got[s], 32 * (before_ + 1))
                dve.wait_ge(f_out[s], 16 * before_)
                k = Chain(dve, f_vo, 2 * NT + t)
                dve.wait_ge(f_ready, t)
                k.link(dve.scalar_tensor_tensor(out=tmp[:, :], in0=hs[:, s, :], scalar=gate1[:, bass.ds(t, 1)],
                                                in1=nodes[:, bass.ds(t, 1), :], op0=ALU.mult, op1=ALU.add))
                dve.scalar_tensor_tensor(out=st[:, s, :], in0=hT[:, s, :], scalar=gate2[:, bass.ds(t, 1)],
                                         in1=tmp[:, :], op0=ALU.mult, op1=ALU.add).then_inc(f_ready, 1)

            def ask(t, s, before_):
                copy(sidx[:, s, 0:1], take1[:, bass.ds(t, 1)])
                copy(sidx[:, s, 1:2], take2[:, bass.ds(t, 1)]).then_inc(f_idx, 1)

            ask(0, 0, 0)
            with dve.Fori(0, NT // 2) as i:
                ask(2 * i + 1, 1, i)
                combine(2 * i, 0, i)
                ask(2 * i + 2, 0, i)
                combine(2 * i + 1, 1, i)
            combine(NT - 1, 0, NT // 2)


_GNN = ("L0_gnn_W", "L0_gnn_b")
_INS = ["x", "src", "dst", "L0_gnn_W0", "L0_gnn_b0", "L0_gnn_W1", "L0_gnn_b1", "L0_gnn_W2", "L0_gnn_b2", "L0_mix_Wqkv",
        "L0_mix_ln1_g", "L0_mix_ln1_b", "L0_mix_W1", "L0_mix_b1", "L0_mix_W2", "L0_mix_b2", "L0_mix_ln2_g", "L0_mix_ln2_b",
        "L0_ffn_Wr", "L0_ffn_br", "L0_ffn_ln_g", "L0_ffn_ln_b", "L0_ffn_W1", "L0_ffn_b1", "L0_ffn_W2", "L0_ffn_b2"]


def kernel(**inputs):
    import concourse.bacc as _bacc
    from concourse.bass_utils import run_bass_kernel_spmd as _run

    nc = _bacc.Bacc("TRN2", target_bir_lowering=False, num_devices=1)
    arrays, a = {}, {}
    for name in _INS:
        v = np.ascontiguousarray(inputs[name])
        arrays[f"in_{name}_dram"] = v
        a[name] = nc.dram_tensor(f"in_{name}_dram", v.shape, mybir.dt.from_np(v.dtype), kind="ExternalInput").ap()
    out = nc.dram_tensor("out_0_dram", arrays["in_x_dram"].shape, F32, kind="ExternalOutput").ap()
    gps_layer(nc, a["x"], a["src"], a["dst"], [a[f"L0_gnn_W{l}"] for l in range(3)], [a[f"L0_gnn_b{l}"] for l in range(3)],
              a["L0_mix_Wqkv"], a["L0_mix_ln1_g"], a["L0_mix_ln1_b"], a["L0_mix_W1"], a["L0_mix_b1"], a["L0_mix_W2"],
              a["L0_mix_b2"], a["L0_mix_ln2_g"], a["L0_mix_ln2_b"], a["L0_ffn_Wr"], a["L0_ffn_br"], a["L0_ffn_ln_g"],
              a["L0_ffn_ln_b"], a["L0_ffn_W1"], a["L0_ffn_b1"], a["L0_ffn_W2"], a["L0_ffn_b2"], out)
    r = _run(nc, [arrays], core_ids=[0])
    return r.results[0]["out_0_dram"]
```

```python
from contextlib import ExitStack

import numpy as np

import concourse.bass as bass
from concourse import mybir

ALU = mybir.AluOpType
ACT = mybir.ActivationFunctionType
AX_X = mybir.AxisListType.X
F32 = mybir.dt.float32
F16 = mybir.dt.float16
I32 = mybir.dt.int32
U32 = mybir.dt.uint32

P = 128
LN_EPS = 1e-5
ATTN_EPS = 1e-6
RING = 2


class Chain:

    def __init__(self, eng, sem, start=0):
        self.eng, self.sem, self.start, self.n = eng, sem, start, 0

    def link(self, ins, alone=None):
        self.n += 1
        ins.then_inc(self.sem, 1)
        self.eng.wait_ge(self.sem, self.start + self.n)
        if alone is not None:
            self.eng.sem_inc(alone, 1)


def gps_layer(nc, x, src, dst, gnn_W, gnn_b, Wqkv, ln1_g, ln1_b, mix_W1, mix_b1, mix_W2, mix_b2,
              ln2_g, ln2_b, Wr, br, ffn_g, ffn_b, ffn_W1, ffn_b1, ffn_W2, ffn_b2, out):
    N, D = x.shape
    E = src.shape[0]
    HALVES = D // P
    NT = -(-N // P)
    LAST = N - (NT - 1) * P
    NX = ffn_W1.shape[0]
    HID = ffn_W1.shape[2]
    MH = HID // P
    HEADS = 8
    HD = D // HEADS
    HPB = P // HD

    CB = -(-E // (P * P))
    FULLB = E // (P * P)
    TAILCH = (E - FULLB * P * P) // P
    TAILE = E - FULLB * P * P - TAILCH * P

    SC = 2
    SE = SC * P
    NS = -(-E // SE)
    SB = -(-NS // P)
    FULLS = E // SE
    DW = 16
    WPT = P // DW
    NW = NT * WPT
    HW_ = DW // 2 * NT
    WS = 4
    WSP = NW // WS
    assert WS * WSP == NW and WSP <= P and HW_ <= 512 and NT % 2 == 1

    BT = 256
    NBLK = (2 * N) // BT + NX
    SLOTS = NBLK * BT
    LEAST = -(-2 * N // BT)
    NE = NT * NX

    adj = nc.dram_tensor("adj", (NT, P, NT * P), F16, kind="Internal").ap()
    bounds_d = nc.dram_tensor("bounds", (2, NW), I32, kind="Internal").ap()
    routed_in = nc.dram_tensor("routed_in", (SLOTS + 2 * P, D), F32, kind="Internal").ap()
    routed_out = nc.dram_tensor("routed_out", (SLOTS, D), F32, kind="Internal").ap()

    with ExitStack() as ctx:
        def sb(name, shape, dt=F32):
            return ctx.enter_context(nc.sbuf_tensor(name, shape, dt))

        def sem(name):
            return ctx.enter_context(nc.semaphore(name))

        nodes = sb("nodes", [P, NT, D])
        prod = sb("prod", [P, NT, D])
        xbuf = sb("xbuf", [P, (NT * (2 * D + 2) + 2) // 2])
        x16 = xbuf[:, :].bitcast(F16)
        x_hi = x16[:, 0:NT * (D + 2)].rearrange("p (t d) -> p t d", t=NT)[:, :, 0:D + 1]
        x_lo = x16[:, NT * (D + 2):NT * (2 * D + 2)].rearrange("p (t d) -> p t d", t=NT)
        abuf = sb("abuf", [P, NT * P])
        a16 = abuf[:, :].bitcast(F16).rearrange("p (s h d) -> p s h d", s=RING, h=NT)
        wqkvT = sb("wqkvT", [P, HALVES, 3 * D])
        wg = sb("wg", [P, RING, HALVES, D])
        wr = sb("wr", [P, HALVES, NX])
        rows = sb("rows", [P, 3, D])
        gb = [rows[:, i, :] for i in range(3)]
        br_row = sb("br_row", [P, NX])
        b1col = sb("b1col", [P, HALVES])
        fgcol = sb("fgcol", [P, NX, HALVES])
        fbcol = sb("fbcol", [P, NX, HALVES])
        fb1col = sb("fb1col", [P, NX, MH])
        desc8 = sb("desc8", [P, NX])
        fb2row = sb("fb2row", [1, RING, D])
        ident = sb("ident", [P, P])
        before = sb("before", [P, P])
        ones = sb("ones", [P, P])
        zeros = sb("zeros", [P, D + 8])
        eps_ln = sb("eps_ln", [P, 1])
        cum = sb("cum", [1, NW + 1], I32)
        shift = sb("shift", [1, NW], I32)
        mm = sb("mm", [P, 2, SB], I32)
        mmf = sb("mmf", [P, 2, SB])
        span_no = sb("span_no", [P, 2, SB])
        wl = sb("wl", [P, 2, WS])
        wi = sb("wi", [P, 2, WS], I32)
        ymax = sb("ymax", [P, 2, NT])
        col = sb("col", [P, 8])
        nss = sb("nss", [P, NT])
        norm_src = sb("norm_src", [P, NT])
        norm_dst = sb("norm_dst", [P, NT])
        deg = sb("deg", [P, NT])
        mv = sb("mv", [P, NT, 2])
        st6 = sb("st6", [P, 6])
        rstd = sb("rstd", [P, NT])
        hrow = sb("hrow", [P, D])
        hrowT = sb("hrowT", [P, D])
        tmp = sb("tmp", [P, D])
        mix4 = sb("mix4", [P, 4, D])
        mrow, mT, melu, mexp = (mix4[:, i, :] for i in range(4))
        mfeat = sb("mfeat", [P, D])
        vaug = sb("vaug", [P, HALVES, P + 1])
        kvblk = sb("kvblk", [P, HALVES, P + HPB])
        z = sb("z", [P, HALVES, HPB])
        mv1 = sb("mv1", [P, 2])
        sd1 = sb("sd1", [P, 1])

        W_ = CB * P
        key, sl, src_t, hi_f = (xbuf[:, i * W_:(i + 1) * W_] for i in range(4))
        dst_i, src_i, dst_f, src_f = key.bitcast(I32), src_t.bitcast(I32), sl, hi_f
        src_t = src_t.bitcast(I32)
        o_ = 2 * W_
        deg_acc = xbuf[:, o_:o_ + NT * P]
        o_ += NT * P
        onehot_w = xbuf[:, o_:o_ + HW_ * SC].bitcast(F16).rearrange("p (j n) -> p j n", j=SC)
        o_ += HW_ * SC
        onehot_lo = xbuf[:, o_:o_ + SC * P // 2].bitcast(F16).rearrange("p (j n) -> p j n", j=SC)
        o_ += SC * P // 2
        iota_w = xbuf[:, o_:o_ + HW_].bitcast(F16)
        o_ += HW_
        w_base = xbuf[:, o_:o_ + NW]
        iota_lo = mix4[:, 0, 0:P // 2].bitcast(F16)
        pf = prod[:, :, :].rearrange("p a b -> p (a b)")
        span_rows = pf[:, 0:SB * SE].bitcast(I32).rearrange("p (j e) -> p j e", j=SB)
        o_ = SB * SE
        raw_qkv = pf[:, o_:o_ + 6 * D].rearrange("p (o c) -> p o c", o=6)
        o_ += 6 * D
        far = pf[:, o_:o_ + 2 * NW].rearrange("p (k n) -> p k n", k=2)
        mask = pf[:, o_ + 2 * NW:o_ + 3 * NW]
        w_no = pf[:, o_ + 3 * NW:o_ + 4 * NW]
        cnt_f = pf[0:1, o_ + 4 * NW:o_ + 8 * NW].rearrange("p (k n) -> p k n", k=4)
        def piece(i, n=1):
            return pf[:, i * D:(i + n) * D]
        w1T, w2T, raw_w1, raw_w2 = (piece(2 * i, 2).rearrange("p (c n) -> p c n", c=2) for i in range(4))
        r1g, r1b, r2g, r2b, rb2, x1, xo = (piece(8 + i) for i in range(7))
        turned = [(raw_qkv, wqkvT, c, o, n) for c in range(HALVES) for o, n in ((0, 4), (4, 2))]
        turned2 = [(raw, to, c, 0, 2) for raw, to in ((raw_w1, w1T), (raw_w2, w2T)) for c in range(HALVES)]

        flat = xbuf[:, :]
        def cut(i):
            return flat[:, i * 400:i * 400 + NE]
        logits, s_a, s_b, oh1, oh2, pick, incl, tot, start_r, ex = (cut(i) for i in range(10))
        small = flat[:, 4000:4000 + 20 * NT].rearrange("p (a b) -> p a b", b=NT)
        w_up = [flat[:, s * 4096:s * 4096 + HALVES * HID].rearrange("p (c n) -> p c n", c=HALVES) for s in range(2)]
        w_dn = [flat[:, s * 4096 + HALVES * HID:(s + 1) * 4096].rearrange("p (m n) -> p m n", m=MH) for s in range(2)]
        gate1 = sb("gate1", [P, NT])
        gate2 = sb("gate2", [P, NT])
        slot1 = sb("slot1", [P, NT], I32)
        slot2 = sb("slot2", [P, NT], I32)
        take1 = sb("take1", [P, NT], I32)
        take2 = sb("take2", [P, NT], I32)
        valid = sb("valid", [P, NT])
        dump = sb("dump", [P, NT])
        sidx = sb("sidx", [P, RING, 2], I32)
        blk_no = sb("blk_no", [P, 16], I32)
        cnt8 = sb("cnt8", [P, 4, 16])
        cnt8i = sb("cnt8i", [P, 16], I32)
        xs = abuf[:, 0:2 * D].rearrange("p (a n) -> p a n", a=2)
        xeT = abuf[:, 2 * D:4 * D].rearrange("p (a n) -> p a n", a=2)
        ys = abuf[:, 4 * D:6 * D].rearrange("p (a n) -> p a n", a=2)
        hidT = abuf[:, 6 * D:6 * D + MH * BT].rearrange("p (m n) -> p m n", m=MH)
        hs, hT, st = (abuf[:, 3584 + i * 2 * D:3584 + (i + 1) * 2 * D].rearrange("p (s n) -> p s n", s=RING) for i in range(3))

        bank = [ctx.enter_context(nc.psum_tensor(f"bank{i}", [P, 512], F32)) for i in range(8)]
        acc = [bank[0], bank[7]]
        windows = [(bank[0], bank[3]), (bank[6], bank[7])]
        psT = [bank[1], bank[4]]
        psO = [bank[2], bank[5]]
        psKV = bank[3][:, 0:HALVES * (P + 1)]
        psA = bank[4]
        psB = bank[5]
        psC = bank[6]
        psH = bank[7]

        c_iota = sem("c_iota"); c_mat = sem("c_mat"); c_vec = sem("c_vec")
        vo = sem("vo"); po = sem("po")
        dve_past = sem("dve_past"); pe_past = sem("pe_past"); pool_past = sem("pool_past")
        act_past = sem("act_past")
        raw_clear = sem("raw_clear"); dst_in = sem("dst_in"); src_in = sem("src_in")
        sp_clear = sem("sp_clear"); sp_in = sem("sp_in"); far_ready = sem("far_ready"); farT = sem("farT")
        wi_ready = sem("wi_ready")
        bounds_out = sem("bounds_out"); bounds_in = sem("bounds_in"); cum_ready = sem("cum_ready")
        edges_f = sem("edges_f"); edgesT = sem("edgesT"); edges_c = sem("edges_c"); key_ready = sem("key_ready")
        w_in = sem("w_in"); wraw_in = sem("wraw_in"); wT = sem("wT"); wT_out = sem("wT_out")
        wg_in = sem("wg_in"); w2_in = sem("w2_in"); w2raw_in = sem("w2raw_in")
        wmT = sem("wmT"); wmT_out = sem("wmT_out")
        x_in = sem("x_in"); mv_ready = sem("mv_ready"); sd_ready = sem("sd_ready"); xn_ready = sem("xn_ready")
        oh_ready = [sem(f"oh_ready{j}") for j in range(SC)]
        oh_free = [sem(f"oh_free{j}") for j in range(SC)]
        win_ready = [sem(f"win_ready{s}") for s in range(RING)]
        win_free = [sem(f"win_free{s}") for s in range(RING)]
        a_ready = sem("a_ready"); a_out = [sem(f"a_out{s}") for s in range(RING)]; deg_added = sem("deg_added")
        h_ready = sem("h_ready"); h_T = sem("h_T"); h_Tc = sem("h_Tc"); h_p = sem("h_p"); prod_ready = sem("prod_ready")
        max_done = sem("max_done")
        a_in = [sem(f"a_in{s}") for s in range(RING)]
        acc_done = sem("acc_done"); acc_used = sem("acc_used")
        g_T = sem("g_T"); g_row = sem("g_row"); g_col = sem("g_col"); nss_ready = sem("nss_ready")
        hi_ready = sem("hi_ready"); lo_ready = sem("lo_ready"); p_vo = sem("p_vo")
        r_hs = sem("r_hs"); r_hsT = sem("r_hsT"); r_hT = sem("r_hT"); r_row = sem("r_row")
        m_row = sem("m_row"); m_T = sem("m_T"); m_xT = sem("m_xT"); m_P = sem("m_P"); m_min = sem("m_min")
        m_exp = sem("m_exp"); m_v = sem("m_v"); m_f = sem("m_f"); m_KV = sem("m_KV"); kv_ready = sem("kv_ready")
        n_t = sem("n_t"); n_mv = sem("n_mv"); n_sd = sem("n_sd"); n_x1 = sem("n_x1"); n_T = sem("n_T")
        n_x1T = sem("n_x1T"); n_h = sem("n_h"); n_g = sem("n_g"); n_y = sem("n_y")
        n_out = sem("n_out"); xo_in = sem("xo_in"); n_vo = sem("n_vo")
        deg_ready = sem("deg_ready"); deg_sd = sem("deg_sd"); nd_ready = sem("nd_ready")
        zero_out = sem("zero_out"); degs = sem("degs")
        r_u = sem("r_u"); u_kept = sem("u_kept"); r_vo = sem("r_vo"); r_T = sem("r_T"); r_uT = sem("r_uT"); r_l = sem("r_l"); r_lc = sem("r_lc")
        r_xs = sem("r_xs"); scat = [sem(f"scat{s}") for s in range(RING)]
        fm = sem("fm"); fe = sem("fe"); rank_mm = sem("rank_mm"); mask_ready = sem("mask_ready")
        slots_ready = sem("slots_ready"); pool_c = sem("pool_c")
        wx_in = [sem(f"wx_in{s}") for s in range(RING)]
        xs_in = sem("xs_in"); b_T = sem("b_T"); b_xT = sem("b_xT"); b_up = sem("b_up"); b_h = sem("b_h")
        b_y = sem("b_y"); b_yc = sem("b_yc"); b_out = sem("b_out")
        f_idx = sem("f_idx"); f_got = [sem(f"f_got{s}") for s in range(RING)]; f_vo = sem("f_vo")
        f_ready = sem("f_ready"); f_out = [sem(f"f_out{s}") for s in range(RING)]

        block = ctx.enter_context(nc.Block())

        def by_two(eng, body):
            with eng.Fori(0, NT // 2) as i:
                body(2 * i, 0, i)
                body(2 * i + 1, 1, i)
            body(NT - 1, 0, NT // 2)

        USES = [NT // 2 + 1, NT // 2]

        @block.sync
        def _(sp):
            for s in range(RING):
                sp.sem_inc(a_out[s], 16)
            sp.wait_ge(raw_clear, 2)
            for e_dram, e_sb, s in ((dst, dst_i, dst_in), (src, src_i, src_in)):
                v = e_sb.rearrange("p (g e) -> p g e", e=P)
                full = FULLB * P * P
                sp.dma_start(v[:, 0:FULLB, :], e_dram[0:full].rearrange("(g q e) -> q g e", q=P, e=P)).then_inc(s, 16)
                sp.dma_start(v[0:TAILCH, FULLB, :],
                             e_dram[full:full + TAILCH * P].rearrange("(q e) -> q e", e=P)).then_inc(s, 16)
                sp.dma_start(v[TAILCH:TAILCH + 1, FULLB, 0:TAILE],
                             e_dram[full + TAILCH * P:E].rearrange("(q e) -> q e", q=1)).then_inc(s, 16)
            sp.wait_ge(sp_clear, 1)
            whole = FULLS // P
            sp.dma_start(span_rows[:, 0:whole, :], dst[0:whole * P * SE].rearrange("(j q e) -> q j e", q=P, e=SE)).then_inc(sp_in, 16)
            rest = FULLS - whole * P
            sp.dma_start(span_rows[0:rest, whole, :], dst[whole * P * SE:FULLS * SE].rearrange("(q e) -> q e", e=SE)).then_inc(sp_in, 16)
            sp.dma_start(span_rows[rest:rest + 1, whole, :], dst[E - SE:E].rearrange("(q e) -> q e", q=1)).then_inc(sp_in, 16)
            sp.wait_ge(c_vec, 1)
            sp.dma_start(nodes[:, 0:NT - 1, :], x[0:(NT - 1) * P, :].rearrange("(t p) d -> p t d", p=P)).then_inc(x_in, 16)
            sp.dma_start(nodes[0:LAST, NT - 1, :], x[(NT - 1) * P:N, :]).then_inc(x_in, 16)
            for l in range(2):
                sp.dma_start(wg[:, l, :, :], gnn_W[l].rearrange("(c p) n -> p c n", p=P)).then_inc(w_in, 16)
            sp.dma_start(wr[:, :, :], Wr.rearrange("(c p) n -> p c n", p=P)).then_inc(w_in, 16)
            for l in range(3):
                sp.dma_start(gb[l], gnn_b[l].rearrange("(a n) -> a n", a=1).broadcast_to([P, D])).then_inc(w_in, 16)
            sp.dma_start(br_row[:, :], br.rearrange("(a n) -> a n", a=1).broadcast_to([P, NX])).then_inc(w_in, 16)
            sp.dma_start(b1col[:, :], mix_b1.rearrange("(c p) -> p c", p=P), allow_slow_non_contiguous=True).then_inc(w_in, 16)
            sp.wait_ge(wi_ready, 1)
            for m in range(2):
                sp.dma_start(bounds_d[m:m + 1, :].rearrange("m (s p) -> p m s", p=WSP), wi[0:WSP, m:m + 1, :], allow_slow_non_contiguous=True).then_inc(bounds_out, 16)
            sp.wait_ge(bounds_out, 32)
            sp.dma_start(shift[0:1, :], bounds_d[0:1, :]).then_inc(bounds_in, 16)
            sp.dma_start(cum[0:1, 1:NW + 1], bounds_d[1:2, :]).then_inc(bounds_in, 16)
            for c_sb, c_dram in ((fgcol, ffn_g), (fbcol, ffn_b), (fb1col, ffn_b1)):
                v = c_dram.rearrange("e (c p) -> p e c", p=P)
                for e in range(NX):
                    sp.dma_start(c_sb[:, e, :], v[:, e, :], allow_slow_non_contiguous=True).then_inc(w_in, 16)
            zr = zeros[:, 0:D].unsqueeze(1).broadcast_to([P, NBLK * BT // P, D])
            sp.dma_start(routed_in[0:SLOTS, :].rearrange("(a p) d -> p a d", p=P), zr).then_inc(zero_out, 16)
            zr = zeros[:, 0:D].unsqueeze(1).broadcast_to([P, (NBLK - LEAST) * BT // P, D])
            sp.dma_start(routed_out[LEAST * BT:SLOTS, :].rearrange("(a p) d -> p a d", p=P), zr).then_inc(zero_out, 16)

            def store_adj(t, s, before_):
                sp.wait_ge(a_ready, t + 1)
                sp.dma_start(adj[bass.ds(t, 1), :, :].rearrange("a p n -> p (a n)"), a16[:, s, :, :].rearrange("p h d -> p (h d)")).then_inc(a_out[s], 16)
            by_two(sp, store_adj)
            for s in range(RING):
                sp.wait_ge(a_out[s], 16 * (USES[s] + 1))
            sp.wait_ge(deg_added, NT + RING)

            for l in range(3):
                def load_adj(t, s, before_, first=False):
                    sp.wait_ge(acc_done, l * NT + t + (2 if first else 1))
                    half = NT // 2 * P
                    for lo, hi in ((0, half), (half, NT * P)):
                        sp.dma_start(a16[:, s, :, :].rearrange("p h d -> p (h d)")[:, lo:hi],
                                     adj[bass.ds(t, 1), :, lo:hi].rearrange("a p n -> p (a n)")).then_inc(a_in[s], 16)
                if l == 1:
                    sp.wait_ge(prod_ready, NT + 1)
                    sp.dma_start(wg[:, 0, :, :], gnn_W[2].rearrange("(c p) n -> p c n", p=P)).then_inc(wg_in, 16)
                if l == 2:
                    sp.wait_ge(lo_ready, 3 * NT)
                    sp.wait_ge(hi_ready, 3 * NT)
                    for raw, w_dram in ((raw_w1, mix_W1), (raw_w2, mix_W2)):
                        sp.dma_start(raw, w_dram.rearrange("(o p) c -> p o c", p=P)).then_inc(w2raw_in, 16)
                    for to, v in ((r1g, ln1_g), (r1b, ln1_b), (r2g, ln2_g), (r2b, ln2_b), (rb2, mix_b2)):
                        sp.dma_start(to, v.rearrange("(a n) -> a n", a=1).broadcast_to([P, D])).then_inc(w2_in, 16)

                def again(t, rows_=P):
                    sp.wait_ge(n_out, t)
                    sp.dma_start(xo[0:rows_, :], x[bass.ds(t * P, rows_), :]).then_inc(xo_in, 16)

                def pair_of_tiles(i, rows_=P):
                    load_adj(2 * i + 1, 1, i)
                    if l == 2:
                        again(2 * i + 1)
                    load_adj(2 * i + 2, 0, i + 1)
                    if l == 2:
                        again(2 * i + 2, rows_)
                load_adj(0, 0, 0, True)
                if l == 2:
                    again(0)
                with sp.Fori(0, NT // 2 - 1) as i:
                    pair_of_tiles(i)
                pair_of_tiles(NT // 2 - 1, LAST)

            sp.wait_ge(slots_ready, 1)
            sp.wait_ge(zero_out, 32)
            for s in range(RING):
                sp.wait_ge(scat[s], 32 * USES[s])
            last = sp.value_load(blk_no[0:1, NX:NX + 1], min_val=NX, max_val=NBLK)
            with sp.Fori(0, last) as b:
                sp.wait_ge(b_T, b)
                sp.dma_start(xs, routed_in[bass.ds(b * BT, BT), :].rearrange("(a p) d -> p a d", p=P)).then_inc(xs_in, 16)

            def store(t, s, rows_=P):
                sp.wait_ge(f_ready, t + 1)
                sp.dma_start(out[bass.ds(t * P, rows_), :], st[0:rows_, s, :]).then_inc(f_out[s], 16)
            with sp.Fori(0, NT // 2) as i:
                store(2 * i, 0)
                store(2 * i + 1, 1)
            store(NT - 1, 0, LAST)
            for s in range(RING):
                sp.wait_ge(f_out[s], 16 * USES[s])

        @block.gpsimd
        def _(pool):
            c = Chain(pool, po)
            pool.iota(span_no[:, 0, :], [[P, SB]], base=1, channel_multiplier=1, allow_small_or_imprecise_dtypes=True)
            pool.iota(span_no[:, 1, :], [[-P, SB]], base=NS, channel_multiplier=-1, allow_small_or_imprecise_dtypes=True)
            pool.iota(w_no, [[1, NW]], base=0, channel_multiplier=0, allow_small_or_imprecise_dtypes=True)
            pool.iota(iota_lo, [[1, P]], base=0, channel_multiplier=0, allow_small_or_imprecise_dtypes=True)
            pool.iota(iota_w, [[1, 2 * HW_]], base=0, channel_multiplier=0, allow_small_or_imprecise_dtypes=True)
            pool.iota(w_base, [[2 * HW_, NW]], base=0, channel_multiplier=0, allow_small_or_imprecise_dtypes=True).then_inc(c_iota, 1)
            pool.memset(ident[:, :], 0.0)
            pool.memset(before[:, :], 1.0)
            pool.memset(ones[:, :], 1.0)
            pool.memset(valid[:, :], 1.0)
            c.link(pool.iota(dump[:, :], [[0, NT]], base=SLOTS, channel_multiplier=1, allow_small_or_imprecise_dtypes=True))
            pool.affine_select(out=ident[:, :], in_=ident[:, :], compare_op=ALU.not_equal, fill=1.0, base=0,
                               pattern=[[-1, P]], channel_multiplier=1)
            pool.affine_select(out=before[:, :], in_=before[:, :], compare_op=ALU.is_gt, fill=0.0, base=0,
                               pattern=[[1, P]], channel_multiplier=-1)
            pool.affine_select(out=valid[:, :], in_=valid[:, :], compare_op=ALU.is_ge, fill=0.0, base=N - 1,
                               pattern=[[-P, NT]], channel_multiplier=-1)
            pool.affine_select(out=dump[:, :], in_=dump[:, :], compare_op=ALU.is_ge, fill=0.0, base=-N,
                               pattern=[[P, NT]], channel_multiplier=1)
            pool.iota(desc8[:, :], [[-1, NX]], base=NX, channel_multiplier=0, allow_small_or_imprecise_dtypes=True)
            pool.memset(vaug[:, :, P:P + 1], 1.0).then_inc(c_mat, 1)

            pool.wait_ge(key_ready, 1)
            pool.memset(deg_acc, 0.0).then_inc(deg_added, RING)

            def add(t, s, before_):
                pool.wait_ge(a_ready, t + 1)
                pool.wait_ge(deg_added, t + RING)
                pool.tensor_tensor(deg_acc, deg_acc, a16[:, s, :, :].rearrange("p h d -> p (h d)"), ALU.add).then_inc(deg_added, 1)
            by_two(pool, add)

            pool.wait_ge(slots_ready, 1)
            pool.wait_ge(zero_out, 32)

            def scatter(t, s, before_):
                pool.wait_ge(r_xs, t + 1)
                pool.sem_inc(pool_past, 1)
                for k in range(2):
                    pool.indirect_dma_start(
                        out=routed_in, out_offset=bass.IndirectOffsetOnAxis(ap=sidx[:, s, k:k + 1].bitcast(U32), axis=0),
                        in_=st[:, s, :], in_offset=None).then_inc(scat[s], 16)
            by_two(pool, scatter)

            def weights(e, s):
                if not (isinstance(e, int) and e < RING):
                    pool.wait_ge(b_y, pool.value_load(blk_no[0:1, bass.ds(e - 1, 1)], min_val=0, max_val=NBLK))
                pool.dma_start(w_up[s], ffn_W1[bass.ds(e, 1), :, :].rearrange("e (c p) n -> p (e c) n", p=P)).then_inc(wx_in[s], 16)
                pool.dma_start(w_dn[s], ffn_W2[bass.ds(e, 1), :, :].rearrange("e (m p) n -> p (e m) n", p=P)).then_inc(wx_in[s], 16)
                pool.dma_start(fb2row[0:1, s, :], ffn_b2[bass.ds(e, 1), :]).then_inc(wx_in[s], 16)

            def stores(e):
                lo = pool.value_load(blk_no[0:1, bass.ds(e, 1)], min_val=0, max_val=NBLK)
                hi = pool.value_load(blk_no[0:1, bass.ds(e + 1, 1)], min_val=0, max_val=NBLK)
                with pool.Fori(lo, hi) as b:
                    pool.wait_ge(b_yc, b + 1)
                    pool.dma_start(routed_out[bass.ds(b * BT, BT), :].rearrange("(a p) d -> p a d", p=P), ys).then_inc(b_out, 16)
            weights(0, 0)
            weights(1, 1)
            with pool.Fori(0, NX // 2 - 1) as i:
                stores(2 * i)
                weights(2 * i + 2, 0)
                stores(2 * i + 1)
                weights(2 * i + 3, 1)
            stores(NX - 2)
            stores(NX - 1)

            total = pool.value_load(blk_no[0:1, NX:NX + 1], min_val=NX, max_val=NBLK)
            pool.wait_ge(b_out, total * 16)
            pool.sem_inc(pool_past, 1)

            def fetch(t, s, before_):
                pool.wait_ge(f_idx, t + 1)
                pool.sem_inc(pool_past, 1)
                for k, to in ((0, hs), (1, hT)):
                    pool.indirect_dma_start(
                        out=to[:, s, :], out_offset=None, in_=routed_out,
                        in_offset=bass.IndirectOffsetOnAxis(ap=sidx[:, s, k:k + 1].bitcast(U32), axis=0)
                    ).then_inc(f_got[s], 16)
            by_two(pool, fetch)

        @block.tensor
        def _(pe):
            pe.wait_ge(c_mat, 1)
            pe.wait_ge(c_vec, 1)
            for sem_ in oh_free:
                pe.sem_inc(sem_, 1)
            pe.sem_inc(acc_done, RING)
            pe.sem_inc(r_hsT, RING)
            pe.sem_inc(r_row, RING)
            pe.sem_inc(h_T, 1)
            pe.sem_inc(h_p, 1)
            pe.wait_ge(edges_f, 2)
            n = 0
            for v in (dst_f, src_f):
                for b0 in range(0, CB, 4):
                    if n >= 2:
                        pe.wait_ge(edges_c, n - 1)
                    ps = (psA, psB)[n % 2]
                    for b in range(b0, min(b0 + 4, CB)):
                        mm_ = pe.transpose(ps[:, (b - b0) * P:(b - b0 + 1) * P], v[:, b * P:(b + 1) * P], ident[:, :])
                    mm_.then_inc(edgesT, 1)
                    n += 1
            pe.wait_ge(wraw_in, 16)
            for i, (raw, _, c_, o0, nb) in enumerate(turned):
                pe.wait_ge((edges_c if i < 2 else wT_out), (n - 1 + i if i < 2 else i - 1))
                for o in range(nb):
                    mm_ = pe.transpose((psA, psB)[i % 2][:, o * P:(o + 1) * P], raw[:, o0 + o, c_ * P:(c_ + 1) * P], ident[:, :])
                mm_.then_inc(wT, 1)
            pe.wait_ge(far_ready, 1)
            for k in range(2):
                for s in range(WS):
                    mm_ = pe.transpose((psC, psH)[k][0:WSP, s * P:(s + 1) * P], far[:, k, s * WSP:(s + 1) * WSP], ident[:, :])
            mm_.then_inc(farT, 1)
            pe.wait_ge(cum_ready, 1)
            pe.wait_ge(wT_out, len(turned))
            zb = zeros[:, :].bitcast(F16)

            def turn(n):
                pe.wait_ge(h_ready, n + 1)
                pe.wait_ge(h_Tc, n + 1)
                for c_ in range(HALVES):
                    mm_ = pe.transpose(psT[0][:, c_ * P:(c_ + 1) * P], hrow[:, c_ * P:(c_ + 1) * P], ident[:, :])
                mm_.then_inc(h_T, 1)

            def project(l, n):
                pe.wait_ge(h_Tc, n + 2)
                pe.wait_ge(prod_ready, n + 1)
                for c_ in range(HALVES):
                    mm_ = pe.matmul(psO[0][:, 0:D], hrowT[:, c_ * P:(c_ + 1) * P], wg[:, l % 2, c_, :], start=(c_ == 0), stop=(c_ == HALVES - 1))
                mm_.then_inc(h_p, 1)

            pe.wait_ge(w_in, 16 * (3 + 3 + 2 + 3 * NX))

            def build(t, s, before_):
                lo = pe.value_load(cum[0:1, bass.ds(t * WPT, 1)], min_val=0, max_val=NW * NS)
                for i in range(WPT):
                    if i == 1:
                        turn(t)
                    if i == 4:
                        project(0, t)
                    hi = pe.value_load(cum[0:1, bass.ds(t * WPT + i + 1, 1)], min_val=0, max_val=NW * NS)
                    pe.wait_ge(win_free[i % 2], t * (WPT // 2) + i // 2 + 1)
                    for half in windows[i % 2]:
                        pe.matmul(half[:, 0:HW_], zb[:, 0:P], zb[:, 0:HW_], start=True, stop=False)
                    with pe.Fori(lo, hi) as p:
                        for j in range(SC):
                            pe.wait_ge(oh_ready[j], p + 1)
                            for h, half in enumerate(windows[i % 2]):
                                mm_ = pe.matmul(half[:, 0:HW_], onehot_lo[:, j, :], onehot_w[:, j, h * HW_:(h + 1) * HW_], start=False, stop=False)
                            mm_.then_inc(oh_free[j], 1)
                    for half in windows[i % 2]:
                        mm_ = pe.matmul(half[:, 0:HW_], zb[:, 0:P], zb[:, 0:HW_], start=False, stop=True)
                    mm_.then_inc(win_ready[i % 2], 1)
                    lo = hi
            by_two(pe, build)

            def kv_step(t, g, rows_=P):
                if g == 0:
                    pe.wait_ge(m_row, t + 1)
                    pe.wait_ge(m_xT, t)
                    for c_ in range(HALVES):
                        mm_ = pe.transpose(psA[:, c_ * P:(c_ + 1) * P], mrow[:, c_ * P:(c_ + 1) * P], ident[:, :])
                    mm_.then_inc(m_T, 1)
                if g == 1:
                    pe.wait_ge(m_xT, t + 1)
                    pe.wait_ge(m_f, t)
                    pe.wait_ge(m_v, t)
                    for ps, o in ((psB, D), (psC, 2 * D)):
                        for c_ in range(HALVES):
                            mm_ = pe.matmul(ps[:, 0:D], mT[:, c_ * P:(c_ + 1) * P], wqkvT[:, c_, o:o + D], start=(c_ == 0), stop=(c_ == HALVES - 1))
                    mm_.then_inc(m_P, 1)
                if g == 3:
                    pe.wait_ge(m_f, t + 1)
                    pe.wait_ge(m_v, t + 1)
                    for c_ in range(HALVES):
                        mm_ = pe.matmul(psKV[:, c_ * (P + 1):(c_ + 1) * (P + 1)], mfeat[0:rows_, c_ * P:(c_ + 1) * P],
                                        vaug[0:rows_, c_, :], start=False, stop=False)
                    mm_.then_inc(m_KV, 1)

            def mix_step(t, g):
                if g == 0:
                    pe.wait_ge(m_row, NT + t + 1)
                    pe.wait_ge(n_x1T, t)
                    for c_ in range(HALVES):
                        mm_ = pe.transpose(psA[:, c_ * P:(c_ + 1) * P], mrow[:, c_ * P:(c_ + 1) * P], ident[:, :])
                    mm_.then_inc(m_T, 1)
                    pe.wait_ge(m_xT, NT + t + 1)
                    pe.wait_ge(n_g, 2 * t)
                    for o in range(HALVES):
                        for c_ in range(HALVES):
                            mm_ = pe.matmul(psB[:, o * P:(o + 1) * P], wqkvT[:, c_, o * P:(o + 1) * P],
                                            mT[:, c_ * P:(c_ + 1) * P], start=(c_ == 0), stop=(c_ == HALVES - 1))
                    mm_.then_inc(m_P, 1)
                if g == 1:
                    pe.wait_ge(m_f, NT + t + 1)
                    pe.wait_ge(n_out, t)
                    for o in range(HALVES):
                        mm_ = pe.matmul(psC[:, o * (P + HPB):(o + 1) * (P + HPB)], mfeat[:, o * P:(o + 1) * P], kvblk[:, o, :], start=True, stop=True)
                    mm_.then_inc(n_t, 1)
                if g == 2:
                    pe.wait_ge(n_x1, t + 1)
                    for c_ in range(HALVES):
                        mm_ = pe.transpose(psA[:, c_ * P:(c_ + 1) * P], x1[:, c_ * P:(c_ + 1) * P], ident[:, :])
                    mm_.then_inc(n_T, 1)
                    pe.wait_ge(n_x1T, t + 1)
                    for o in range(HALVES):
                        for c_ in range(HALVES):
                            mm_ = pe.matmul(psB[:, o * P:(o + 1) * P], w1T[:, c_, o * P:(o + 1) * P],
                                            mT[:, c_ * P:(c_ + 1) * P], start=(c_ == 0), stop=(c_ == HALVES - 1))
                    mm_.then_inc(n_h, 1)
                if g == 3:
                    pe.wait_ge(n_g, 2 * t + 2)
                    for c_ in range(HALVES):
                        mm_ = pe.matmul(psC[:, 0:D], mfeat[:, c_ * P:(c_ + 1) * P], w2T[:, c_, :], start=(c_ == 0), stop=(c_ == HALVES - 1))
                    mm_.then_inc(n_y, 1)

            FIRST = "first"
            for l in range(3):
                pe.wait_ge(g_row, 2 * l + 1)
                pe.transpose(psT[0][0:1, 0:P], col[:, 0:1], ident[:, :]).then_inc(g_T, 1)
                pe.wait_ge(g_row, 2 * l + 2)
                pe.matmul(psT[0][:, 0:1], ones[0:1, :], col[0:1, 1:2], start=True, stop=True).then_inc(g_T, 1)
                if l == 0:
                    pe.matmul(psKV, zeros[:, 0:P], zeros[:, 0:HALVES * (P + 1)], start=True, stop=False)
                if l == 1:
                    pe.wait_ge(wg_in, 16)
                if l == 2:
                    pe.wait_ge(w2raw_in, 32)
                    for sem_ in (m_xT, m_f, m_v):
                        pe.wait_ge(sem_, NT)
                    for i, (raw, _, c_, o0, nb) in enumerate(turned2):
                        if i >= 2:
                            pe.wait_ge(wmT_out, i - 1)
                        for o in range(nb):
                            mm_ = pe.transpose((psA, psB)[i % 2][:, o * P:(o + 1) * P], raw[:, o0 + o, c_ * P:(c_ + 1) * P], ident[:, :])
                        mm_.then_inc(wmT, 1)
                    pe.wait_ge(wmT_out, len(turned2))

                def part(t, s, g):
                    edges = [NT * q // 4 for q in range(5)]
                    for h in range(edges[g], edges[g + 1]):
                        if t is FIRST:
                            pe.wait_ge(hi_ready, l * NT + h + 1)
                            pe.wait_ge(lo_ready, l * NT + h + 1)
                        wide_ = D + 1 if l == 0 else D
                        def hi_part():
                            return pe.matmul(acc[s][:, 0:wide_], a16[:, s, h, :], x_hi[:, h, 0:wide_], start=(h == 0), stop=(h == NT - 1))
                        def lo_part():
                            return pe.matmul(acc[s][:, 0:D], a16[:, s, h, :], x_lo[:, h, :], start=False, stop=False)
                        if h < NT - 1:
                            hi_part()
                            lo_part()
                        else:
                            lo_part()
                            hi_part().then_inc(acc_done, 1)

                def tile(t, s, before_, prev=None, rows_=P):
                    n = 0 if t is FIRST else t
                    pe.wait_ge(a_in[s], 32 * (l * USES[s] + before_ + 1))
                    pe.wait_ge(acc_used, l * NT + n + (2 if t is FIRST else 1))
                    for g in range(4):
                        if g == 1 and prev is not None and l < 2:
                            turn((l + 1) * NT + prev)
                        if l == 0:
                            kv_step(n, g, rows_)
                        if l == 2:
                            mix_step(n, g)
                        part(t, s, g)
                    if prev is not None and l < 2:
                        project(l + 1, (l + 1) * NT + prev)
                tile(FIRST, 0, 0)
                with pe.Fori(0, NT // 2 - 1) as i:
                    tile(2 * i + 1, 1, i, 2 * i)
                    tile(2 * i + 2, 0, i + 1, 2 * i + 1)
                tile(NT - 2, 1, NT // 2 - 1, NT - 3)
                tile(NT - 1, 0, NT // 2, NT - 2, LAST)
                if l < 2:
                    turn((l + 1) * NT + NT - 1)
                    project(l + 1, (l + 1) * NT + NT - 1)
                if l == 0:
                    pe.matmul(psKV, zeros[:, 0:P], zeros[:, 0:HALVES * (P + 1)], start=False, stop=True).then_inc(m_KV, 1)

            def turn_u(t, s):
                pe.wait_ge(r_hs, t + 1)
                pe.wait_ge(r_hT, t + 1)
                for c_ in range(HALVES):
                    mm_ = pe.transpose(psT[s][:, c_ * P:(c_ + 1) * P], hs[:, s, c_ * P:(c_ + 1) * P], ident[:, :])
                mm_.then_inc(r_hsT, 1)

            def logit(t, s):
                pe.wait_ge(r_hT, t + 1 + RING)
                for c_ in range(HALVES):
                    mm_ = pe.matmul(psH[:, bass.ds(t * NX, NX)], hT[:, s, c_ * P:(c_ + 1) * P], wr[:, c_, :], start=(c_ == 0), stop=(c_ == HALVES - 1))
                mm_.then_inc(r_row, 1)
            turn_u(0, 0)
            with pe.Fori(0, NT // 2) as i:
                turn_u(2 * i + 1, 1)
                logit(2 * i, 0)
                turn_u(2 * i + 2, 0)
                logit(2 * i + 1, 1)
            logit(NT - 1, 0)
            pe.wait_ge(mask_ready, 1)
            pe.matmul(psA[:, 0:NE], before[:, :], pick, start=True, stop=True)
            pe.matmul(psB[:, 0:NE], ones[:, :], pick, start=True, stop=True).then_inc(rank_mm, 1)

            psX = bank[1]
            ups = [bank[4 + i] for i in range(4)]
            psY = [bank[2], bank[3]]
            pe.wait_ge(slots_ready, 1)

            def up(b, m, s):
                pe.wait_ge(b_h, b * MH + m + 1)
                for c_ in range(HALVES):
                    mm_ = pe.matmul(ups[m % 4][:, 0:BT], w_up[s][:, c_, m * P:(m + 1) * P], xeT[:, c_, :],
                                    start=(c_ == 0), stop=(c_ == HALVES - 1))
                mm_.then_inc(b_up, 1)

            def down(b, m, s):
                pe.wait_ge(b_h, b * MH + m + 1 + 4)
                for a in range(2):
                    mm_ = pe.matmul(psY[a][:, 0:D], hidT[:, m, a * P:(a + 1) * P], w_dn[s][:, m, :], start=False, stop=(m == MH - 1))
                return mm_

            def expert(e, s, i):
                lo = pe.value_load(blk_no[0:1, bass.ds(e, 1)], min_val=0, max_val=NBLK)
                hi = pe.value_load(blk_no[0:1, bass.ds(e + 1, 1)], min_val=0, max_val=NBLK)
                pe.wait_ge(wx_in[s], 48 * (i + 1))
                pe.sem_inc(pe_past, 1)
                with pe.Fori(lo, hi) as b:
                    pe.wait_ge(xs_in, 16 * (b + 1))
                    pe.wait_ge(b_xT, b)
                    for c_ in range(HALVES):
                        for a in range(2):
                            mm_ = pe.transpose(psX[:, c_ * BT + a * P:c_ * BT + (a + 1) * P], xs[:, a, c_ * P:(c_ + 1) * P], ident[:, :])
                    mm_.then_inc(b_T, 1)
                    pe.wait_ge(b_yc, b)
                    for a in range(2):
                        pe.matmul(psY[a][:, 0:D], ones[0:1, :], fb2row[0:1, s, :], start=True, stop=False)
                    pe.wait_ge(b_xT, b + 1)
                    up(b, 0, s)
                    for m in range(1, MH):
                        up(b, m, s)
                        down(b, m - 1, s)
                    down(b, MH - 1, s).then_inc(b_y, 1)
            with pe.Fori(0, NX // 2) as i:
                expert(2 * i, 0, i)
                expert(2 * i + 1, 1, i)

        @block.scalar
        def _(act):
            act.sem_inc(h_Tc, 1)
            act.sem_inc(prod_ready, 1)
            act.sem_inc(r_hT, RING)
            act.sem_inc(b_h, 4)
            for sem_ in win_free:
                act.sem_inc(sem_, 1)
            act.dma_start(raw_qkv, Wqkv.rearrange("(o p) c -> p o c", p=P)).then_inc(wraw_in, 16)
            n = 0
            for v in (key, src_t):
                for b0 in range(0, CB, 4):
                    w = min(4, CB - b0) * P
                    act.wait_ge(edgesT, n + 1)
                    act.activation(v[:, b0 * P:b0 * P + w], (psA, psB)[n % 2][:, 0:w], ACT.Copy).then_inc(edges_c, 1)
                    n += 1
            for i, (_, to, c_, o0, nb) in enumerate(turned):
                act.wait_ge(wT, i + 1)
                act.activation(to[:, c_, o0 * P:(o0 + nb) * P], (psA, psB)[i % 2][:, 0:nb * P], ACT.Copy).then_inc(wT_out, 1)
            act.wait_ge(mv_ready, 1)
            act.activation(rstd[:, :], mv[:, :, 1], ACT.Sqrt, bias=eps_ln[:, 0:1]).then_inc(sd_ready, 1)

            def copy_turned(n):
                act.wait_ge(h_T, n + 2)
                act.wait_ge(h_p, n + 1)
                act.activation(hrowT[:, :], psT[0][:, 0:D], ACT.Copy).then_inc(h_Tc, 1)

            def copy_product(t, n):
                act.wait_ge(h_p, n + 2)
                act.activation(prod[:, bass.ds(t, 1), :], psO[0][:, 0:D].unsqueeze(1), ACT.Copy).then_inc(prod_ready, 1)

            act.wait_ge(cum_ready, 1)
            act.wait_ge(xn_ready, NT)

            def build(t, s, before_):
                act.wait_ge(h_T, t + 1)
                act.activation(hrow[:, :], nodes[:, bass.ds(t, 1), :], ACT.Copy).then_inc(h_ready, 1)
                act.wait_ge(a_out[s], 16 * (before_ + 1))
                act.wait_ge(deg_added, t + 1)
                for i in range(WPT):
                    if i == 2:
                        copy_turned(t)
                    if i == 5:
                        copy_product(t, t)
                    act.wait_ge(win_ready[i % 2], t * (WPT // 2) + i // 2 + 1)
                    for h, half in enumerate(windows[i % 2]):
                        d0 = i * DW + h * DW // 2
                        ins = act.activation(a16[:, s, :, d0:d0 + DW // 2], half[:, 0:HW_].rearrange("p (d n) -> p n d", n=NT),
                                             ACT.Copy, scale=0.25)
                    ins.then_inc(win_free[i % 2], 1)
                act.sem_inc(act_past, 1)
                act.wait_ge(win_free[1], t * (WPT // 2) + WPT // 2 + 1)
                act.wait_ge(win_free[0], t * (WPT // 2) + WPT // 2 + 1)
                act.sem_inc(a_ready, 1)
            by_two(act, build)
            act.wait_ge(degs, 1)
            act.activation(norm_src[:, :], deg[:, :], ACT.Sqrt).then_inc(deg_sd, 1)

            def kv_step(t, g):
                if g == 0:
                    act.wait_ge(m_T, t)
                    act.activation(mrow[:, :], nodes[:, bass.ds(t, 1), :], ACT.Copy).then_inc(m_row, 1)
                    act.wait_ge(m_T, t + 1)
                    act.wait_ge(m_P, t)
                    act.activation(mT[:, :], psA[:, 0:D], ACT.Copy).then_inc(m_xT, 1)
                if g == 2:
                    act.wait_ge(m_P, t + 1)
                    act.wait_ge(m_KV, t)
                    act.activation(vaug[:, :, 0:P], psC[:, 0:D].rearrange("p (c n) -> p c n", c=HALVES), ACT.Copy).then_inc(m_v, 1)
                    act.wait_ge(m_min, t + 1)
                    act.wait_ge(m_f, t)
                    act.activation(mexp[:, :], melu[:, :], ACT.Exp).then_inc(m_exp, 1)

            def mix_step(t, g):
                if g == 0:
                    act.wait_ge(m_T, NT + t)
                    act.wait_ge(n_x1, t)
                    act.activation(mrow[:, :], nodes[:, bass.ds(t, 1), :], ACT.Copy).then_inc(m_row, 1)
                    act.wait_ge(m_T, NT + t + 1)
                    act.wait_ge(n_h, t)
                    act.activation(mT[:, :], psA[:, 0:D], ACT.Copy).then_inc(m_xT, 1)
                    act.wait_ge(m_min, NT + t + 1)
                    act.wait_ge(m_f, NT + t)
                    act.activation(mexp[:, :], melu[:, :], ACT.Exp).then_inc(m_exp, 1)
                if g == 1:
                    act.wait_ge(n_mv, 2 * t + 1)
                    act.activation(sd1[:, :], mv1[:, 1:2], ACT.Sqrt, bias=eps_ln[:, 0:1]).then_inc(n_sd, 1)
                if g == 2:
                    act.wait_ge(n_T, t + 1)
                    act.wait_ge(m_P, NT + t + 1)
                    act.activation(mT[:, :], psA[:, 0:D], ACT.Copy).then_inc(n_x1T, 1)
                    act.wait_ge(n_h, t + 1)
                    act.wait_ge(n_t, t + 1)
                    for o in range(HALVES):
                        act.activation(mfeat[:, o * P:(o + 1) * P], psB[:, o * P:(o + 1) * P], ACT.Gelu, bias=b1col[:, o:o + 1]).then_inc(n_g, 1)
                if g == 3:
                    act.wait_ge(n_mv, 2 * t + 2)
                    act.activation(sd1[:, :], mv1[:, 1:2], ACT.Sqrt, bias=eps_ln[:, 0:1]).then_inc(n_sd, 1)

            for l in range(3):
                act.wait_ge(nss_ready, l + 1)
                def split(t):
                    act.activation(x_hi[:, bass.ds(t, 1), 0:D], prod[:, bass.ds(t, 1), :], ACT.Copy, scale=nss[:, bass.ds(t, 1)]).then_inc(hi_ready, 1)
                with act.Fori(0, NT) as t:
                    split(t)
                if l == 2:
                    for i, (_, to, c_, o0, nb) in enumerate(turned2):
                        act.wait_ge(wmT, i + 1)
                        act.activation(to[:, c_, o0 * P:(o0 + nb) * P], (psA, psB)[i % 2][:, 0:nb * P], ACT.Copy).then_inc(wmT_out, 1)

                def tile(t, prev):
                    if l == 0 and prev is not None:
                        act.wait_ge(degs, prev + 2)
                        act.activation(col[:, 3:4], col[:, 2:3], ACT.Sqrt).then_inc(deg_sd, 1)
                    for g in range(4):
                        if l == 0:
                            kv_step(t, g)
                        if l == 2:
                            mix_step(t, g)
                        if g == 1 and prev is not None and l < 2:
                            copy_turned((l + 1) * NT + prev)
                    if prev is not None and l < 2:
                        copy_product(prev, (l + 1) * NT + prev)
                tile(0, None)
                with act.Fori(1, NT) as t:
                    tile(t, t - 1)
                if l == 0:
                    act.wait_ge(degs, NT + 1)
                    act.activation(col[:, 3:4], col[:, 2:3], ACT.Sqrt).then_inc(deg_sd, 1)
                if l < 2:
                    copy_turned((l + 1) * NT + NT - 1)
                    copy_product(NT - 1, (l + 1) * NT + NT - 1)

            act.wait_ge(mv_ready, 2)
            act.activation(rstd[:, :], mv[:, :, 1], ACT.Sqrt, bias=eps_ln[:, 0:1]).then_inc(sd_ready, 1)

            def copy_u(t, s, before_):
                act.wait_ge(r_hsT, t + 1 + RING)
                act.wait_ge(r_row, t + 1)
                act.activation(hT[:, s, :], psT[s][:, 0:D], ACT.Copy).then_inc(r_hT, 1)
            by_two(act, copy_u)
            act.wait_ge(mv_ready, 3)
            act.activation(rstd[:, :], mv[:, :, 1], ACT.Sqrt, bias=eps_ln[:, 0:1]).then_inc(sd_ready, 1)
            act.wait_ge(fm, 1)
            act.activation(gate2[:, :], gate1[:, :], ACT.Exp).then_inc(fe, 1)

            act.wait_ge(slots_ready, 1)
            with act.Fori(0, NX) as e:
                lo = act.value_load(blk_no[0:1, bass.ds(e, 1)], min_val=0, max_val=NBLK)
                hi = act.value_load(blk_no[0:1, bass.ds(e + 1, 1)], min_val=0, max_val=NBLK)
                with act.Fori(lo, hi) as b:
                    act.wait_ge(b_y, b)
                    for m in range(MH):
                        act.wait_ge(b_up, b * MH + m + 1)
                        act.activation(hidT[:, m, :], bank[4 + m % 4][:, 0:BT], ACT.Gelu,
                                       bias=fb1col[:, bass.ds(e, 1), m:m + 1]).then_inc(b_h, 1)

        @block.vector
        def _(dve):
            c = Chain(dve, vo)

            def copy(to, of):
                return dve.tensor_scalar(to, of, 1.0, None, ALU.mult)

            dve.sem_inc(acc_used, RING)
            dve.memset(dst_i, -1).then_inc(raw_clear, 1)
            dve.memset(src_i, -1).then_inc(raw_clear, 1)
            dve.memset(span_rows, -1).then_inc(sp_clear, 1)
            dve.memset(zeros[:, :], 0.0)
            dve.memset(eps_ln[:, :], LN_EPS)
            dve.memset(cum[:, 0:1], 0)
            dve.memset(cnt_f[:, 3, :], 1.0)
            dve.memset(far, 0.0)
            dve.memset(kvblk[:, :, :], 0.0)
            c.link(dve.memset(nodes[:, NT - 1, :], 0.0))
            dve.sem_inc(c_vec, 1)
            dve.wait_ge(dst_in, 48)
            dve.tensor_copy(dst_f, dst_i).then_inc(edges_f, 1)
            dve.wait_ge(src_in, 48)
            dve.tensor_copy(src_f, src_i).then_inc(edges_f, 1)
            dve.wait_ge(sp_in, 48)
            dve.tensor_reduce(mm[:, 0, :], span_rows, AX_X, ALU.min)
            c.link(dve.tensor_reduce(mm[:, 1, :], span_rows, AX_X, ALU.max))
            c.link(dve.tensor_scalar(mm[:, :, :], mm[:, :, :], DW.bit_length() - 1, None, ALU.arith_shift_right))
            c.link(dve.tensor_copy(mmf[:, :, :], mm[:, :, :]))
            dve.wait_ge(c_iota, 1)
            dve.wait_ge(c_mat, 1)
            for j in range(SB):
                c.link(dve.tensor_scalar(mask, w_no, mmf[:, 0, j:j + 1], None, ALU.is_ge))
                c.link(dve.scalar_tensor_tensor(out=mask, in0=w_no, scalar=mmf[:, 1, j:j + 1], in1=mask, op0=ALU.is_le, op1=ALU.mult))
                for k in range(2):
                    ins = dve.scalar_tensor_tensor(out=far[:, k, :], in0=mask, scalar=span_no[:, k, j:j + 1], in1=far[:, k, :],
                                                   op0=ALU.mult, op1=ALU.max)
                c.link(ins)
            dve.sem_inc(far_ready, 1)
            dve.wait_ge(edges_c, 2 * -(-CB // 4))
            c.link(dve.tensor_scalar(hi_f.bitcast(I32), src_t, 7, None, ALU.arith_shift_right))
            c.link(dve.tensor_scalar(src_t, src_t, P - 1, None, ALU.bitwise_and))
            dve.tensor_copy(sl, src_t)
            c.link(dve.scalar_tensor_tensor(out=key, in0=key, scalar=float(NT), in1=hi_f.bitcast(I32), op0=ALU.mult, op1=ALU.add))
            dve.sem_inc(key_ready, 1)
            dve.wait_ge(farT, 1)
            q = slice(0, WSP)
            for k, ps in enumerate((psC, psH)):
                ins = dve.tensor_reduce(wl[q, k, :], ps[q, 0:WS * P].rearrange("p (s n) -> p s n", s=WS), AX_X, ALU.max)
            c.link(ins)
            c.link(dve.tensor_scalar(wl[q, 0, :], wl[q, 0, :], 1.0, None, ALU.max))
            c.link(dve.tensor_scalar(wl[q, 1, :], wl[q, 1, :], -1.0, float(NS), ALU.mult, ALU.add))
            c.link(dve.tensor_scalar(mmf[q, 0, 0:WS], wl[q, 0, :], -1.0, None, ALU.add))
            c.link(dve.tensor_tensor(wl[q, 1, :], wl[q, 1, :], mmf[q, 0, 0:WS], ALU.min))
            c.link(dve.tensor_copy(wi[q, 0, :], wl[q, 1, :]))
            c.link(dve.tensor_copy(wi[q, 1, :], wl[q, 0, :]))
            dve.sem_inc(wi_ready, 1)

            def stats(l, src_of, order):
                with dve.Fori(0, NT) as t:
                    k = Chain(dve, order, (l * NT + t) * 3)
                    k.link(dve.bn_stats(st6[:, :], src_of(t)), dve_past)
                    k.link(dve.bn_aggr(mv1[:, :], st6[:, :]))
                    k.link(copy(mv[:, bass.ds(t, 1), :], mv1[:, :].unsqueeze(1)), dve_past)
                dve.sem_inc(mv_ready, 1)

            dve.wait_ge(x_in, 32)
            stats(0, lambda t: nodes[:, bass.ds(t, 1), :], r_vo)
            dve.wait_ge(bounds_in, 32)
            lo_r, hi_r = shift[0:1, :], cum[0:1, 1:NW + 1]
            c.link(dve.tensor_tensor(cnt_f[0:1, 0, :], hi_r, lo_r, ALU.subtract))
            c.link(dve.tensor_tensor_scan(cnt_f[0:1, 1, :], cnt_f[0:1, 3, :], cnt_f[0:1, 0, :], 0.0, ALU.mult, ALU.add))
            c.link(dve.tensor_tensor(cnt_f[0:1, 2, :], cnt_f[0:1, 1, :], cnt_f[0:1, 0, :], ALU.subtract))
            c.link(dve.tensor_tensor(shift[0:1, :], lo_r, cnt_f[0:1, 2, :], ALU.subtract))
            c.link(dve.tensor_copy(hi_r, cnt_f[0:1, 1, :]))
            dve.sem_inc(cum_ready, 1)
            dve.wait_ge(sd_ready, 1)
            c.link(dve.reciprocal(rstd[:, :], rstd[:, :]))
            with dve.Fori(0, NT) as t:
                dve.tensor_scalar(nodes[:, bass.ds(t, 1), :], nodes[:, bass.ds(t, 1), :], mv[:, bass.ds(t, 1), 0:1],
                                  rstd[:, bass.ds(t, 1)], ALU.subtract, ALU.mult).then_inc(xn_ready, 1)

            def largest(t, n):
                dve.wait_ge(prod_ready, n + 2)
                dve.tensor_reduce(ymax[:, 0, bass.ds(t, 1)], prod[:, bass.ds(t, 1), :], AX_X, ALU.max)
                dve.tensor_reduce(ymax[:, 1, bass.ds(t, 1)], prod[:, bass.ds(t, 1), :], AX_X, ALU.min).then_inc(max_done, 1)

            def build(t, s, before_):
                lo = dve.value_load(cum[0:1, bass.ds(t * WPT, 1)], min_val=0, max_val=NW * NS)
                for i in range(WPT):
                    w = t * WPT + i
                    hi = dve.value_load(cum[0:1, bass.ds(w + 1, 1)], min_val=0, max_val=NW * NS)
                    off = dve.value_load(shift[0:1, bass.ds(w, 1)], min_val=-NW * NS, max_val=NS)
                    with dve.Fori(lo, hi) as p:
                        q_ = nc.s_assert_within(dve.snap(p + off), 0, NS - 1,
                                                skip_runtime_bounds_check_because="a window's spans, first to last")
                        for j in range(SC):
                            dve.wait_ge(oh_free[j], p + 1)
                            dve.tensor_scalar(onehot_lo[:, j, :], iota_lo, sl[:, bass.ds(q_ * SC + j, 1)], None, ALU.is_equal)
                            dve.tensor_scalar(onehot_w[:, j, :], iota_w, w_base[:, bass.ds(w, 1)], key[:, bass.ds(q_ * SC + j, 1)],
                                              ALU.add, ALU.is_equal).then_inc(oh_ready[j], 1)
                    lo = hi
                largest(t, t)
            by_two(dve, build)
            dve.wait_ge(deg_added, NT + RING)
            c.link(dve.tensor_reduce(deg[:, :], deg_acc.rearrange("p (t n) -> p t n", t=NT), AX_X, ALU.add))
            c.link(dve.tensor_scalar(deg[:, :], deg[:, :], 4.0, 1.0, ALU.mult, ALU.max))
            dve.sem_inc(degs, 1)
            dve.wait_ge(deg_sd, 1)
            c.link(dve.reciprocal(norm_src[:, :], norm_src[:, :]))
            total = dve.value_load(cum[0:1, NW:NW + 1], min_val=1, max_val=NW * NS)
            for j in range(SC):
                dve.wait_ge(oh_free[j], total + 1)
            dve.sem_inc(dve_past, 1)
            c.link(dve.memset(x_hi[:, :, D:D + 1], 4.0))

            def elu_part(base, t, free, free_at):
                dve.wait_ge(m_P, base + t + 1)
                dve.wait_ge(m_exp, base + t)
                dve.tensor_scalar(melu[:, :], psB[:, 0:D], 0.0, None, ALU.min).then_inc(m_min, 1)
                dve.wait_ge(m_exp, base + t + 1)
                dve.wait_ge(free, free_at)
                dve.scalar_tensor_tensor(out=mfeat[:, :], in0=psB[:, 0:D], scalar=0.0, in1=mexp[:, :],
                                         op0=ALU.max, op1=ALU.add).then_inc(m_f, 1)

            def normalise(k, v, g_row, b_row, t, n):
                k.link(dve.bn_stats(st6[:, :], v), dve_past)
                dve.bn_aggr(mv1[:, :], st6[:, :]).then_inc(n_mv, 1)
                dve.wait_ge(n_sd, 2 * t + n)
                k.link(dve.reciprocal(sd1[:, :], sd1[:, :]))
                k.link(dve.tensor_scalar(v, v, mv1[:, 0:1], sd1[:, 0:1], ALU.subtract, ALU.mult))
                k.link(dve.tensor_tensor(v, v, g_row, ALU.mult))

            K1, K2 = 8, 7

            def mix_step(t, g):
                if g == 0:
                    elu_part(NT, t, n_y, t)
                if g == 1:
                    k = Chain(dve, n_vo, t * (K1 + K2))
                    dve.wait_ge(n_t, t + 1)
                    pv = psC[:, 0:HALVES * (P + HPB)].rearrange("p (c n) -> p c n", c=HALVES)
                    k.link(dve.tensor_scalar(z[:, :, :], pv[:, :, P:P + HPB], ATTN_EPS, None, ALU.add))
                    k.link(dve.reciprocal(z[:, :, :], z[:, :, :]))
                    dve.wait_ge(n_T, t)
                    k.link(dve.tensor_tensor(x1[:, :].rearrange("p (c h n) -> p c h n", c=HALVES, h=HPB),
                                             pv[:, :, 0:P].rearrange("p c (h n) -> p c h n", h=HPB),
                                             z[:, :, :].unsqueeze(3).broadcast_to([P, HALVES, HPB, HD]), ALU.mult))
                    k.link(dve.tensor_tensor(x1[:, :], x1[:, :], mrow[:, :], ALU.add), dve_past)
                    normalise(k, x1[:, :], r1g, r1b, t, 1)
                    assert k.n == K1
                    dve.tensor_tensor(x1[:, :], x1[:, :], r1b, ALU.add).then_inc(n_x1, 1)
                if g == 3:
                    k = Chain(dve, n_vo, t * (K1 + K2) + K1)
                    dve.wait_ge(n_y, t + 1)
                    dve.wait_ge(n_x1, t + 1)
                    k.link(dve.tensor_tensor(tmp[:, :], psC[:, 0:D], rb2, ALU.add))
                    k.link(dve.tensor_tensor(tmp[:, :], tmp[:, :], x1[:, :], ALU.add), dve_past)
                    normalise(k, tmp[:, :], r2g, r2b, t, 2)
                    k.link(dve.tensor_tensor(tmp[:, :], tmp[:, :], r2b, ALU.add))
                    assert k.n == K2
                    dve.wait_ge(xo_in, 16 * (t + 1))
                    dve.tensor_tensor(nodes[:, bass.ds(t, 1), :], tmp[:, :].unsqueeze(1), xo[:, :].unsqueeze(1), ALU.add).then_inc(n_out, 1)

            def scale_of(l):
                dve.wait_ge(max_done, (l + 1) * NT)
                c.link(dve.tensor_scalar(ymax[:, 1, :], ymax[:, 1, :], -1.0, None, ALU.mult))
                c.link(dve.tensor_reduce(col[:, 0:1], ymax[:, :, :].rearrange("p k t -> p (k t)"), AX_X, ALU.max))
                dve.sem_inc(g_row, 1)
                dve.wait_ge(g_T, 2 * l + 1)
                c.link(dve.tensor_reduce(col[0:1, 1:2], psT[0][0:1, 0:P], AX_X, ALU.max))
                dve.sem_inc(g_row, 1)
                dve.wait_ge(g_T, 2 * l + 2)
                v = col[:, 4:5]

                def power():
                    c.link(dve.tensor_scalar(v.bitcast(I32), v.bitcast(I32), 0x7F800000, None, ALU.bitwise_and))
                c.link(dve.tensor_scalar(v, psT[0][:, 0:1], 2.0 ** -14, 1e-30, ALU.mult, ALU.max))
                power()
                c.link(dve.reciprocal(v, v))
                power()
                c.link(dve.tensor_scalar(nss[:, :], norm_src[:, :], v, None, ALU.mult))
                dve.sem_inc(nss_ready, 1)
                c.link(dve.reciprocal(v, v))
                c.link(dve.tensor_scalar(v, v, 1.5, None, ALU.mult))
                power()
                c.link(dve.tensor_scalar(col[:, 5:6], v, 4.0, None, ALU.mult))

            dve.wait_ge(w_in, 16 * (3 + 3 + 2 + 3 * NX))
            for l in range(3):
                scale_of(l)
                with dve.Fori(0, NT) as t:
                    dve.wait_ge(hi_ready, l * NT + t + 1)
                    dve.scalar_tensor_tensor(out=x_lo[:, bass.ds(t, 1), :], in0=prod[:, bass.ds(t, 1), :], scalar=nss[:, bass.ds(t, 1)],
                                             in1=x_hi[:, bass.ds(t, 1), 0:D], op0=ALU.mult, op1=ALU.subtract).then_inc(lo_ready, 1)
                if l == 2:
                    dve.wait_ge(w2_in, 16 * 5)

                K = (5, 2, 6)[l]

                def finish(t, s):
                    k = Chain(dve, p_vo, sum((5, 2, 6)[:l]) * NT + t * K)
                    dve.wait_ge(acc_done, l * NT + t + 1 + RING)
                    if l == 2:
                        dve.wait_ge(n_out, t + 1)
                    if l == 0:
                        k.link(dve.tensor_scalar(col[:, 2:3], acc[s][:, D:D + 1], 1.0, None, ALU.max))
                        dve.sem_inc(degs, 1)
                        dve.wait_ge(deg_sd, t + 2)
                        k.link(dve.reciprocal(col[:, 3:4], col[:, 3:4]))
                        k.link(copy(norm_dst[:, bass.ds(t, 1)], col[:, 3:4]))
                        k.link(dve.tensor_scalar(col[:, 6:7], col[:, 3:4], col[:, 5:6], None, ALU.mult))
                    else:
                        k.link(dve.tensor_scalar(col[:, 6:7], norm_dst[:, bass.ds(t, 1)], col[:, 5:6], None, ALU.mult))
                    k.link(dve.scalar_tensor_tensor(out=tmp[:, :], in0=acc[s][:, 0:D], scalar=col[:, 6:7], in1=gb[l], op0=ALU.mult, op1=ALU.add))
                    if l < 2:
                        dve.wait_ge(h_T, (l + 1) * NT + t + 1)
                        dve.tensor_scalar(hrow[:, :], tmp[:, :], 0.0, None, ALU.max).then_inc(h_ready, 1)
                        dve.wait_ge(h_ready, (l + 1) * NT + t + 1)
                        dve.sem_inc(acc_used, 1)
                        return
                    k.link(dve.tensor_tensor(nodes[:, bass.ds(t, 1), :], nodes[:, bass.ds(t, 1), :], tmp[:, :].unsqueeze(1), ALU.add), dve_past)
                    dve.sem_inc(acc_used, 1)
                    k.link(dve.bn_stats(st6[:, :], nodes[:, bass.ds(t, 1), :]), dve_past)
                    k.link(dve.bn_aggr(mv1[:, :], st6[:, :]))
                    k.link(copy(mv[:, bass.ds(t, 1), :], mv1[:, :].unsqueeze(1)), dve_past)

                def mixer(t):
                    for g in range(4):
                        if l == 0 and g == 2:
                            elu_part(0, t, m_KV, t)
                        if l == 2:
                            mix_step(t, g)
                mixer(0)
                with dve.Fori(0, NT // 2) as i:
                    for t, s in ((2 * i + 1, 1), (2 * i + 2, 0)):
                        finish(t - 1, 1 - s)
                        mixer(t)
                        if l < 2:
                            largest(t - 1, (l + 1) * NT + t - 1)
                finish(NT - 1, 0)
                if l < 2:
                    largest(NT - 1, (l + 1) * NT + NT - 1)
                if l == 0:
                    dve.wait_ge(m_KV, NT + 1)
                    for c_ in range(HALVES):
                        for h in range(HPB):
                            q, kv = slice(h * HD, (h + 1) * HD), c_ * (P + 1)
                            dve.tensor_copy(kvblk[q, c_, h * HD:(h + 1) * HD], psKV[q, kv + h * HD:kv + (h + 1) * HD])
                            ins = dve.tensor_copy(kvblk[q, c_, P + h:P + h + 1], psKV[q, kv + P:kv + P + 1])
                    ins.then_inc(kv_ready, 1)
            dve.sem_inc(mv_ready, 1)
            dve.wait_ge(sd_ready, 2)
            c.link(dve.reciprocal(rstd[:, :], rstd[:, :]))

            def u_tile(t, s, before_):
                dve.wait_ge(r_hsT, t + 1)
                k = Chain(dve, r_vo, 3 * NT + t * 3)
                dve.tensor_scalar(hs[:, s, :], nodes[:, bass.ds(t, 1), :], mv[:, bass.ds(t, 1), 0:1], rstd[:, bass.ds(t, 1)],
                                  ALU.subtract, ALU.mult).then_inc(r_hs, 1)
                dve.wait_ge(r_hs, t + 1)
                copy(prod[:, bass.ds(t, 1), :], hs[:, s, :].unsqueeze(1)).then_inc(u_kept, 1)
                k.link(dve.bn_stats(st6[:, :], hs[:, s, :]), dve_past)
                k.link(dve.bn_aggr(mv1[:, :], st6[:, :]))
                k.link(copy(mv[:, bass.ds(t, 1), :], mv1[:, :].unsqueeze(1)), dve_past)
            by_two(dve, u_tile)
            dve.wait_ge(u_kept, NT)
            dve.sem_inc(mv_ready, 1)

            def te(v):
                return v.rearrange("p (t e) -> p t e", e=NX)

            def over_e(v):
                return v.unsqueeze(2).broadcast_to([P, NT, NX])

            m1, p1, m2, p2, d12, inv, f1, f2 = (small[:, i, :] for i in range(8))
            desc = desc8[:, :].unsqueeze(1).broadcast_to([P, NT, NX])
            dve.wait_ge(r_row, NT + RING)
            c.link(dve.tensor_tensor(te(logits), te(psH[:, 0:NE]), br_row[:, :].unsqueeze(1).broadcast_to([P, NT, NX]), ALU.add))

            def first_max(v, m, p_, oh):
                c.link(dve.tensor_reduce(m, te(v), AX_X, ALU.max))
                c.link(dve.tensor_tensor(te(s_a), te(v), over_e(m), ALU.is_equal))
                c.link(dve.tensor_tensor(te(s_a), te(s_a), desc, ALU.mult))
                c.link(dve.tensor_reduce(p_, te(s_a), AX_X, ALU.max))
                c.link(dve.tensor_tensor(te(oh), desc, over_e(p_), ALU.is_equal))

            first_max(logits, m1, p1, oh1)
            c.link(dve.scalar_tensor_tensor(out=s_b, in0=oh1, scalar=-3.0e38, in1=logits, op0=ALU.mult, op1=ALU.add))
            first_max(s_b, m2, p2, oh2)
            c.link(dve.tensor_tensor(gate1[:, :], m2, m1, ALU.subtract))
            dve.sem_inc(fm, 1)
            for oh in (oh1, oh2):
                c.link(dve.tensor_tensor(te(oh), te(oh), over_e(valid[:, :]), ALU.mult))
            c.link(dve.tensor_tensor(pick, oh1, oh2, ALU.add))
            dve.sem_inc(mask_ready, 1)
            dve.wait_ge(fe, 1)
            c.link(dve.tensor_scalar(d12, gate2[:, :], 1.0, None, ALU.add))
            c.link(dve.reciprocal(gate1[:, :], d12))
            c.link(dve.tensor_tensor(gate2[:, :], gate2[:, :], gate1[:, :], ALU.mult))
            dve.wait_ge(rank_mm, 1)
            c.link(dve.tensor_copy(tot, psB[:, 0:NE]))
            for e in range(NX):
                c.link(dve.tensor_tensor_scan(incl.rearrange("p (t e) -> p e t", e=NX)[:, e, :], ones[:, 0:NT],
                                              tot.rearrange("p (t e) -> p e t", e=NX)[:, e, :], 0.0, ALU.mult, ALU.add))
            c.link(dve.tensor_tensor(start_r, incl, tot, ALU.subtract))
            c.link(dve.tensor_tensor(start_r, start_r, psA[:, 0:NE], ALU.add))
            c.link(dve.tensor_scalar(cnt8i[:, 0:NX], te(incl)[:, NT - 1, :], float(BT - 1), None, ALU.add))
            c.link(dve.tensor_scalar(cnt8i[:, 0:NX], cnt8i[:, 0:NX], 8, None, ALU.arith_shift_right))
            c.link(dve.tensor_scalar(cnt8[:, 0, 0:NX], cnt8i[:, 0:NX], 1.0, None, ALU.max))
            c.link(dve.tensor_tensor_scan(cnt8[:, 1, 0:NX], ones[:, 0:NX], cnt8[:, 0, 0:NX], 0.0, ALU.mult, ALU.add))
            c.link(dve.tensor_tensor(cnt8[:, 2, 0:NX], cnt8[:, 1, 0:NX], cnt8[:, 0, 0:NX], ALU.subtract))
            c.link(dve.memset(blk_no[:, 0:1], 0))
            c.link(dve.tensor_copy(blk_no[:, 1:NX + 1], cnt8[:, 1, 0:NX]))
            c.link(dve.tensor_scalar(cnt8[:, 2, 0:NX], cnt8[:, 2, 0:NX], float(BT), None, ALU.mult))
            c.link(dve.tensor_tensor(te(start_r), te(start_r), cnt8[:, 2, 0:NX].unsqueeze(1).broadcast_to([P, NT, NX]), ALU.add))
            c.link(dve.tensor_scalar(inv, valid[:, :], -float(P), float(P), ALU.mult, ALU.add))
            for oh, f, slot, take in ((oh1, f1, slot1, take1), (oh2, f2, slot2, take2)):
                c.link(dve.tensor_tensor(s_a, oh, start_r, ALU.mult))
                c.link(dve.tensor_reduce(f, te(s_a), AX_X, ALU.add))
                c.link(dve.tensor_copy(take[:, :], f))
                if oh is oh2:
                    c.link(dve.tensor_tensor(f, f, inv, ALU.add))
                c.link(dve.tensor_tensor(slot[:, :], f, dump[:, :], ALU.add))
            dve.sem_inc(slots_ready, 1)

            dve.wait_ge(sd_ready, 3)
            c.link(dve.reciprocal(rstd[:, :], rstd[:, :]))

            def spread(t, s, before_):
                dve.wait_ge(scat[s], 32 * before_)
                copy(sidx[:, s, 0:1], slot1[:, bass.ds(t, 1)])
                copy(sidx[:, s, 1:2], slot2[:, bass.ds(t, 1)])
                dve.tensor_scalar(st[:, s, :], prod[:, bass.ds(t, 1), 0:D], mv[:, bass.ds(t, 1), 0:1], rstd[:, bass.ds(t, 1)],
                                  ALU.subtract, ALU.mult).then_inc(r_xs, 1)
            by_two(dve, spread)

            with dve.Fori(0, NX) as e:
                lo = dve.value_load(blk_no[0:1, bass.ds(e, 1)], min_val=0, max_val=NBLK)
                hi = dve.value_load(blk_no[0:1, bass.ds(e + 1, 1)], min_val=0, max_val=NBLK)
                with dve.Fori(lo, hi) as b:
                    dve.wait_ge(b_T, b + 1)
                    dve.wait_ge(b_y, b)
                    for c_ in range(HALVES):
                        ins = dve.tensor_scalar(xeT[:, c_, :], bank[1][:, c_ * BT:(c_ + 1) * BT], fgcol[:, bass.ds(e, 1), c_:c_ + 1],
                                                fbcol[:, bass.ds(e, 1), c_:c_ + 1], ALU.mult, ALU.add)
                    ins.then_inc(b_xT, 1)
                    dve.wait_ge(b_y, b + 1)
                    dve.wait_ge(b_out, b * 16)
                    for a in range(2):
                        ins = dve.tensor_copy(ys[:, a, :], bank[2 + a][:, 0:D])
                    ins.then_inc(b_yc, 1)

            def combine(t, s, before_):
                dve.wait_ge(f_idx, t)
                if not isinstance(before_, int) or before_:
                    pass
                dve.wait_ge(f_got[s], 32 * (before_ + 1))
                dve.wait_ge(f_out[s], 16 * before_)
                k = Chain(dve, f_vo, t)
                dve.wait_ge(f_ready, t)
                k.link(dve.scalar_tensor_tensor(out=tmp[:, :], in0=hs[:, s, :], scalar=gate1[:, bass.ds(t, 1)],
                                                in1=nodes[:, bass.ds(t, 1), :], op0=ALU.mult, op1=ALU.add))
                dve.scalar_tensor_tensor(out=st[:, s, :], in0=hT[:, s, :], scalar=gate2[:, bass.ds(t, 1)],
                                         in1=tmp[:, :], op0=ALU.mult, op1=ALU.add).then_inc(f_ready, 1)

            def ask(t, s, before_):
                copy(sidx[:, s, 0:1], take1[:, bass.ds(t, 1)])
                copy(sidx[:, s, 1:2], take2[:, bass.ds(t, 1)]).then_inc(f_idx, 1)

            ask(0, 0, 0)
            with dve.Fori(0, NT // 2) as i:
                ask(2 * i + 1, 1, i)
                combine(2 * i, 0, i)
                ask(2 * i + 2, 0, i)
                combine(2 * i + 1, 1, i)
            combine(NT - 1, 0, NT // 2)


_GNN = ("L0_gnn_W", "L0_gnn_b")
_INS = ["x", "src", "dst", "L0_gnn_W0", "L0_gnn_b0", "L0_gnn_W1", "L0_gnn_b1", "L0_gnn_W2", "L0_gnn_b2", "L0_mix_Wqkv",
        "L0_mix_ln1_g", "L0_mix_ln1_b", "L0_mix_W1", "L0_mix_b1", "L0_mix_W2", "L0_mix_b2", "L0_mix_ln2_g", "L0_mix_ln2_b",
        "L0_ffn_Wr", "L0_ffn_br", "L0_ffn_ln_g", "L0_ffn_ln_b", "L0_ffn_W1", "L0_ffn_b1", "L0_ffn_W2", "L0_ffn_b2"]


def kernel(**inputs):
    import concourse.bacc as _bacc
    from concourse.bass_utils import run_bass_kernel_spmd as _run

    nc = _bacc.Bacc("TRN2", target_bir_lowering=False, num_devices=1)
    arrays, a = {}, {}
    for name in _INS:
        v = np.ascontiguousarray(inputs[name])
        arrays[f"in_{name}_dram"] = v
        a[name] = nc.dram_tensor(f"in_{name}_dram", v.shape, mybir.dt.from_np(v.dtype), kind="ExternalInput").ap()
    out = nc.dram_tensor("out_0_dram", arrays["in_x_dram"].shape, F32, kind="ExternalOutput").ap()
    gps_layer(nc, a["x"], a["src"], a["dst"], [a[f"L0_gnn_W{l}"] for l in range(3)], [a[f"L0_gnn_b{l}"] for l in range(3)],
              a["L0_mix_Wqkv"], a["L0_mix_ln1_g"], a["L0_mix_ln1_b"], a["L0_mix_W1"], a["L0_mix_b1"], a["L0_mix_W2"],
              a["L0_mix_b2"], a["L0_mix_ln2_g"], a["L0_mix_ln2_b"], a["L0_ffn_Wr"], a["L0_ffn_br"], a["L0_ffn_ln_g"],
              a["L0_ffn_ln_b"], a["L0_ffn_W1"], a["L0_ffn_b1"], a["L0_ffn_W2"], a["L0_ffn_b2"], out)
    r = _run(nc, [arrays], core_ids=[0])
    return r.results[0]["out_0_dram"]
```

```python
from contextlib import ExitStack

import numpy as np

import concourse.bass as bass
from concourse import mybir

ALU = mybir.AluOpType
ACT = mybir.ActivationFunctionType
AX_X = mybir.AxisListType.X
F32 = mybir.dt.float32
F16 = mybir.dt.float16
I32 = mybir.dt.int32
U32 = mybir.dt.uint32

P = 128
LN_EPS = 1e-5
ATTN_EPS = 1e-6
RING = 2


class Chain:

    def __init__(self, eng, sem, start=0):
        self.eng, self.sem, self.start, self.n = eng, sem, start, 0

    def link(self, ins, alone=None):
        self.n += 1
        ins.then_inc(self.sem, 1)
        self.eng.wait_ge(self.sem, self.start + self.n)
        if alone is not None:
            self.eng.sem_inc(alone, 1)


def gps_layer(nc, x, src, dst, gnn_W, gnn_b, Wqkv, ln1_g, ln1_b, mix_W1, mix_b1, mix_W2, mix_b2,
              ln2_g, ln2_b, Wr, br, ffn_g, ffn_b, ffn_W1, ffn_b1, ffn_W2, ffn_b2, out):
    N, D = x.shape
    E = src.shape[0]
    HALVES = D // P
    NT = -(-N // P)
    LAST = N - (NT - 1) * P
    NX = ffn_W1.shape[0]
    HID = ffn_W1.shape[2]
    MH = HID // P
    HEADS = 8
    HD = D // HEADS
    HPB = P // HD

    CB = -(-E // (P * P))
    FULLB = E // (P * P)
    TAILCH = (E - FULLB * P * P) // P
    TAILE = E - FULLB * P * P - TAILCH * P

    SC = 2
    SE = SC * P
    NS = -(-E // SE)
    SB = -(-NS // P)
    FULLS = E // SE
    DW = 16
    WPT = P // DW
    NW = NT * WPT
    HW_ = DW // 2 * NT
    WS = 4
    WSP = NW // WS
    SPAN_MOD = 1 << NS.bit_length()
    assert NS * SPAN_MOD < 1 << 24
    assert WS * WSP == NW and WSP <= P and HW_ <= 512 and NT % 2 == 1

    BT = 256
    NBLK = (2 * N) // BT + NX
    SLOTS = NBLK * BT
    LEAST = -(-2 * N // BT)
    NE = NT * NX

    adj = nc.dram_tensor("adj", (NT, P, NT * P), F16, kind="Internal").ap()
    bounds_d = nc.dram_tensor("bounds", (2, NW), I32, kind="Internal").ap()
    routed_in = nc.dram_tensor("routed_in", (SLOTS + 2 * P, D), F32, kind="Internal").ap()
    routed_out = nc.dram_tensor("routed_out", (SLOTS, D), F32, kind="Internal").ap()

    with ExitStack() as ctx:
        def sb(name, shape, dt=F32):
            return ctx.enter_context(nc.sbuf_tensor(name, shape, dt))

        def sem(name):
            return ctx.enter_context(nc.semaphore(name))

        nodes = sb("nodes", [P, NT, D])
        prod = sb("prod", [P, NT, D])
        xbuf = sb("xbuf", [P, (NT * (2 * D + 2) + 2) // 2])
        x16 = xbuf[:, :].bitcast(F16)
        x_hi = x16[:, 0:NT * (D + 2)].rearrange("p (t d) -> p t d", t=NT)[:, :, 0:D + 1]
        x_lo = x16[:, NT * (D + 2):NT * (2 * D + 2)].rearrange("p (t d) -> p t d", t=NT)
        abuf = sb("abuf", [P, NT * P])
        a16 = abuf[:, :].bitcast(F16).rearrange("p (s h d) -> p s h d", s=RING, h=NT)
        wqkvT = sb("wqkvT", [P, HALVES, 3 * D])
        wg = sb("wg", [P, RING, HALVES, D])
        wr = sb("wr", [P, HALVES, NX])
        rows = sb("rows", [P, 3, D])
        gb = [rows[:, i, :] for i in range(3)]
        br_row = sb("br_row", [P, NX])
        b1col = sb("b1col", [P, HALVES])
        fgcol = sb("fgcol", [P, NX, HALVES])
        fbcol = sb("fbcol", [P, NX, HALVES])
        fb1col = sb("fb1col", [P, NX, MH])
        desc8 = sb("desc8", [P, NX])
        fb2row = sb("fb2row", [1, RING, D])
        ident = sb("ident", [P, P])
        before = sb("before", [P, P])
        ones = sb("ones", [P, P])
        zeros = sb("zeros", [P, D + 8])
        cum = sb("cum", [1, NW + 1], I32)
        spans = sb("spans", [1, NW], I32)
        mm = sb("mm", [P, 2, SB], I32)
        mmf = sb("mmf", [P, 2, SB])
        span_no = sb("span_no", [P, 2, SB])
        wl = sb("wl", [P, 2, WS])
        wi = sb("wi", [P, 2, WS], I32)
        ymax = sb("ymax", [P, 2, NT])
        col = sb("col", [P, 8])
        nss = sb("nss", [P, NT])
        norm_src = sb("norm_src", [P, NT])
        norm_dst = sb("norm_dst", [P, NT])
        deg = sb("deg", [P, NT])
        mv = sb("mv", [P, NT, 2])
        st6 = sb("st6", [P, 6])
        rstd = sb("rstd", [P, NT])
        hrow = sb("hrow", [P, D])
        hrowT = sb("hrowT", [P, D])
        tmp = sb("tmp", [P, D])
        mix4 = sb("mix4", [P, 4, D])
        mrow, mT, melu, mexp = (mix4[:, i, :] for i in range(4))
        mfeat = sb("mfeat", [P, D])
        vaug = sb("vaug", [P, HALVES, P + 1])
        kvblk = sb("kvblk", [P, HALVES, P + HPB])
        z = sb("z", [P, HALVES, HPB])
        mv1 = sb("mv1", [P, 2])
        sd1 = sb("sd1", [P, 1])
        spare = mmf[:, 0, :]

        W_ = CB * P
        key, sl, src_t, hi_f = (xbuf[:, i * W_:(i + 1) * W_] for i in range(4))
        dst_i, src_i, dst_f, src_f = key.bitcast(I32), src_t.bitcast(I32), sl, hi_f
        src_t = src_t.bitcast(I32)
        o_ = 2 * W_
        deg_acc = xbuf[:, o_:o_ + NT * P]
        o_ += NT * P
        onehot_w = xbuf[:, o_:o_ + HW_ * SC].bitcast(F16).rearrange("p (j n) -> p j n", j=SC)
        o_ += HW_ * SC
        onehot_lo = xbuf[:, o_:o_ + SC * P // 2].bitcast(F16).rearrange("p (j n) -> p j n", j=SC)
        o_ += SC * P // 2
        iota_w = xbuf[:, o_:o_ + HW_].bitcast(F16)
        o_ += HW_
        w_base = xbuf[:, o_:o_ + NW]
        iota_lo = mix4[:, 0, 0:P // 2].bitcast(F16)
        pf = prod[:, :, :].rearrange("p a b -> p (a b)")
        span_rows = pf[:, 0:SB * SE].bitcast(I32).rearrange("p (j e) -> p j e", j=SB)
        o_ = SB * SE
        raw_qkv = pf[:, o_:o_ + 6 * D].rearrange("p (o c) -> p o c", o=6)
        o_ += 6 * D
        far = pf[:, o_:o_ + 2 * NW].rearrange("p (k n) -> p k n", k=2)
        mask = pf[:, o_ + 2 * NW:o_ + 3 * NW]
        w_no = pf[:, o_ + 3 * NW:o_ + 4 * NW]
        cnt_f = pf[0:1, o_ + 4 * NW:o_ + 8 * NW].rearrange("p (k n) -> p k n", k=4)
        def piece(i, n=1):
            return pf[:, i * D:(i + n) * D]
        w1T, w2T, raw_w1, raw_w2 = (piece(2 * i, 2).rearrange("p (c n) -> p c n", c=2) for i in range(4))
        r1g, r1b, r2g, r2b, rb2, xo, mgelu, grow = (piece(8 + i) for i in range(8))
        xg = piece(20)
        x1s = [piece(16 + i) for i in range(RING)]
        urow, urowT = piece(18), piece(19)
        turned = [(raw_qkv, wqkvT, c, o, n) for c in range(HALVES) for o, n in ((0, 4), (4, 2))]
        turned2 = [(raw, to, c, 0, 2) for raw, to in ((raw_w1, w1T), (raw_w2, w2T)) for c in range(HALVES)]

        flat = xbuf[:, :]
        def cut(i):
            return flat[:, i * 400:i * 400 + NE]
        logits, s_a, s_b, oh1, oh2, pick, incl, tot, start_r, ex = (cut(i) for i in range(10))
        small = flat[:, 4000:4000 + 20 * NT].rearrange("p (a b) -> p a b", b=NT)
        w_up = [flat[:, s * 4096:s * 4096 + HALVES * HID].rearrange("p (c n) -> p c n", c=HALVES) for s in range(2)]
        w_dn = [flat[:, s * 4096 + HALVES * HID:(s + 1) * 4096].rearrange("p (m n) -> p m n", m=MH) for s in range(2)]
        gate1 = sb("gate1", [P, NT])
        gate2 = sb("gate2", [P, NT])
        slot1 = sb("slot1", [P, NT], I32)
        slot2 = sb("slot2", [P, NT], I32)
        take1 = sb("take1", [P, NT], I32)
        take2 = sb("take2", [P, NT], I32)
        valid = sb("valid", [P, NT])
        halves = sb("halves", [P, NT])
        dump = sb("dump", [P, NT])
        sidx = sb("sidx", [P, RING, 2], I32)
        blk_no = sb("blk_no", [P, 16], I32)
        cnt8 = sb("cnt8", [P, 4, 16])
        cnt8i = sb("cnt8i", [P, 16], I32)
        xs = abuf[:, 0:2 * D].rearrange("p (a n) -> p a n", a=2)
        xeT = abuf[:, 2 * D:4 * D].rearrange("p (a n) -> p a n", a=2)
        ys = abuf[:, 4 * D:6 * D].rearrange("p (a n) -> p a n", a=2)
        hidT = abuf[:, 6 * D:6 * D + MH * BT].rearrange("p (m n) -> p m n", m=MH)
        hs, hT, st = (abuf[:, 3584 + i * 2 * D:3584 + (i + 1) * 2 * D].rearrange("p (s n) -> p s n", s=RING) for i in range(3))

        bank = [ctx.enter_context(nc.psum_tensor(f"bank{i}", [P, 512], F32)) for i in range(8)]
        acc = [bank[0], bank[7]]
        windows = [(bank[0], bank[3]), (bank[6], bank[7])]
        psT = [bank[1], bank[4]]
        psKV = bank[2][:, 0:HALVES * (P + 1)]
        psA = bank[4]
        psB = bank[5]
        psC = bank[6]
        psH = bank[7]
        psL = bank[2][:, 0:NE]
        psY0 = bank[3]

        c_iota = sem("c_iota"); c_mat = sem("c_mat"); c_vec = sem("c_vec")
        vo = sem("vo"); po = sem("po")
        dve_past = sem("dve_past"); pe_past = sem("pe_past"); pool_past = sem("pool_past")
        act_past = sem("act_past")
        raw_clear = sem("raw_clear"); dst_in = sem("dst_in"); src_in = sem("src_in")
        sp_clear = sem("sp_clear"); sp_in = sem("sp_in"); far_ready = sem("far_ready"); farT = sem("farT")
        wi_ready = sem("wi_ready")
        bounds_out = sem("bounds_out"); bounds_in = sem("bounds_in"); cum_ready = sem("cum_ready")
        edges_f = sem("edges_f"); edgesT = sem("edgesT"); edges_c = sem("edges_c"); key_ready = sem("key_ready")
        w_in = sem("w_in"); wraw_in = sem("wraw_in"); wT = sem("wT"); wT_out = sem("wT_out")
        wg_in = sem("wg_in"); w2_in = sem("w2_in"); w2raw_in = sem("w2raw_in")
        wmT = sem("wmT"); wmT_out = sem("wmT_out")
        x_in = sem("x_in"); mv_ready = sem("mv_ready"); sd_ready = sem("sd_ready"); xn_ready = sem("xn_ready")
        oh_ready = [sem(f"oh_ready{j}") for j in range(SC)]
        oh_free = [sem(f"oh_free{j}") for j in range(SC)]
        win_ready = [sem(f"win_ready{s}") for s in range(RING)]
        win_free = [sem(f"win_free{s}") for s in range(RING)]
        a_ready = sem("a_ready"); a_out = [sem(f"a_out{s}") for s in range(RING)]; deg_added = sem("deg_added")
        h_ready = sem("h_ready"); h_T = sem("h_T"); h_Tc = sem("h_Tc"); h_p = sem("h_p"); prod_ready = sem("prod_ready")
        max_done = sem("max_done")
        a_in = [sem(f"a_in{s}") for s in range(RING)]
        acc_done = sem("acc_done"); acc_used = sem("acc_used")
        g_T = sem("g_T"); g_row = sem("g_row"); nss_ready = sem("nss_ready")
        hi_ready = sem("hi_ready"); lo_ready = sem("lo_ready"); p_vo = sem("p_vo")
        r_hs = sem("r_hs"); r_hsT = sem("r_hsT"); r_hT = sem("r_hT"); r_row = sem("r_row")
        m_row = sem("m_row"); m_T = sem("m_T"); m_xT = sem("m_xT"); m_P = sem("m_P"); m_min = sem("m_min")
        m_exp = sem("m_exp"); m_v = sem("m_v"); m_f = sem("m_f"); m_KV = sem("m_KV"); kv_ready = sem("kv_ready")
        n_t = sem("n_t"); n_mv = sem("n_mv"); n_sd = sem("n_sd"); n_x1 = sem("n_x1"); n_T = sem("n_T")
        n_x1T = sem("n_x1T"); n_h = sem("n_h"); n_g = sem("n_g"); n_y = sem("n_y")
        n_out = sem("n_out"); xo_in = sem("xo_in"); n_vo = sem("n_vo")
        deg_sd = sem("deg_sd");
        zero_out = sem("zero_out"); degs = sem("degs")
        n_xn = sem("n_xn"); xg_ready = sem("xg_ready"); r_vo = sem("r_vo");
        r_xs = sem("r_xs"); scat = [sem(f"scat{s}") for s in range(RING)]
        fm = sem("fm"); fe = sem("fe"); rank_mm = sem("rank_mm"); mask_ready = sem("mask_ready")
        slots_ready = sem("slots_ready"); pool_c = sem("pool_c")
        wx_in = [sem(f"wx_in{s}") for s in range(RING)]
        xs_in = sem("xs_in"); b_T = sem("b_T"); b_xT = sem("b_xT"); b_up = sem("b_up"); b_h = sem("b_h")
        b_y = sem("b_y"); b_yc = sem("b_yc"); b_out = sem("b_out")
        f_idx = sem("f_idx"); f_got = [sem(f"f_got{s}") for s in range(RING)]; f_vo = sem("f_vo")
        f_ready = sem("f_ready"); f_out = [sem(f"f_out{s}") for s in range(RING)]

        block = ctx.enter_context(nc.Block())

        def by_two(eng, body):
            with eng.Fori(0, NT // 2) as i:
                body(2 * i, 0, i)
                body(2 * i + 1, 1, i)
            body(NT - 1, 0, NT // 2)

        USES = [NT // 2 + 1, NT // 2]

        @block.sync
        def _(sp):
            sp.sem_inc(b_out, 16)
            for s in range(RING):
                sp.sem_inc(f_out[s], 16)
                sp.sem_inc(a_out[s], 16)
            sp.wait_ge(raw_clear, 2)
            for e_dram, e_sb, s in ((dst, dst_i, dst_in), (src, src_i, src_in)):
                v = e_sb.rearrange("p (g e) -> p g e", e=P)
                full = FULLB * P * P
                sp.dma_start(v[:, 0:FULLB, :], e_dram[0:full].rearrange("(g q e) -> q g e", q=P, e=P)).then_inc(s, 16)
                sp.dma_start(v[0:TAILCH, FULLB, :],
                             e_dram[full:full + TAILCH * P].rearrange("(q e) -> q e", e=P)).then_inc(s, 16)
                sp.dma_start(v[TAILCH:TAILCH + 1, FULLB, 0:TAILE],
                             e_dram[full + TAILCH * P:E].rearrange("(q e) -> q e", q=1)).then_inc(s, 16)
            sp.wait_ge(sp_clear, 1)
            whole = FULLS // P
            sp.dma_start(span_rows[:, 0:whole, :], dst[0:whole * P * SE].rearrange("(j q e) -> q j e", q=P, e=SE)).then_inc(sp_in, 16)
            rest = FULLS - whole * P
            sp.dma_start(span_rows[0:rest, whole, :], dst[whole * P * SE:FULLS * SE].rearrange("(q e) -> q e", e=SE)).then_inc(sp_in, 16)
            sp.dma_start(span_rows[rest:rest + 1, whole, :], dst[E - SE:E].rearrange("(q e) -> q e", q=1)).then_inc(sp_in, 16)
            sp.wait_ge(c_vec, 1)
            sp.dma_start(nodes[:, 0:NT - 1, :], x[0:(NT - 1) * P, :].rearrange("(t p) d -> p t d", p=P)).then_inc(x_in, 16)
            sp.dma_start(nodes[0:LAST, NT - 1, :], x[(NT - 1) * P:N, :]).then_inc(x_in, 16)
            for l in range(2):
                sp.dma_start(wg[:, l, :, :], gnn_W[l].rearrange("(c p) n -> p c n", p=P)).then_inc(w_in, 16)
            sp.dma_start(wr[:, :, :], Wr.rearrange("(c p) n -> p c n", p=P)).then_inc(w_in, 16)
            for l in range(3):
                sp.dma_start(gb[l], gnn_b[l].rearrange("(a n) -> a n", a=1).broadcast_to([P, D])).then_inc(w_in, 16)
            sp.dma_start(br_row[:, :], br.rearrange("(a n) -> a n", a=1).broadcast_to([P, NX])).then_inc(w_in, 16)
            sp.dma_start(b1col[:, :], mix_b1.rearrange("(c p) -> p c", p=P), allow_slow_non_contiguous=True).then_inc(w_in, 16)
            sp.wait_ge(wi_ready, 1)
            for m in range(2):
                sp.dma_start(bounds_d[m:m + 1, :].rearrange("m (s p) -> p m s", p=WSP), wi[0:WSP, m:m + 1, :], allow_slow_non_contiguous=True).then_inc(bounds_out, 16)
            sp.wait_ge(bounds_out, 32)
            sp.dma_start(spans[0:1, :], bounds_d[0:1, :]).then_inc(bounds_in, 16)
            sp.dma_start(cum[0:1, 1:NW + 1], bounds_d[1:2, :]).then_inc(bounds_in, 16)
            for c_sb, c_dram in ((fgcol, ffn_g), (fbcol, ffn_b), (fb1col, ffn_b1)):
                v = c_dram.rearrange("e (c p) -> p e c", p=P)
                for e in range(NX):
                    sp.dma_start(c_sb[:, e, :], v[:, e, :], allow_slow_non_contiguous=True).then_inc(w_in, 16)
            zr = zeros[:, 0:D].unsqueeze(1).broadcast_to([P, NBLK * BT // P, D])
            sp.dma_start(routed_in[0:SLOTS, :].rearrange("(a p) d -> p a d", p=P), zr).then_inc(zero_out, 16)
            zr = zeros[:, 0:D].unsqueeze(1).broadcast_to([P, (NBLK - LEAST) * BT // P, D])
            sp.dma_start(routed_out[LEAST * BT:SLOTS, :].rearrange("(a p) d -> p a d", p=P), zr).then_inc(zero_out, 16)

            def store_adj(t, s, before_):
                sp.wait_ge(a_ready, t + 1)
                sp.dma_start(adj[bass.ds(t, 1), :, :].rearrange("a p n -> p (a n)"), a16[:, s, :, :].rearrange("p h d -> p (h d)")).then_inc(a_out[s], 16)
            by_two(sp, store_adj)
            for s in range(RING):
                sp.wait_ge(a_out[s], 16 * (USES[s] + 1))
            sp.wait_ge(deg_added, NT + RING)

            for l in range(3):
                def load_adj(t, s, before_, first=False):
                    sp.wait_ge(acc_done, l * NT + t + (2 if first else 1))
                    half = NT // 2 * P
                    for lo, hi in ((0, half), (half, NT * P)):
                        sp.dma_start(a16[:, s, :, :].rearrange("p h d -> p (h d)")[:, lo:hi],
                                     adj[bass.ds(t, 1), :, lo:hi].rearrange("a p n -> p (a n)")).then_inc(a_in[s], 16)
                if l == 1:
                    sp.wait_ge(prod_ready, NT + 1)
                    sp.dma_start(wg[:, 0, :, :], gnn_W[2].rearrange("(c p) n -> p c n", p=P)).then_inc(wg_in, 16)
                if l == 2:
                    sp.wait_ge(lo_ready, 3 * NT)
                    sp.wait_ge(hi_ready, 3 * NT)
                    for raw, w_dram in ((raw_w1, mix_W1), (raw_w2, mix_W2)):
                        sp.dma_start(raw, w_dram.rearrange("(o p) c -> p o c", p=P)).then_inc(w2raw_in, 16)
                    for to, v in ((r1g, ln1_g), (r1b, ln1_b), (r2g, ln2_g), (r2b, ln2_b), (rb2, mix_b2)):
                        sp.dma_start(to, v.rearrange("(a n) -> a n", a=1).broadcast_to([P, D])).then_inc(w2_in, 16)

                load_adj(0, 0, 0, True)
                with sp.Fori(0, NT // 2) as i:
                    load_adj(2 * i + 1, 1, i)
                    load_adj(2 * i + 2, 0, i + 1)

            sp.wait_ge(slots_ready, 1)
            sp.wait_ge(zero_out, 32)
            for s in range(RING):
                sp.wait_ge(scat[s], 32 * USES[s])
            last = sp.value_load(blk_no[0:1, NX:NX + 1], min_val=NX, max_val=NBLK)

            def load_rows(b):
                sp.wait_ge(b_T, b + 1)
                sp.dma_start(xs, routed_in[bass.ds(b * BT, BT), :].rearrange("(a p) d -> p a d", p=P)).then_inc(xs_in, 16)

            def store_rows(b):
                sp.wait_ge(b_yc, b + 2)
                sp.dma_start(routed_out[bass.ds(b * BT, BT), :].rearrange("(a p) d -> p a d", p=P), ys).then_inc(b_out, 16)
            load_rows(0)
            with sp.Fori(0, last - 1) as b:
                load_rows(b + 1)
                store_rows(b)
            store_rows(last - 1)

            def store(t, s, rows_=P):
                sp.wait_ge(f_ready, t + 2)
                sp.dma_start(out[bass.ds(t * P, rows_), :], st[0:rows_, s, :]).then_inc(f_out[s], 16)
            with sp.Fori(0, NT // 2) as i:
                store(2 * i, 0)
                store(2 * i + 1, 1)
            store(NT - 1, 0, LAST)
            for s in range(RING):
                sp.wait_ge(f_out[s], 16 * (USES[s] + 1))

        @block.gpsimd
        def _(pool):
            c = Chain(pool, po)
            pool.iota(span_no[:, 0, :], [[P, SB]], base=1, channel_multiplier=1, allow_small_or_imprecise_dtypes=True)
            pool.iota(span_no[:, 1, :], [[-P, SB]], base=NS, channel_multiplier=-1, allow_small_or_imprecise_dtypes=True)
            pool.iota(w_no, [[1, NW]], base=0, channel_multiplier=0, allow_small_or_imprecise_dtypes=True)
            pool.iota(iota_lo, [[1, P]], base=0, channel_multiplier=0, allow_small_or_imprecise_dtypes=True)
            pool.iota(iota_w, [[1, 2 * HW_]], base=0, channel_multiplier=0, allow_small_or_imprecise_dtypes=True)
            pool.iota(w_base, [[2 * HW_, NW]], base=0, channel_multiplier=0, allow_small_or_imprecise_dtypes=True).then_inc(c_iota, 1)
            pool.memset(ident[:, :], 0.0)
            pool.memset(before[:, :], 1.0)
            pool.memset(ones[:, :], 1.0)
            pool.memset(valid[:, :], 1.0)
            pool.memset(halves[:, :], -0.5)
            c.link(pool.iota(dump[:, :], [[0, NT]], base=SLOTS, channel_multiplier=1, allow_small_or_imprecise_dtypes=True))
            pool.affine_select(out=ident[:, :], in_=ident[:, :], compare_op=ALU.not_equal, fill=1.0, base=0,
                               pattern=[[-1, P]], channel_multiplier=1)
            pool.affine_select(out=before[:, :], in_=before[:, :], compare_op=ALU.is_gt, fill=0.0, base=0,
                               pattern=[[1, P]], channel_multiplier=-1)
            pool.affine_select(out=valid[:, :], in_=valid[:, :], compare_op=ALU.is_ge, fill=0.0, base=N - 1,
                               pattern=[[-P, NT]], channel_multiplier=-1)
            pool.affine_select(out=dump[:, :], in_=dump[:, :], compare_op=ALU.is_ge, fill=0.0, base=-N,
                               pattern=[[P, NT]], channel_multiplier=1)
            pool.iota(desc8[:, :], [[-1, NX]], base=NX, channel_multiplier=0, allow_small_or_imprecise_dtypes=True)
            pool.memset(vaug[:, :, P:P + 1], 1.0).then_inc(c_mat, 1)

            def root_recip(to, of, n):
                return pool.tensor_tensor(to, of, halves[:, 0:n], ALU.pow)

            pool.wait_ge(mv_ready, 1)
            root_recip(rstd[:, :], mv[:, :, 1], NT).then_inc(sd_ready, 1)

            pool.wait_ge(key_ready, 1)
            pool.memset(deg_acc, 0.0).then_inc(deg_added, RING)

            def add(t, s, before_):
                pool.wait_ge(a_ready, t + 1)
                pool.wait_ge(deg_added, t + RING)
                pool.tensor_tensor(deg_acc, deg_acc, a16[:, s, :, :].rearrange("p h d -> p (h d)"), ALU.add).then_inc(deg_added, 1)
            by_two(pool, add)
            pool.wait_ge(degs, 1)
            root_recip(norm_src[:, :], deg[:, :], NT).then_inc(deg_sd, 1)

            with pool.Fori(0, NT) as t:
                pool.wait_ge(degs, t + 2)
                root_recip(col[:, 3:4], col[:, 2:3], 1).then_inc(deg_sd, 1)
            pool.wait_ge(lo_ready, 3 * NT)
            pool.wait_ge(hi_ready, 3 * NT)

            def root(n):
                pool.wait_ge(n_mv, n)
                root_recip(sd1[:, :], sd1[:, :], 1).then_inc(n_sd, 1)

            def scale_x1(t, x1):
                k = Chain(pool, pool_c, t)
                pool.wait_ge(n_xn, t + 1)
                k.link(pool.tensor_tensor(x1[:, :], x1[:, :], r1g, ALU.mult))
                pool.tensor_tensor(x1[:, :], x1[:, :], r1b, ALU.add).then_inc(n_x1, 1)

            def add_x(t):
                pool.wait_ge(xo_in, 16 * (t + 1))
                pool.wait_ge(acc_used, 2 * NT + t + 1 + RING)
                pool.wait_ge(n_out, t + 1)
                pool.tensor_tensor(xg, xo, grow, ALU.add).then_inc(xg_ready, 1)

            def again(t, rows_=P):
                pool.wait_ge(xg_ready, t)
                pool.sem_inc(pool_past, 1)
                pool.dma_start(xo[0:rows_, :], x[bass.ds(t * P, rows_), :]).then_inc(xo_in, 16)

            def tile(t, s, ahead, n, rows_=P):
                add_x(t)
                if ahead:
                    root(n)
                    scale_x1(t + 1, x1s[1 - s])
                    again(t + 1, rows_)
                root(n + ahead)
                root(n + ahead + 1)
            again(0)
            root(1)
            pool.wait_ge(w2_in, 16 * 5)
            scale_x1(0, x1s[0])
            with pool.Fori(0, NT // 2 - 1) as i:
                tile(2 * i, 0, 1, 6 * i + 2)
                tile(2 * i + 1, 1, 1, 6 * i + 5)
            tile(NT - 3, 0, 1, 3 * NT - 7)
            tile(NT - 2, 1, 1, 3 * NT - 4, LAST)
            tile(NT - 1, 0, 0, 3 * NT - 1)
            pool.wait_ge(mv_ready, 2)
            root_recip(rstd[:, :], mv[:, :, 1], NT).then_inc(sd_ready, 1)

            pool.wait_ge(slots_ready, 1)
            pool.wait_ge(zero_out, 32)

            def weights(e, s):
                if not (isinstance(e, int) and e < RING):
                    pool.wait_ge(b_y, pool.value_load(blk_no[0:1, bass.ds(e - 1, 1)], min_val=0, max_val=NBLK) + 1)
                pool.dma_start(w_up[s], ffn_W1[bass.ds(e, 1), :, :].rearrange("e (c p) n -> p (e c) n", p=P)).then_inc(wx_in[s], 16)
                pool.dma_start(w_dn[s], ffn_W2[bass.ds(e, 1), :, :].rearrange("e (m p) n -> p (e m) n", p=P)).then_inc(wx_in[s], 16)
                pool.dma_start(fb2row[0:1, s, :], ffn_b2[bass.ds(e, 1), :]).then_inc(wx_in[s], 16)

            weights(0, 0)
            weights(1, 1)

            def scatter(t, s, before_):
                pool.wait_ge(r_xs, t + 1)
                pool.sem_inc(pool_past, 1)
                for k in range(2):
                    pool.indirect_dma_start(
                        out=routed_in, out_offset=bass.IndirectOffsetOnAxis(ap=sidx[:, s, k:k + 1].bitcast(U32), axis=0),
                        in_=st[:, s, :], in_offset=None).then_inc(scat[s], 16)
            by_two(pool, scatter)

            with pool.Fori(1, NX // 2) as i:
                weights(2 * i, 0)
                weights(2 * i + 1, 1)

            total = pool.value_load(blk_no[0:1, NX:NX + 1], min_val=NX, max_val=NBLK)
            pool.wait_ge(b_out, total * 16 + 16)
            pool.sem_inc(pool_past, 1)

            def fetch(t, s, before_):
                pool.wait_ge(f_idx, t + 1)
                pool.sem_inc(pool_past, 1)
                for k, to in ((0, hs), (1, hT)):
                    pool.indirect_dma_start(
                        out=to[:, s, :], out_offset=None, in_=routed_out,
                        in_offset=bass.IndirectOffsetOnAxis(ap=sidx[:, s, k:k + 1].bitcast(U32), axis=0)
                    ).then_inc(f_got[s], 16)
            by_two(pool, fetch)

        @block.tensor
        def _(pe):
            pe.wait_ge(c_mat, 1)
            pe.wait_ge(c_vec, 1)
            for sem_ in oh_free:
                pe.sem_inc(sem_, 1)
            pe.sem_inc(acc_done, RING)
            pe.sem_inc(r_hsT, 1)
            pe.sem_inc(r_row, 1)
            pe.sem_inc(h_T, 1)
            pe.sem_inc(h_p, 1)
            pe.sem_inc(b_T, 1)
            pe.sem_inc(b_y, 1)
            pe.sem_inc(n_y, 1)
            pe.sem_inc(m_KV, 1)
            pe.wait_ge(edges_f, 2)
            n = 0
            for v in (dst_f, src_f):
                for b0 in range(0, CB, 4):
                    if n >= 2:
                        pe.wait_ge(edges_c, n - 1)
                    ps = (psA, psB)[n % 2]
                    for b in range(b0, min(b0 + 4, CB)):
                        mm_ = pe.transpose(ps[:, (b - b0) * P:(b - b0 + 1) * P], v[:, b * P:(b + 1) * P], ident[:, :])
                    mm_.then_inc(edgesT, 1)
                    n += 1
            pe.wait_ge(wraw_in, 16)
            for i, (raw, _, c_, o0, nb) in enumerate(turned):
                pe.wait_ge((edges_c if i < 2 else wT_out), (n - 1 + i if i < 2 else i - 1))
                for o in range(nb):
                    mm_ = pe.transpose((psA, psB)[i % 2][:, o * P:(o + 1) * P], raw[:, o0 + o, c_ * P:(c_ + 1) * P], ident[:, :])
                mm_.then_inc(wT, 1)
            pe.wait_ge(far_ready, 1)
            for k in range(2):
                for s in range(WS):
                    mm_ = pe.transpose((psC, psH)[k][0:WSP, s * P:(s + 1) * P], far[:, k, s * WSP:(s + 1) * WSP], ident[:, :])
            mm_.then_inc(farT, 1)
            pe.wait_ge(cum_ready, 1)
            pe.wait_ge(wT_out, len(turned))
            zb = zeros[:, :].bitcast(F16)

            def turn(n):
                pe.wait_ge(h_ready, n + 1)
                pe.wait_ge(h_Tc, n + 1)
                for c_ in range(HALVES):
                    mm_ = pe.transpose(psT[0][:, c_ * P:(c_ + 1) * P], hrow[:, c_ * P:(c_ + 1) * P], ident[:, :])
                mm_.then_inc(h_T, 1)

            def project(l, n):
                pe.wait_ge(h_Tc, n + 2)
                pe.wait_ge(prod_ready, n + 1)
                for c_ in range(HALVES):
                    mm_ = pe.matmul(psT[0][:, 0:D], hrowT[:, c_ * P:(c_ + 1) * P], wg[:, l % 2, c_, :], start=(c_ == 0), stop=(c_ == HALVES - 1))
                mm_.then_inc(h_p, 1)

            def keys_values(t):
                pe.wait_ge(m_f, t + 1)
                pe.wait_ge(m_v, t + 1)
                for ps, o in ((psA, D), (psB, 2 * D)):
                    for c_ in range(HALVES):
                        mm_ = pe.matmul(ps[:, 0:D], hrowT[:, c_ * P:(c_ + 1) * P], wqkvT[:, c_, o:o + D], start=(c_ == 0), stop=(c_ == HALVES - 1))
                mm_.then_inc(m_P, 1)

            def key_value_sums(t, rows_=P):
                pe.wait_ge(m_f, t + 2)
                pe.wait_ge(m_v, t + 2)
                for c_ in range(HALVES):
                    mm_ = pe.matmul(psKV[:, c_ * (P + 1):(c_ + 1) * (P + 1)], mfeat[0:rows_, c_ * P:(c_ + 1) * P],
                                    vaug[0:rows_, c_, :], start=False, stop=False)
                mm_.then_inc(m_KV, 1)

            def turn_row(t):
                pe.wait_ge(m_row, t + 1)
                for c_ in range(HALVES):
                    mm_ = pe.transpose(psA[:, c_ * P:(c_ + 1) * P], mrow[:, c_ * P:(c_ + 1) * P], ident[:, :])
                mm_.then_inc(m_T, 1)

            def queries(t):
                pe.wait_ge(m_xT, t + 1)
                for o in range(HALVES):
                    for c_ in range(HALVES):
                        mm_ = pe.matmul(psB[:, o * P:(o + 1) * P], wqkvT[:, c_, o * P:(o + 1) * P],
                                        mT[:, c_ * P:(c_ + 1) * P], start=(c_ == 0), stop=(c_ == HALVES - 1))
                mm_.then_inc(m_P, 1)

            def attend(t):
                pe.wait_ge(m_f, NT + t + 2)
                for o in range(HALVES):
                    mm_ = pe.matmul(psC[:, o * (P + HPB):(o + 1) * (P + HPB)], mfeat[:, o * P:(o + 1) * P], kvblk[:, o, :], start=True, stop=True)
                mm_.then_inc(n_t, 1)

            def turn_x1(t, x1):
                pe.wait_ge(n_x1, t + 1)
                for c_ in range(HALVES):
                    mm_ = pe.transpose(psA[:, c_ * P:(c_ + 1) * P], x1[:, c_ * P:(c_ + 1) * P], ident[:, :])
                mm_.then_inc(n_T, 1)

            def hidden(t):
                pe.wait_ge(n_x1T, t + 1)
                for o in range(HALVES):
                    for c_ in range(HALVES):
                        mm_ = pe.matmul(psA[:, D + o * P:D + (o + 1) * P], w1T[:, c_, o * P:(o + 1) * P],
                                        mT[:, c_ * P:(c_ + 1) * P], start=(c_ == 0), stop=(c_ == HALVES - 1))
                mm_.then_inc(n_h, 1)

            def mixed(t):
                pe.wait_ge(n_g, 2 * t + 2)
                pe.wait_ge(n_out, t + 1)
                for c_ in range(HALVES):
                    mm_ = pe.matmul(psY0[:, 0:D], mgelu[:, c_ * P:(c_ + 1) * P], w2T[:, c_, :], start=(c_ == 0), stop=(c_ == HALVES - 1))
                mm_.then_inc(n_y, 1)

            def turn_u(t):
                pe.wait_ge(r_hs, t + 1)
                pe.wait_ge(r_hT, t + 1)
                for c_ in range(HALVES):
                    mm_ = pe.transpose(psT[0][:, c_ * P:(c_ + 1) * P], urow[:, c_ * P:(c_ + 1) * P], ident[:, :])
                mm_.then_inc(r_hsT, 1)

            def logit(t):
                pe.wait_ge(r_hT, t + 2)
                for c_ in range(HALVES):
                    mm_ = pe.matmul(psL[:, bass.ds(t * NX, NX)], urowT[:, c_ * P:(c_ + 1) * P], wr[:, c_, :], start=(c_ == 0), stop=(c_ == HALVES - 1))
                mm_.then_inc(r_row, 1)

            pe.wait_ge(w_in, 16 * (3 + 3 + 2 + 3 * NX))

            def build(t, s, before_, rows_=P):
                lo = pe.value_load(cum[0:1, bass.ds(t * WPT, 1)], min_val=0, max_val=NW * NS)
                for i in range(WPT):
                    if i == 1:
                        turn(t)
                    if i == 3:
                        project(0, t)
                        keys_values(t)
                    hi = pe.value_load(cum[0:1, bass.ds(t * WPT + i + 1, 1)], min_val=0, max_val=NW * NS)
                    pe.wait_ge(win_free[i % 2], t * (WPT // 2) + i // 2 + 1)
                    for half in windows[i % 2]:
                        pe.matmul(half[:, 0:HW_], zb[:, 0:P], zb[:, 0:HW_], start=True, stop=False)
                    with pe.Fori(lo, hi) as p:
                        for j in range(SC):
                            pe.wait_ge(oh_ready[j], p + 1)
                            for h, half in enumerate(windows[i % 2]):
                                mm_ = pe.matmul(half[:, 0:HW_], onehot_lo[:, j, :], onehot_w[:, j, h * HW_:(h + 1) * HW_], start=False, stop=False)
                            mm_.then_inc(oh_free[j], 1)
                    for half in windows[i % 2]:
                        mm_ = pe.matmul(half[:, 0:HW_], zb[:, 0:P], zb[:, 0:HW_], start=False, stop=True)
                    mm_.then_inc(win_ready[i % 2], 1)
                    lo = hi
                key_value_sums(t, rows_)
            pe.matmul(psKV, zeros[:, 0:P], zeros[:, 0:HALVES * (P + 1)], start=True, stop=False)
            with pe.Fori(0, NT // 2) as i:
                build(2 * i, 0, i)
                build(2 * i + 1, 1, i)
            build(NT - 1, 0, NT // 2, LAST)
            pe.matmul(psKV, zeros[:, 0:P], zeros[:, 0:HALVES * (P + 1)], start=False, stop=True).then_inc(m_KV, 1)

            FIRST = "first"
            for l in range(3):
                pe.wait_ge(g_row, 2 * l + 1)
                pe.transpose(psT[0][0:1, 0:P], col[:, 0:1], ident[:, :]).then_inc(g_T, 1)
                pe.wait_ge(g_row, 2 * l + 2)
                pe.matmul(psT[0][:, 0:1], ones[0:1, :], col[0:1, 1:2], start=True, stop=True).then_inc(g_T, 1)
                if l == 1:
                    pe.wait_ge(wg_in, 16)
                if l == 2:
                    pe.wait_ge(w2raw_in, 32)
                    for i, (raw, _, c_, o0, nb) in enumerate(turned2):
                        if i >= 2:
                            pe.wait_ge(wmT_out, i - 1)
                        for o in range(nb):
                            mm_ = pe.transpose((psA, psB)[i % 2][:, o * P:(o + 1) * P], raw[:, o0 + o, c_ * P:(c_ + 1) * P], ident[:, :])
                        mm_.then_inc(wmT, 1)
                    pe.wait_ge(wmT_out, len(turned2))

                def part(t, s, g):
                    edges = [NT * q // 8 for q in range(9)]
                    for h in range(edges[g], edges[g + 1]):
                        if t is FIRST:
                            pe.wait_ge(hi_ready, l * NT + h + 1)
                            pe.wait_ge(lo_ready, l * NT + h + 1)
                        wide_ = D + 1 if l == 0 else D
                        def hi_part():
                            return pe.matmul(acc[s][:, 0:wide_], a16[:, s, h, :], x_hi[:, h, 0:wide_], start=(h == 0), stop=(h == NT - 1))
                        def lo_part():
                            return pe.matmul(acc[s][:, 0:D], a16[:, s, h, :], x_lo[:, h, :], start=False, stop=False)
                        if h < NT - 1:
                            hi_part()
                            lo_part()
                        else:
                            lo_part()
                            hi_part().then_inc(acc_done, 1)

                def tile(t, s, before_, prev=None, u=None):
                    n = 0 if t is FIRST else t
                    pe.wait_ge(a_in[s], 32 * (l * USES[s] + before_ + 1))
                    pe.wait_ge(acc_used, l * NT + n + (2 if t is FIRST else 1))
                    for g in range(8):
                        if l < 2 and prev is not None:
                            if g == 2:
                                turn((l + 1) * NT + prev)
                            if g == 5:
                                project(l + 1, (l + 1) * NT + prev)
                        if l == 2:
                            if g == 0:
                                turn_row(n)
                            if g == 1:
                                queries(n)
                            if g == 2 and prev is not None:
                                turn_x1(prev, x1s[1 - s])
                            if g == 3 and prev is not None:
                                hidden(prev)
                            if g == 5 and u is not None:
                                turn_u(u)
                            if g == 6 and prev is not None:
                                mixed(prev)
                            if g == 7 and u is not None:
                                logit(u)
                            if g == 4:
                                attend(n)
                        part(t, s, g)
                tile(FIRST, 0, 0)
                tile(1, 1, 0, 0)
                tile(2, 0, 1, 1, 0)
                with pe.Fori(1, NT // 2) as i:
                    tile(2 * i + 1, 1, i, 2 * i, 2 * i - 1)
                    tile(2 * i + 2, 0, i + 1, 2 * i + 1, 2 * i)
                if l < 2:
                    turn((l + 1) * NT + NT - 1)
                    project(l + 1, (l + 1) * NT + NT - 1)
                if l == 2:
                    turn_x1(NT - 1, x1s[0])
                    hidden(NT - 1)
                    turn_u(NT - 2)
                    mixed(NT - 1)
                    logit(NT - 2)
                    turn_u(NT - 1)
                    logit(NT - 1)


            pe.wait_ge(mask_ready, 1)
            pe.matmul(psA[:, 0:NE], before[:, :], pick, start=True, stop=True)
            pe.matmul(psB[:, 0:NE], ones[:, :], pick, start=True, stop=True).then_inc(rank_mm, 1)

            psX = bank[1]
            ups = [bank[4 + i] for i in range(4)]
            psY = [bank[2], bank[3]]
            pe.wait_ge(slots_ready, 1)

            def up(b, m, s):
                pe.wait_ge(b_h, b * MH + m + 1)
                for c_ in range(HALVES):
                    if m == 0:
                        pe.wait_ge(b_xT, HALVES * b + c_ + 2)
                    mm_ = pe.matmul(ups[m % 4][:, 0:BT], w_up[s][:, c_, m * P:(m + 1) * P], xeT[:, c_, :],
                                    start=(c_ == 0), stop=(c_ == HALVES - 1))
                mm_.then_inc(b_up, 1)

            def down(b, m, s):
                pe.wait_ge(b_h, b * MH + m + 1 + 4)
                for a in range(2):
                    mm_ = pe.matmul(psY[a][:, 0:D], hidT[:, m, a * P:(a + 1) * P], w_dn[s][:, m, :], start=False, stop=(m == MH - 1))
                return mm_

            def expert(e, s, i):
                lo = pe.value_load(blk_no[0:1, bass.ds(e, 1)], min_val=0, max_val=NBLK)
                hi = pe.value_load(blk_no[0:1, bass.ds(e + 1, 1)], min_val=0, max_val=NBLK)
                pe.wait_ge(wx_in[s], 48 * (i + 1))
                pe.sem_inc(pe_past, 1)
                with pe.Fori(lo, hi) as b:
                    pe.wait_ge(xs_in, 16 * (b + 1))
                    pe.wait_ge(b_xT, HALVES * b + 1)
                    for c_ in range(HALVES):
                        for a in range(2):
                            mm_ = pe.transpose(psX[:, c_ * BT + a * P:c_ * BT + (a + 1) * P], xs[:, a, c_ * P:(c_ + 1) * P], ident[:, :])
                    mm_.then_inc(b_T, 1)
                    pe.wait_ge(b_yc, b + 1)
                    for a in range(2):
                        pe.matmul(psY[a][:, 0:D], ones[0:1, :], fb2row[0:1, s, :], start=True, stop=False)
                    up(b, 0, s)
                    for m in range(1, MH):
                        up(b, m, s)
                        down(b, m - 1, s)
                    down(b, MH - 1, s).then_inc(b_y, 1)
            with pe.Fori(0, NX // 2) as i:
                expert(2 * i, 0, i)
                expert(2 * i + 1, 1, i)

        @block.scalar
        def _(act):
            act.sem_inc(h_Tc, 1)
            act.sem_inc(prod_ready, 1)
            act.sem_inc(r_hT, 1)
            act.sem_inc(m_v, 1)
            act.sem_inc(m_exp, 1)
            act.sem_inc(b_h, 4)
            for sem_ in win_free:
                act.sem_inc(sem_, 1)
            act.dma_start(raw_qkv, Wqkv.rearrange("(o p) c -> p o c", p=P)).then_inc(wraw_in, 16)
            n = 0
            for v in (key, src_t):
                for b0 in range(0, CB, 4):
                    w = min(4, CB - b0) * P
                    act.wait_ge(edgesT, n + 1)
                    act.activation(v[:, b0 * P:b0 * P + w], (psA, psB)[n % 2][:, 0:w], ACT.Copy).then_inc(edges_c, 1)
                    n += 1
            for i, (_, to, c_, o0, nb) in enumerate(turned):
                act.wait_ge(wT, i + 1)
                act.activation(to[:, c_, o0 * P:(o0 + nb) * P], (psA, psB)[i % 2][:, 0:nb * P], ACT.Copy).then_inc(wT_out, 1)

            def copy_turned(n):
                act.wait_ge(h_T, n + 2)
                act.wait_ge(h_p, n + 1)
                act.activation(hrowT[:, :], psT[0][:, 0:D], ACT.Copy).then_inc(h_Tc, 1)

            def copy_product(t, n):
                act.wait_ge(h_p, n + 2)
                act.activation(prod[:, bass.ds(t, 1), :], psT[0][:, 0:D].unsqueeze(1), ACT.Copy).then_inc(prod_ready, 1)

            act.wait_ge(cum_ready, 1)
            act.wait_ge(xn_ready, NT)

            def build(t, s, before_):
                act.wait_ge(h_T, t + 1)
                act.activation(hrow[:, :], nodes[:, bass.ds(t, 1), :], ACT.Copy).then_inc(h_ready, 1)
                act.wait_ge(a_out[s], 16 * (before_ + 1))
                act.wait_ge(deg_added, t + 1)
                for i in range(WPT):
                    if i == 2:
                        copy_turned(t)
                    if i == 4:
                        copy_product(t, t)
                        act.wait_ge(m_P, t + 1)
                        act.wait_ge(m_KV, t + 1)
                        act.activation(vaug[:, :, 0:P], psB[:, 0:D].rearrange("p (c n) -> p c n", c=HALVES), ACT.Copy).then_inc(m_v, 1)
                    if i == 5:
                        act.wait_ge(m_min, t + 1)
                        act.activation(mexp[:, :], melu[:, :], ACT.Exp).then_inc(m_exp, 1)
                    act.wait_ge(win_ready[i % 2], t * (WPT // 2) + i // 2 + 1)
                    for h, half in enumerate(windows[i % 2]):
                        d0 = i * DW + h * DW // 2
                        ins = act.activation(a16[:, s, :, d0:d0 + DW // 2], half[:, 0:HW_].rearrange("p (d n) -> p n d", n=NT),
                                             ACT.Copy, scale=0.25)
                    ins.then_inc(win_free[i % 2], 1)
                act.sem_inc(act_past, 1)
                act.wait_ge(win_free[1], t * (WPT // 2) + WPT // 2 + 1)
                act.wait_ge(win_free[0], t * (WPT // 2) + WPT // 2 + 1)
                act.sem_inc(a_ready, 1)
            by_two(act, build)

            def queries(t):
                if not (isinstance(t, int) and t == 0):
                    act.wait_ge(m_T, t)
                act.activation(mrow[:, :], nodes[:, bass.ds(t, 1), :], ACT.Copy).then_inc(m_row, 1)
                act.wait_ge(m_T, t + 1)
                act.activation(mT[:, :], psA[:, 0:D], ACT.Copy).then_inc(m_xT, 1)

            def queries_exp(t):
                act.wait_ge(m_min, NT + t + 1)
                act.activation(mexp[:, :], melu[:, :], ACT.Exp).then_inc(m_exp, 1)

            def copy_x1(t, asked):
                act.wait_ge(n_T, t + 1)
                act.wait_ge(m_P, NT + asked)
                act.activation(mT[:, :], psA[:, 0:D], ACT.Copy).then_inc(n_x1T, 1)

            def hidden(t):
                act.wait_ge(n_h, t + 1)
                act.wait_ge(n_y, t + 1)
                for o in range(HALVES):
                    act.activation(mgelu[:, o * P:(o + 1) * P], psA[:, D + o * P:D + (o + 1) * P], ACT.Gelu, bias=b1col[:, o:o + 1]).then_inc(n_g, 1)

            for l in range(3):
                act.wait_ge(nss_ready, l + 1)
                def split(t):
                    act.activation(x_hi[:, bass.ds(t, 1), 0:D], prod[:, bass.ds(t, 1), :], ACT.Copy, scale=nss[:, bass.ds(t, 1)]).then_inc(hi_ready, 1)
                with act.Fori(0, NT) as t:
                    split(t)
                if l == 2:
                    for i, (_, to, c_, o0, nb) in enumerate(turned2):
                        act.wait_ge(wmT, i + 1)
                        act.activation(to[:, c_, o0 * P:(o0 + nb) * P], (psA, psB)[i % 2][:, 0:nb * P], ACT.Copy).then_inc(wmT_out, 1)

                def copy_u(t):
                    act.wait_ge(r_hsT, t + 2)
                    act.wait_ge(r_row, t + 1)
                    act.activation(urowT[:, :], psT[0][:, 0:D], ACT.Copy).then_inc(r_hT, 1)

                def tile(t, prev, u):
                    if l == 2:
                        queries(t)
                        if prev is not None:
                            copy_x1(prev, prev + 2)
                        queries_exp(t)
                    if prev is None:
                        return
                    if l == 2:
                        hidden(prev)
                        if u is not None:
                            copy_u(u)
                    else:
                        copy_turned((l + 1) * NT + prev)
                        copy_product(prev, (l + 1) * NT + prev)
                tile(0, None, None)
                tile(1, 0, None)
                with act.Fori(2, NT) as t:
                    tile(t, t - 1, t - 2)
                if l == 2:
                    copy_x1(NT - 1, NT)
                    hidden(NT - 1)
                    copy_u(NT - 2)
                    copy_u(NT - 1)
                else:
                    copy_turned((l + 1) * NT + NT - 1)
                    copy_product(NT - 1, (l + 1) * NT + NT - 1)

            act.wait_ge(fm, 1)
            act.activation(gate2[:, :], gate1[:, :], ACT.Exp).then_inc(fe, 1)

            act.wait_ge(slots_ready, 1)
            with act.Fori(0, NX) as e:
                lo = act.value_load(blk_no[0:1, bass.ds(e, 1)], min_val=0, max_val=NBLK)
                hi = act.value_load(blk_no[0:1, bass.ds(e + 1, 1)], min_val=0, max_val=NBLK)
                with act.Fori(lo, hi) as b:
                    act.activation(spare[0:1, 0:1], ident[0:1, 0:1], ACT.Gelu).then_inc(act_past, 1)
                    act.wait_ge(b_y, b + 1)
                    for m in range(MH):
                        act.wait_ge(b_up, b * MH + m + 1)
                        act.activation(hidT[:, m, :], bank[4 + m % 4][:, 0:BT], ACT.Gelu,
                                       bias=fb1col[:, bass.ds(e, 1), m:m + 1]).then_inc(b_h, 1)

        @block.vector
        def _(dve):
            c = Chain(dve, vo)

            def copy(to, of):
                return dve.tensor_scalar(to, of, 1.0, None, ALU.mult)

            dve.sem_inc(acc_used, RING)
            dve.sem_inc(m_f, 1)
            dve.sem_inc(n_out, 1)
            dve.sem_inc(b_xT, 1)
            dve.sem_inc(b_yc, 1)
            dve.sem_inc(f_ready, 1)
            dve.memset(dst_i, -1).then_inc(raw_clear, 1)
            dve.memset(src_i, -1).then_inc(raw_clear, 1)
            dve.memset(span_rows, -1).then_inc(sp_clear, 1)
            dve.memset(zeros[:, :], 0.0)
            dve.memset(cum[:, 0:1], 0)
            dve.memset(cnt_f[:, 3, :], 1.0)
            dve.memset(far, 0.0)
            dve.memset(kvblk[:, :, :], 0.0)
            c.link(dve.memset(nodes[:, NT - 1, :], 0.0))
            dve.sem_inc(c_vec, 1)
            dve.wait_ge(dst_in, 48)
            dve.tensor_copy(dst_f, dst_i).then_inc(edges_f, 1)
            dve.wait_ge(src_in, 48)
            dve.tensor_copy(src_f, src_i).then_inc(edges_f, 1)
            dve.wait_ge(sp_in, 48)
            dve.tensor_reduce(mm[:, 0, :], span_rows, AX_X, ALU.min)
            c.link(dve.tensor_reduce(mm[:, 1, :], span_rows, AX_X, ALU.max))
            c.link(dve.tensor_scalar(mm[:, :, :], mm[:, :, :], DW.bit_length() - 1, None, ALU.arith_shift_right))
            c.link(dve.tensor_copy(mmf[:, :, :], mm[:, :, :]))
            dve.wait_ge(c_iota, 1)
            dve.wait_ge(c_mat, 1)
            for j in range(SB):
                c.link(dve.tensor_scalar(mask, w_no, mmf[:, 0, j:j + 1], None, ALU.is_ge))
                c.link(dve.scalar_tensor_tensor(out=mask, in0=w_no, scalar=mmf[:, 1, j:j + 1], in1=mask, op0=ALU.is_le, op1=ALU.mult))
                for k in range(2):
                    ins = dve.scalar_tensor_tensor(out=far[:, k, :], in0=mask, scalar=span_no[:, k, j:j + 1], in1=far[:, k, :],
                                                   op0=ALU.mult, op1=ALU.max)
                c.link(ins)
            dve.sem_inc(far_ready, 1)
            dve.wait_ge(edges_c, 2 * -(-CB // 4))
            c.link(dve.tensor_scalar(hi_f.bitcast(I32), src_t, 7, None, ALU.arith_shift_right))
            c.link(dve.tensor_scalar(src_t, src_t, P - 1, None, ALU.bitwise_and))
            dve.tensor_copy(sl, src_t)
            c.link(dve.scalar_tensor_tensor(out=key, in0=key, scalar=float(NT), in1=hi_f.bitcast(I32), op0=ALU.mult, op1=ALU.add))
            dve.sem_inc(key_ready, 1)
            dve.wait_ge(farT, 1)
            q = slice(0, WSP)
            for k, ps in enumerate((psC, psH)):
                ins = dve.tensor_reduce(wl[q, k, :], ps[q, 0:WS * P].rearrange("p (s n) -> p s n", s=WS), AX_X, ALU.max)
            c.link(ins)
            c.link(dve.tensor_scalar(wl[q, 0, :], wl[q, 0, :], 1.0, None, ALU.max))
            c.link(dve.tensor_scalar(wl[q, 1, :], wl[q, 1, :], -1.0, float(NS), ALU.mult, ALU.add))
            c.link(dve.tensor_scalar(mmf[q, 0, 0:WS], wl[q, 0, :], -1.0, None, ALU.add))
            c.link(dve.tensor_tensor(wl[q, 1, :], wl[q, 1, :], mmf[q, 0, 0:WS], ALU.min))
            c.link(dve.tensor_copy(wi[q, 0, :], wl[q, 1, :]))
            c.link(dve.tensor_copy(wi[q, 1, :], wl[q, 0, :]))
            dve.sem_inc(wi_ready, 1)

            def stats(l, src_of, order):
                with dve.Fori(0, NT) as t:
                    k = Chain(dve, order, (l * NT + t) * 3)
                    k.link(dve.bn_stats(st6[:, :], src_of(t)), dve_past)
                    k.link(dve.bn_aggr(mv1[:, :], st6[:, :]))
                    k.link(copy(mv[:, bass.ds(t, 1), :], mv1[:, :].unsqueeze(1)), dve_past)
                c.link(dve.tensor_scalar(mv[:, :, 1], mv[:, :, 1], LN_EPS, None, ALU.add))
                dve.sem_inc(mv_ready, 1)

            dve.wait_ge(x_in, 32)
            stats(0, lambda t: nodes[:, bass.ds(t, 1), :], r_vo)
            dve.wait_ge(bounds_in, 32)
            lo_r, hi_r = spans[0:1, :], cum[0:1, 1:NW + 1]
            c.link(dve.tensor_tensor(cnt_f[0:1, 0, :], hi_r, lo_r, ALU.subtract))
            c.link(dve.tensor_tensor_scan(cnt_f[0:1, 1, :], cnt_f[0:1, 3, :], cnt_f[0:1, 0, :], 0.0, ALU.mult, ALU.add))
            c.link(dve.scalar_tensor_tensor(out=spans[0:1, :], in0=cnt_f[0:1, 0, :], scalar=float(SPAN_MOD), in1=lo_r, op0=ALU.mult, op1=ALU.add))
            c.link(dve.tensor_copy(hi_r, cnt_f[0:1, 1, :]))
            dve.sem_inc(cum_ready, 1)
            dve.wait_ge(sd_ready, 1)
            with dve.Fori(0, NT) as t:
                dve.tensor_scalar(nodes[:, bass.ds(t, 1), :], nodes[:, bass.ds(t, 1), :], mv[:, bass.ds(t, 1), 0:1],
                                  rstd[:, bass.ds(t, 1)], ALU.subtract, ALU.mult).then_inc(xn_ready, 1)

            def largest(t, n):
                dve.wait_ge(prod_ready, n + 2)
                dve.tensor_reduce(ymax[:, 0, bass.ds(t, 1)], prod[:, bass.ds(t, 1), :], AX_X, ALU.max)
                dve.tensor_reduce(ymax[:, 1, bass.ds(t, 1)], prod[:, bass.ds(t, 1), :], AX_X, ALU.min).then_inc(max_done, 1)

            def elu_min(ps, n):
                dve.wait_ge(m_P, n + 1)
                dve.wait_ge(m_exp, n + 1)
                dve.tensor_scalar(melu[:, :], ps[:, 0:D], 0.0, None, ALU.min).then_inc(m_min, 1)

            def elu_sum(ps, n):
                dve.wait_ge(m_exp, n + 2)
                dve.scalar_tensor_tensor(out=mfeat[:, :], in0=ps[:, 0:D], scalar=0.0, in1=mexp[:, :],
                                         op0=ALU.max, op1=ALU.add).then_inc(m_f, 1)

            def build(t, s, before_):
                lo = dve.value_load(cum[0:1, bass.ds(t * WPT, 1)], min_val=0, max_val=NW * NS)
                for i in range(WPT):
                    if i == 4:
                        elu_min(psA, t)
                    if i == 7:
                        dve.wait_ge(m_KV, t + 1)
                        elu_sum(psA, t)
                    w = t * WPT + i
                    both = dve.value_load(spans[0:1, bass.ds(w, 1)], min_val=SPAN_MOD, max_val=NS * SPAN_MOD + NS)
                    hi = dve.snap(lo + both // SPAN_MOD)
                    off = dve.snap(both % SPAN_MOD - lo)
                    with dve.Fori(lo, hi) as p:
                        q_ = nc.s_assert_within(dve.snap(p + off), 0, NS - 1,
                                                skip_runtime_bounds_check_because="a window's spans, first to last")
                        for j in range(SC):
                            dve.wait_ge(oh_free[j], p + 1)
                            dve.tensor_scalar(onehot_lo[:, j, :], iota_lo, sl[:, bass.ds(q_ * SC + j, 1)], None, ALU.is_equal)
                            dve.tensor_scalar(onehot_w[:, j, :], iota_w, w_base[:, bass.ds(w, 1)], key[:, bass.ds(q_ * SC + j, 1)],
                                              ALU.add, ALU.is_equal).then_inc(oh_ready[j], 1)
                    lo = hi
                largest(t, t)
            by_two(dve, build)
            dve.wait_ge(deg_added, NT + RING)
            c.link(dve.tensor_reduce(deg[:, :], deg_acc.rearrange("p (t n) -> p t n", t=NT), AX_X, ALU.add))
            c.link(dve.tensor_scalar(deg[:, :], deg[:, :], 4.0, 1.0, ALU.mult, ALU.max))
            dve.sem_inc(degs, 1)
            dve.wait_ge(deg_sd, 1)
            total = dve.value_load(cum[0:1, NW:NW + 1], min_val=1, max_val=NW * NS)
            for j in range(SC):
                dve.wait_ge(oh_free[j], total + 1)
            dve.sem_inc(dve_past, 1)
            c.link(dve.memset(x_hi[:, :, D:D + 1], 4.0))

            def normalise(k, v, n):
                k.link(dve.bn_stats(st6[:, :], v), dve_past)
                k.link(dve.bn_aggr(mv1[:, :], st6[:, :]))
                dve.tensor_scalar(sd1[:, :], mv1[:, 1:2], LN_EPS, None, ALU.add).then_inc(n_mv, 1)
                dve.wait_ge(n_sd, n)
                return dve.tensor_scalar(v, v, mv1[:, 0:1], sd1[:, 0:1], ALU.subtract, ALU.mult)

            K1, K2 = 6, 7

            def attended(t, x1, start, n):
                k = Chain(dve, n_vo, start)
                dve.wait_ge(n_t, t + 1)
                pv = psC[:, 0:HALVES * (P + HPB)].rearrange("p (c n) -> p c n", c=HALVES)
                k.link(dve.tensor_scalar(z[:, :, :], pv[:, :, P:P + HPB], ATTN_EPS, None, ALU.add))
                k.link(dve.reciprocal(z[:, :, :], z[:, :, :]))
                k.link(dve.tensor_tensor(x1[:, :].rearrange("p (c h n) -> p c h n", c=HALVES, h=HPB),
                                         pv[:, :, 0:P].rearrange("p c (h n) -> p c h n", h=HPB),
                                         z[:, :, :].unsqueeze(3).broadcast_to([P, HALVES, HPB, HD]), ALU.mult))
                k.link(dve.tensor_tensor(x1[:, :].unsqueeze(1), x1[:, :].unsqueeze(1), nodes[:, bass.ds(t, 1), :], ALU.add), dve_past)
                normalise(k, x1[:, :], n).then_inc(n_xn, 1)
                dve.wait_ge(n_xn, t + 1)
                assert k.n == K1

            def mixed(t, x1, start, n):
                k = Chain(dve, n_vo, start)
                dve.wait_ge(n_y, t + 2)
                dve.wait_ge(n_x1, t + 1)
                k.link(dve.tensor_tensor(tmp[:, :], psY0[:, 0:D], rb2, ALU.add))
                k.link(dve.tensor_tensor(tmp[:, :], tmp[:, :], x1[:, :], ALU.add), dve_past)
                k.link(normalise(k, tmp[:, :], n))
                k.link(dve.tensor_tensor(tmp[:, :], tmp[:, :], r2g, ALU.mult))
                k.link(dve.tensor_tensor(tmp[:, :], tmp[:, :], r2b, ALU.add))
                assert k.n == K2
                dve.wait_ge(xg_ready, t + 1)
                dve.tensor_tensor(nodes[:, bass.ds(t, 1), :], tmp[:, :].unsqueeze(1), xg[:, :].unsqueeze(1), ALU.add).then_inc(n_out, 1)

            def scale_of(l):
                dve.wait_ge(max_done, (l + 1) * NT)
                c.link(dve.tensor_scalar(ymax[:, 1, :], ymax[:, 1, :], -1.0, None, ALU.mult))
                c.link(dve.tensor_reduce(col[:, 0:1], ymax[:, :, :].rearrange("p k t -> p (k t)"), AX_X, ALU.max))
                dve.sem_inc(g_row, 1)
                dve.wait_ge(g_T, 2 * l + 1)
                c.link(dve.tensor_reduce(col[0:1, 1:2], psT[0][0:1, 0:P], AX_X, ALU.max))
                dve.sem_inc(g_row, 1)
                dve.wait_ge(g_T, 2 * l + 2)
                v = col[:, 4:5]

                def power():
                    c.link(dve.tensor_scalar(v.bitcast(I32), v.bitcast(I32), 0x7F800000, None, ALU.bitwise_and))
                c.link(dve.tensor_scalar(v, psT[0][:, 0:1], 2.0 ** -14, 1e-30, ALU.mult, ALU.max))
                power()
                c.link(dve.reciprocal(v, v))
                power()
                c.link(dve.tensor_scalar(nss[:, :], norm_src[:, :], v, None, ALU.mult))
                dve.sem_inc(nss_ready, 1)
                c.link(dve.reciprocal(v, v))
                c.link(dve.tensor_scalar(v, v, 1.5, None, ALU.mult))
                power()
                c.link(dve.tensor_scalar(col[:, 5:6], v, 4.0, None, ALU.mult))

            dve.wait_ge(w_in, 16 * (3 + 3 + 2 + 3 * NX))
            for l in range(3):
                scale_of(l)
                with dve.Fori(0, NT) as t:
                    dve.wait_ge(hi_ready, l * NT + t + 1)
                    dve.scalar_tensor_tensor(out=x_lo[:, bass.ds(t, 1), :], in0=prod[:, bass.ds(t, 1), :], scalar=nss[:, bass.ds(t, 1)],
                                             in1=x_hi[:, bass.ds(t, 1), 0:D], op0=ALU.mult, op1=ALU.subtract).then_inc(lo_ready, 1)
                if l == 2:
                    dve.wait_ge(w2_in, 16 * 5)

                K = (3, 2, 5)[l]

                def finish(t, s):
                    k = Chain(dve, p_vo, sum((3, 2, 5)[:l]) * NT + t * K)
                    dve.wait_ge(acc_done, l * NT + t + 1 + RING)
                    if l == 0:
                        dve.tensor_scalar(col[:, 2:3], acc[s][:, D:D + 1], 1.0, None, ALU.max).then_inc(degs, 1)
                        dve.wait_ge(deg_sd, t + 2)
                        k.link(copy(norm_dst[:, bass.ds(t, 1)], col[:, 3:4]))
                        k.link(dve.tensor_scalar(col[:, 6:7], col[:, 3:4], col[:, 5:6], None, ALU.mult))
                    else:
                        k.link(dve.tensor_scalar(col[:, 6:7], norm_dst[:, bass.ds(t, 1)], col[:, 5:6], None, ALU.mult))
                    to = tmp[:, :] if l < 2 else grow
                    k.link(dve.scalar_tensor_tensor(out=to, in0=acc[s][:, 0:D], scalar=col[:, 6:7], in1=gb[l], op0=ALU.mult, op1=ALU.add))
                    if l < 2:
                        dve.wait_ge(h_T, (l + 1) * NT + t + 1)
                        dve.tensor_scalar(hrow[:, :], tmp[:, :], 0.0, None, ALU.max).then_inc(h_ready, 1)
                        dve.wait_ge(h_ready, (l + 1) * NT + t + 1)
                        dve.sem_inc(acc_used, 1)
                    else:
                        dve.sem_inc(acc_used, 1)

                def before_router(t, n):
                    k = Chain(dve, p_vo, sum((3, 2)) * NT + t * K + 2)
                    dve.wait_ge(n_out, t + 2)
                    dve.sem_inc(dve_past, 1)
                    k.link(dve.bn_stats(st6[:, :], nodes[:, bass.ds(t, 1), :]), dve_past)
                    k.link(dve.bn_aggr(mv1[:, :], st6[:, :]))
                    dve.tensor_scalar(sd1[:, :], mv1[:, 1:2], LN_EPS, None, ALU.add).then_inc(n_mv, 1)
                    k.link(copy(mv[:, bass.ds(t, 1), :], mv1[:, :].unsqueeze(1)))
                    dve.wait_ge(r_hsT, t + 1)
                    dve.wait_ge(n_sd, n)
                    dve.tensor_scalar(urow.unsqueeze(1), nodes[:, bass.ds(t, 1), :], mv1[:, 0:1], sd1[:, 0:1], ALU.subtract, ALU.mult).then_inc(r_hs, 1)
                    dve.wait_ge(r_hs, t + 1)
                    dve.sem_inc(dve_past, 1)

                def queries(t):
                    elu_min(psB, NT + t)
                    dve.wait_ge(n_t, t)
                    elu_sum(psB, NT + t)

                def after(t, s, ahead):
                    finish(t, s)
                    if l < 2:
                        largest(t, (l + 1) * NT + t)
                        return
                    if ahead is not None:
                        queries(ahead)
                        attended(ahead, x1s[1 - s], K1 + t * (K1 + K2), 3 * t + 2)
                        mixed(t, x1s[s], K1 + t * (K1 + K2) + K1, 3 * t + 3)
                        before_router(t, 3 * t + 4)
                    else:
                        mixed(t, x1s[s], K1 + t * (K1 + K2), 3 * NT - 1)
                        before_router(t, 3 * NT)
                if l == 2:
                    queries(0)
                    attended(0, x1s[0], 0, 1)
                with dve.Fori(0, NT // 2) as i:
                    after(2 * i, 0, 2 * i + 1)
                    after(2 * i + 1, 1, 2 * i + 2)
                after(NT - 1, 0, None)
                if l == 0:
                    dve.wait_ge(m_KV, NT + 2)
                    for c_ in range(HALVES):
                        for h in range(HPB):
                            q, kv = slice(h * HD, (h + 1) * HD), c_ * (P + 1)
                            dve.tensor_copy(kvblk[q, c_, h * HD:(h + 1) * HD], psKV[q, kv + h * HD:kv + (h + 1) * HD])
                            ins = dve.tensor_copy(kvblk[q, c_, P + h:P + h + 1], psKV[q, kv + P:kv + P + 1])
                    ins.then_inc(kv_ready, 1)
            c.link(dve.tensor_scalar(mv[:, :, 1], mv[:, :, 1], 1.0 + LN_EPS, LN_EPS * LN_EPS, ALU.mult, ALU.add))
            dve.sem_inc(mv_ready, 1)

            def te(v):
                return v.rearrange("p (t e) -> p t e", e=NX)

            def over_e(v):
                return v.unsqueeze(2).broadcast_to([P, NT, NX])

            m1, p1, m2, p2, d12, inv, f1, f2 = (small[:, i, :] for i in range(8))
            desc = desc8[:, :].unsqueeze(1).broadcast_to([P, NT, NX])
            dve.wait_ge(r_row, NT + 1)
            c.link(dve.tensor_tensor(te(logits), te(psL), br_row[:, :].unsqueeze(1).broadcast_to([P, NT, NX]), ALU.add))

            def first_max(v, m, p_, oh):
                c.link(dve.tensor_reduce(m, te(v), AX_X, ALU.max))
                c.link(dve.tensor_tensor(te(s_a), te(v), over_e(m), ALU.is_equal))
                c.link(dve.tensor_tensor(te(s_a), te(s_a), desc, ALU.mult))
                c.link(dve.tensor_reduce(p_, te(s_a), AX_X, ALU.max))
                c.link(dve.tensor_tensor(te(oh), desc, over_e(p_), ALU.is_equal))

            first_max(logits, m1, p1, oh1)
            c.link(dve.scalar_tensor_tensor(out=s_b, in0=oh1, scalar=-3.0e38, in1=logits, op0=ALU.mult, op1=ALU.add))
            first_max(s_b, m2, p2, oh2)
            c.link(dve.tensor_tensor(gate1[:, :], m2, m1, ALU.subtract))
            dve.sem_inc(fm, 1)
            for oh in (oh1, oh2):
                c.link(dve.tensor_tensor(te(oh), te(oh), over_e(valid[:, :]), ALU.mult))
            c.link(dve.tensor_tensor(pick, oh1, oh2, ALU.add))
            dve.sem_inc(mask_ready, 1)
            dve.wait_ge(fe, 1)
            c.link(dve.tensor_scalar(d12, gate2[:, :], 1.0, None, ALU.add))
            c.link(dve.reciprocal(gate1[:, :], d12))
            c.link(dve.tensor_tensor(gate2[:, :], gate2[:, :], gate1[:, :], ALU.mult))
            dve.wait_ge(rank_mm, 1)
            c.link(dve.tensor_copy(tot, psB[:, 0:NE]))
            for e in range(NX):
                c.link(dve.tensor_tensor_scan(incl.rearrange("p (t e) -> p e t", e=NX)[:, e, :], ones[:, 0:NT],
                                              tot.rearrange("p (t e) -> p e t", e=NX)[:, e, :], 0.0, ALU.mult, ALU.add))
            c.link(dve.tensor_tensor(start_r, incl, tot, ALU.subtract))
            c.link(dve.tensor_tensor(start_r, start_r, psA[:, 0:NE], ALU.add))
            c.link(dve.tensor_scalar(cnt8i[:, 0:NX], te(incl)[:, NT - 1, :], float(BT - 1), None, ALU.add))
            c.link(dve.tensor_scalar(cnt8i[:, 0:NX], cnt8i[:, 0:NX], 8, None, ALU.arith_shift_right))
            c.link(dve.tensor_scalar(cnt8[:, 0, 0:NX], cnt8i[:, 0:NX], 1.0, None, ALU.max))
            c.link(dve.tensor_tensor_scan(cnt8[:, 1, 0:NX], ones[:, 0:NX], cnt8[:, 0, 0:NX], 0.0, ALU.mult, ALU.add))
            c.link(dve.tensor_tensor(cnt8[:, 2, 0:NX], cnt8[:, 1, 0:NX], cnt8[:, 0, 0:NX], ALU.subtract))
            c.link(dve.memset(blk_no[:, 0:1], 0))
            c.link(dve.tensor_copy(blk_no[:, 1:NX + 1], cnt8[:, 1, 0:NX]))
            c.link(dve.tensor_scalar(cnt8[:, 2, 0:NX], cnt8[:, 2, 0:NX], float(BT), None, ALU.mult))
            c.link(dve.tensor_tensor(te(start_r), te(start_r), cnt8[:, 2, 0:NX].unsqueeze(1).broadcast_to([P, NT, NX]), ALU.add))
            c.link(dve.tensor_scalar(inv, valid[:, :], -float(P), float(P), ALU.mult, ALU.add))
            for oh, f, slot, take in ((oh1, f1, slot1, take1), (oh2, f2, slot2, take2)):
                c.link(dve.tensor_tensor(s_a, oh, start_r, ALU.mult))
                c.link(dve.tensor_reduce(f, te(s_a), AX_X, ALU.add))
                c.link(dve.tensor_copy(take[:, :], f))
                if oh is oh2:
                    c.link(dve.tensor_tensor(f, f, inv, ALU.add))
                c.link(dve.tensor_tensor(slot[:, :], f, dump[:, :], ALU.add))
            dve.sem_inc(slots_ready, 1)

            dve.wait_ge(sd_ready, 2)

            def spread(t, s, before_):
                dve.wait_ge(scat[s], 32 * before_)
                copy(sidx[:, s, 0:1], slot1[:, bass.ds(t, 1)])
                copy(sidx[:, s, 1:2], slot2[:, bass.ds(t, 1)])
                dve.tensor_scalar(st[:, s, :].unsqueeze(1), nodes[:, bass.ds(t, 1), :], mv[:, bass.ds(t, 1), 0:1], rstd[:, bass.ds(t, 1)],
                                  ALU.subtract, ALU.mult).then_inc(r_xs, 1)
            spread(0, 0, 0)
            spread(1, 1, 0)
            with dve.Fori(1, NT // 2) as i:
                spread(2 * i, 0, i)
                spread(2 * i + 1, 1, i)
            spread(NT - 1, 0, NT // 2)

            with dve.Fori(0, NX) as e:
                lo = dve.value_load(blk_no[0:1, bass.ds(e, 1)], min_val=0, max_val=NBLK)
                hi = dve.value_load(blk_no[0:1, bass.ds(e + 1, 1)], min_val=0, max_val=NBLK)
                with dve.Fori(lo, hi) as b:
                    dve.wait_ge(b_T, b + 2)
                    dve.wait_ge(b_y, b + 1)
                    for c_ in range(HALVES):
                        ins = dve.tensor_scalar(xeT[:, c_, :], bank[1][:, c_ * BT:(c_ + 1) * BT], fgcol[:, bass.ds(e, 1), c_:c_ + 1],
                                                fbcol[:, bass.ds(e, 1), c_:c_ + 1], ALU.mult, ALU.add)
                        ins.then_inc(b_xT, 1)
                    dve.wait_ge(b_y, b + 2)
                    dve.wait_ge(b_out, b * 16 + 16)
                    for a in range(2):
                        ins = dve.tensor_copy(ys[:, a, :], bank[2 + a][:, 0:D])
                    ins.then_inc(b_yc, 1)

            def combine(t, s, before_):
                dve.wait_ge(f_got[s], 32 * (before_ + 1))
                dve.wait_ge(f_out[s], 16 * (before_ + 1))
                k = Chain(dve, f_vo, t)
                dve.wait_ge(f_ready, t + 1)
                k.link(dve.scalar_tensor_tensor(out=tmp[:, :], in0=hs[:, s, :], scalar=gate1[:, bass.ds(t, 1)],
                                                in1=nodes[:, bass.ds(t, 1), :], op0=ALU.mult, op1=ALU.add))
                dve.scalar_tensor_tensor(out=st[:, s, :], in0=hT[:, s, :], scalar=gate2[:, bass.ds(t, 1)],
                                         in1=tmp[:, :], op0=ALU.mult, op1=ALU.add).then_inc(f_ready, 1)

            def ask(t, s, before_):
                copy(sidx[:, s, 0:1], take1[:, bass.ds(t, 1)])
                copy(sidx[:, s, 1:2], take2[:, bass.ds(t, 1)]).then_inc(f_idx, 1)

            ask(0, 0, 0)
            with dve.Fori(0, NT // 2) as i:
                ask(2 * i + 1, 1, i)
                combine(2 * i, 0, i)
                ask(2 * i + 2, 0, i)
                combine(2 * i + 1, 1, i)
            combine(NT - 1, 0, NT // 2)


_GNN = ("L0_gnn_W", "L0_gnn_b")
_INS = ["x", "src", "dst", "L0_gnn_W0", "L0_gnn_b0", "L0_gnn_W1", "L0_gnn_b1", "L0_gnn_W2", "L0_gnn_b2", "L0_mix_Wqkv",
        "L0_mix_ln1_g", "L0_mix_ln1_b", "L0_mix_W1", "L0_mix_b1", "L0_mix_W2", "L0_mix_b2", "L0_mix_ln2_g", "L0_mix_ln2_b",
        "L0_ffn_Wr", "L0_ffn_br", "L0_ffn_ln_g", "L0_ffn_ln_b", "L0_ffn_W1", "L0_ffn_b1", "L0_ffn_W2", "L0_ffn_b2"]


def kernel(**inputs):
    import concourse.bacc as _bacc
    from concourse.bass_utils import run_bass_kernel_spmd as _run

    nc = _bacc.Bacc("TRN2", target_bir_lowering=False, num_devices=1)
    arrays, a = {}, {}
    for name in _INS:
        v = np.ascontiguousarray(inputs[name])
        arrays[f"in_{name}_dram"] = v
        a[name] = nc.dram_tensor(f"in_{name}_dram", v.shape, mybir.dt.from_np(v.dtype), kind="ExternalInput").ap()
    out = nc.dram_tensor("out_0_dram", arrays["in_x_dram"].shape, F32, kind="ExternalOutput").ap()
    gps_layer(nc, a["x"], a["src"], a["dst"], [a[f"L0_gnn_W{l}"] for l in range(3)], [a[f"L0_gnn_b{l}"] for l in range(3)],
              a["L0_mix_Wqkv"], a["L0_mix_ln1_g"], a["L0_mix_ln1_b"], a["L0_mix_W1"], a["L0_mix_b1"], a["L0_mix_W2"],
              a["L0_mix_b2"], a["L0_mix_ln2_g"], a["L0_mix_ln2_b"], a["L0_ffn_Wr"], a["L0_ffn_br"], a["L0_ffn_ln_g"],
              a["L0_ffn_ln_b"], a["L0_ffn_W1"], a["L0_ffn_b1"], a["L0_ffn_W2"], a["L0_ffn_b2"], out)
    r = _run(nc, [arrays], core_ids=[0])
    return r.results[0]["out_0_dram"]
```
